# Optimizing a Trainium2 kernel written in Bass

```python
import numpy as np
import jax
import jax.numpy as jnp

def _softmax(x, axis=-1):
    return jax.nn.softmax(x, axis=axis)

def _gelu(x):
    return jax.nn.gelu(x, approximate=True)

def _silu(x):
    return jax.nn.silu(x)

def _sigmoid(x):
    return jax.nn.sigmoid(x)

def _layernorm(x, axis=-1, eps=1e-05):
    m = jnp.mean(x, axis=axis, keepdims=True)
    v = jnp.var(x, axis=axis, keepdims=True)
    return (x - m) / jnp.sqrt(v + eps)

def _scatter_add(tgt, idx, src, axis=0):
    return tgt.at[idx].add(src)

def _segment_sum(src, seg, n):
    return jax.ops.segment_sum(src, seg, n)
kernel_name = 'mk_gnn_resnorm_d4_gnn_r8_12854f'

def setup_inputs(seed: int=0):
    np.random.seed(seed)
    _w = jnp.asarray

    def _rec_inputs():
        import jax
        import jax.numpy as jnp
        _gk = jax.random.key(seed)
        x = -0.0009044 + 1 * jax.random.normal(jax.random.fold_in(_gk, 1), (12500, 16), jnp.float32)
        src = jax.random.randint(jax.random.fold_in(_gk, 2), (400000,), 0, 12500, jnp.int32)
        dst = jax.random.randint(jax.random.fold_in(_gk, 3), (400000,), 0, 12500, jnp.int32)
        _o = jnp.argsort(dst, stable=True)
        src = src[_o]
        dst = dst[_o]
        edge_attr_3 = -1.09012e-05 + 0.99985 * jax.random.normal(jax.random.fold_in(_gk, 11), (400000, 3), jnp.float32)
        edge_attr_48 = -3.69585e-06 + 0.999911 * jax.random.normal(jax.random.fold_in(_gk, 12), (400000, 48), jnp.float32)
        edge_attr_8 = -5.3897e-05 + 0.999841 * jax.random.normal(jax.random.fold_in(_gk, 13), (400000, 8), jnp.float32)
        node_vec1 = -0.00472126 + 0.997171 * jax.random.normal(jax.random.fold_in(_gk, 15), (12500, 1), jnp.float32)
        return (x, src, dst, edge_attr_3, edge_attr_48, edge_attr_8, node_vec1)
    x, src, dst, edge_attr_3, edge_attr_48, edge_attr_8, node_vec1 = _rec_inputs()

    def _L0_gnn_setup():
        import jax, jax.numpy as jnp
        import numpy as np
        N_NODES = 12500
        N_EDGES = 400000
        D_NODE = 16
        D_EDGE = 8
        D_HIDDEN = 16
        key = jax.random.key(seed)
        ks = jax.random.split(key, 8)
        node_features = jax.random.normal(ks[0], (N_NODES, D_NODE), dtype=jnp.float32)
        edge_attr_e3nn = jax.random.normal(ks[1], (N_EDGES, D_EDGE), dtype=jnp.float32)
        node_attr_scalar_raw = jax.random.normal(ks[2], (N_NODES, 1), dtype=jnp.float32)
        W_msg_tp = jax.random.normal(ks[3], (D_NODE, D_EDGE, D_HIDDEN), dtype=jnp.float32)
        W_msg_lin = jax.random.normal(ks[4], (D_HIDDEN, D_HIDDEN), dtype=jnp.float32)
        W_upd_tp = jax.random.normal(ks[5], (D_NODE, D_HIDDEN, D_HIDDEN), dtype=jnp.float32)
        W_upd_lin = jax.random.normal(ks[6], (D_HIDDEN, D_NODE), dtype=jnp.float32)
        edge_index = jax.random.randint(ks[7], (2, N_EDGES), 0, N_NODES, dtype=jnp.int64)
        return {'node_features': node_features, 'edge_attr_e3nn': edge_attr_e3nn, 'node_attr_scalar_raw': node_attr_scalar_raw, 'W_msg_tp': W_msg_tp, 'W_msg_lin': W_msg_lin, 'W_upd_tp': W_upd_tp, 'W_upd_lin': W_upd_lin, 'edge_index': edge_index}
    _L0_gnn_all = _L0_gnn_setup()
    _L0_gnn_in = {k: v for k, v in _L0_gnn_all.items() if k in ('W_msg_tp', 'W_msg_lin', 'W_upd_tp', 'W_upd_lin')}
    del _L0_gnn_all

    def _L1_gnn_setup():
        import jax, jax.numpy as jnp
        import numpy as np
        N_NODES = 25000
        N_EDGES = 400000
        F_IN = 16
        N_CLASSES = 16

        def _gin_conv(x, src, dst, eps, wa, ba, wb, bb, n_nodes):
            agg = jax.ops.segment_sum(x[src], dst, num_segments=n_nodes)
            h = (1.0 + eps) * x + agg
            h = jax.nn.relu(h @ wa + ba) @ wb + bb
            return h
        key = jax.random.key(seed)
        ks = jax.random.split(key, 8)
        s = 1.0 / np.sqrt(F_IN)
        return {'x': jax.random.normal(ks[0], (N_NODES, F_IN), dtype=jnp.float32), 'edge_index': jax.random.randint(ks[1], (2, N_EDGES), 0, N_NODES, dtype=jnp.int32), 'eps1': jnp.zeros((), dtype=jnp.float32), 'w1a': jax.random.normal(ks[2], (F_IN, 16), dtype=jnp.float32) * s, 'b1a': jnp.zeros((16,), dtype=jnp.float32), 'w1b': jax.random.normal(ks[3], (16, 16), dtype=jnp.float32) * 0.25, 'b1b': jnp.zeros((16,), dtype=jnp.float32), 'eps2': jnp.zeros((), dtype=jnp.float32), 'w2a': jax.random.normal(ks[4], (16, N_CLASSES), dtype=jnp.float32) * 0.25, 'b2a': jnp.zeros((N_CLASSES,), dtype=jnp.float32), 'w2b': jax.random.normal(ks[5], (N_CLASSES, N_CLASSES), dtype=jnp.float32) * 0.25, 'b2b': jnp.zeros((N_CLASSES,), dtype=jnp.float32)}
    _L1_gnn_all = _L1_gnn_setup()
    _L1_gnn_in = {k: v for k, v in _L1_gnn_all.items() if k in ('eps1', 'w1a', 'b1a', 'w1b', 'b1b', 'eps2', 'w2a', 'b2a', 'w2b', 'b2b')}
    del _L1_gnn_all

    def _L2_gnn_setup():
        import jax, jax.numpy as jnp
        import numpy as np
        N_NODES = 125000
        key = jax.random.key(seed)
        k1, k2, k3 = jax.random.split(key, 3)
        x = jax.random.normal(k1, (N_NODES, 16), dtype=jnp.float32)
        edge_index = jax.random.randint(k2, (2, 500000), 0, N_NODES, dtype=jnp.int64)
        W = jax.random.normal(k3, (16, 16), dtype=jnp.float32) * (1.0 / np.sqrt(16.0))
        b = jnp.zeros((16,), dtype=jnp.float32)
        return {'x': x, 'edge_index': edge_index, 'W': W, 'b': b}
    _L2_gnn_all = _L2_gnn_setup()
    _L2_gnn_in = {k: v for k, v in _L2_gnn_all.items() if k in ('W', 'b')}
    del _L2_gnn_all

    def _L3_gnn_setup():
        import jax, jax.numpy as jnp
        import numpy as np
        NS, NV = (16, 4)
        EPS = 1e-05
        N_NODES, N_EDGES = (5000, 50000)

        def _bn_scalar(x, g, b):
            m = x.mean(0)
            v = ((x - m) ** 2).mean(0)
            return (x - m) / jnp.sqrt(v + EPS) * g + b

        def _seg_mean(x, idx, n):
            s = jax.ops.segment_sum(x, idx, num_segments=n)
            c = jax.ops.segment_sum(jnp.ones((idx.shape[0],), x.dtype), idx, num_segments=n)
            return s / jnp.maximum(c, 1.0)[:, None]

        def _edge_weights(edge_attr, w1, b1, w2, b2):
            h = jax.nn.relu(edge_attr @ w1 + b1)
            return h @ w2 + b2

        def _forward(node_attr, edge_attr, edge_vec, fc0_w1, fc0_b1, fc0_w2, fc0_b2, fc1_w1, fc1_b1, fc1_w2, fc1_b2, bn0_gs, bn0_bs, bn0_gv, bn1_gs, bn1_bs, edge_index):
            N = node_attr.shape[0]
            E = edge_attr.shape[0]
            src, dst = (edge_index[0], edge_index[1])
            rhat = edge_vec / (jnp.linalg.norm(edge_vec, axis=-1, keepdims=True) + 1e-12)
            sh1 = rhat * float(np.sqrt(3.0))
            w = _edge_weights(edge_attr, fc0_w1, fc0_b1, fc0_w2, fc0_b2)
            wa = w[:, :NS * NS].reshape(E, NS, NS)
            wb = w[:, NS * NS:].reshape(E, NS, NV)
            x = node_attr[dst]
            inv = float(1.0 / np.sqrt(NS))
            msg_s = jnp.einsum('ei,eij->ej', x, wa) * inv
            msg_v = jnp.einsum('ei,eij,ec->ejc', x, wb, sh1) * inv
            msg = jnp.concatenate([msg_s, msg_v.reshape(E, NV * 3)], axis=-1)
            out = _seg_mean(msg, src, N)
            s0 = _bn_scalar(out[:, :NS], bn0_gs, bn0_bs)
            v0 = out[:, NS:].reshape(N, NV, 3)
            vn = jnp.sqrt((v0 ** 2).mean(axis=(0, 2)) + EPS)
            v0 = v0 / vn[None, :, None] * bn0_gv[None, :, None]
            w = _edge_weights(edge_attr, fc1_w1, fc1_b1, fc1_w2, fc1_b2)
            wa = w[:, :NS * NS].reshape(E, NS, NS)
            wb = w[:, NS * NS:].reshape(E, NV, NS)
            s = s0[dst]
            v = v0[dst]
            path_a = jnp.einsum('ei,eij->ej', s, wa)
            path_b = jnp.einsum('eic,ec,eij->ej', v, sh1, wb) * float(1.0 / np.sqrt(3.0))
            msg = (path_a + path_b) * float(1.0 / np.sqrt(NS + NV))
            node1 = _seg_mean(msg, src, N)
            return _bn_scalar(node1, bn1_gs, bn1_bs)
        key = jax.random.key(seed)
        ks = jax.random.split(key, 8)
        d = 3 * NS
        wn = NS * NS + NS * NV
        g = lambda k, shape, sc: jax.random.normal(k, shape, jnp.float32) * sc
        return {'node_attr': g(ks[0], (N_NODES, NS), 1.0), 'edge_attr': g(ks[1], (N_EDGES, d), 1.0), 'edge_vec': g(ks[2], (N_EDGES, 3), 1.0), 'fc0_w1': g(ks[3], (d, d), d ** (-0.5)), 'fc0_b1': jnp.zeros((d,), jnp.float32), 'fc0_w2': g(ks[4], (d, wn), d ** (-0.5)), 'fc0_b2': jnp.zeros((wn,), jnp.float32), 'fc1_w1': g(ks[5], (d, d), d ** (-0.5)), 'fc1_b1': jnp.zeros((d,), jnp.float32), 'fc1_w2': g(ks[6], (d, wn), d ** (-0.5)), 'fc1_b2': jnp.zeros((wn,), jnp.float32), 'bn0_gs': jnp.ones((NS,), jnp.float32), 'bn0_bs': jnp.zeros((NS,), jnp.float32), 'bn0_gv': jnp.ones((NV,), jnp.float32), 'bn1_gs': jnp.ones((NS,), jnp.float32), 'bn1_bs': jnp.zeros((NS,), jnp.float32), 'edge_index': jax.random.randint(ks[7], (2, N_EDGES), 0, N_NODES)}
    _L3_gnn_all = _L3_gnn_setup()
    _L3_gnn_in = {k: v for k, v in _L3_gnn_all.items() if k in ('fc0_w1', 'fc0_b1', 'fc0_w2', 'fc0_b2', 'fc1_w1', 'fc1_b1', 'fc1_w2', 'fc1_b2', 'bn0_gs', 'bn0_bs', 'bn0_gv', 'bn1_gs', 'bn1_bs')}
    del _L3_gnn_all
    return {'x': x, 'src': src, 'dst': dst, 'edge_attr_3': edge_attr_3, 'edge_attr_48': edge_attr_48, 'edge_attr_8': edge_attr_8, 'node_vec1': node_vec1, 'L0_gnn_W_msg_tp': _L0_gnn_in['W_msg_tp'], 'L0_gnn_W_msg_lin': _L0_gnn_in['W_msg_lin'], 'L0_gnn_W_upd_tp': _L0_gnn_in['W_upd_tp'], 'L0_gnn_W_upd_lin': _L0_gnn_in['W_upd_lin'], 'L1_gnn_eps1': _L1_gnn_in['eps1'], 'L1_gnn_w1a': _L1_gnn_in['w1a'], 'L1_gnn_b1a': _L1_gnn_in['b1a'], 'L1_gnn_w1b': _L1_gnn_in['w1b'], 'L1_gnn_b1b': _L1_gnn_in['b1b'], 'L1_gnn_eps2': _L1_gnn_in['eps2'], 'L1_gnn_w2a': _L1_gnn_in['w2a'], 'L1_gnn_b2a': _L1_gnn_in['b2a'], 'L1_gnn_w2b': _L1_gnn_in['w2b'], 'L1_gnn_b2b': _L1_gnn_in['b2b'], 'L2_gnn_W': _L2_gnn_in['W'], 'L2_gnn_b': _L2_gnn_in['b'], 'L3_gnn_fc0_w1': _L3_gnn_in['fc0_w1'], 'L3_gnn_fc0_b1': _L3_gnn_in['fc0_b1'], 'L3_gnn_fc0_w2': _L3_gnn_in['fc0_w2'], 'L3_gnn_fc0_b2': _L3_gnn_in['fc0_b2'], 'L3_gnn_fc1_w1': _L3_gnn_in['fc1_w1'], 'L3_gnn_fc1_b1': _L3_gnn_in['fc1_b1'], 'L3_gnn_fc1_w2': _L3_gnn_in['fc1_w2'], 'L3_gnn_fc1_b2': _L3_gnn_in['fc1_b2'], 'L3_gnn_bn0_gs': _L3_gnn_in['bn0_gs'], 'L3_gnn_bn0_bs': _L3_gnn_in['bn0_bs'], 'L3_gnn_bn0_gv': _L3_gnn_in['bn0_gv'], 'L3_gnn_bn1_gs': _L3_gnn_in['bn1_gs'], 'L3_gnn_bn1_bs': _L3_gnn_in['bn1_bs']}

def reference(x, src, dst, edge_attr_3, edge_attr_48, edge_attr_8, node_vec1, L0_gnn_W_msg_tp, L0_gnn_W_msg_lin, L0_gnn_W_upd_tp, L0_gnn_W_upd_lin, L1_gnn_eps1, L1_gnn_w1a, L1_gnn_b1a, L1_gnn_w1b, L1_gnn_b1b, L1_gnn_eps2, L1_gnn_w2a, L1_gnn_b2a, L1_gnn_w2b, L1_gnn_b2b, L2_gnn_W, L2_gnn_b, L3_gnn_fc0_w1, L3_gnn_fc0_b1, L3_gnn_fc0_w2, L3_gnn_fc0_b2, L3_gnn_fc1_w1, L3_gnn_fc1_b1, L3_gnn_fc1_w2, L3_gnn_fc1_b2, L3_gnn_bn0_gs, L3_gnn_bn0_bs, L3_gnn_bn0_gv, L3_gnn_bn1_gs, L3_gnn_bn1_bs):
    import jax
    import jax.numpy as jnp

    def _L0_gnn_ref(node_features, edge_attr_e3nn, node_attr_scalar_raw, W_msg_tp, W_msg_lin, W_upd_tp, W_upd_lin, edge_index):
        import jax, jax.numpy as jnp
        import numpy as np
        N_NODES = 12500
        N_EDGES = 400000
        D_NODE = 16
        D_EDGE = 8
        D_HIDDEN = 16
        n_nodes = node_features.shape[0]
        row = edge_index[0]
        col = edge_index[1]
        norm_msg_tp = 1.0 / np.float32(np.sqrt(D_NODE * D_EDGE))
        norm_upd_tp = 1.0 / np.float32(np.sqrt(D_NODE * D_HIDDEN))
        norm_lin = 1.0 / np.float32(np.sqrt(D_HIDDEN))
        x_j = node_features[col]
        m = jnp.einsum('ei,ej,ijh->eh', x_j, edge_attr_e3nn, W_msg_tp) * norm_msg_tp
        m = jax.nn.silu(m)
        m = m @ W_msg_lin * norm_lin
        agg = jax.ops.segment_sum(m, row, num_segments=n_nodes)
        u = jnp.einsum('ni,nh,ihk->nk', node_features, agg, W_upd_tp) * norm_upd_tp
        u = jax.nn.silu(u)
        u = u @ W_upd_lin * norm_lin
        return node_features + u

    def _L1_gnn_ref(x, edge_index, eps1, w1a, b1a, w1b, b1b, eps2, w2a, b2a, w2b, b2b):
        import jax, jax.numpy as jnp
        import numpy as np
        N_NODES = 25000
        N_EDGES = 400000
        F_IN = 16
        N_CLASSES = 16

        def _gin_conv(x, src, dst, eps, wa, ba, wb, bb, n_nodes):
            agg = jax.ops.segment_sum(x[src], dst, num_segments=n_nodes)
            h = (1.0 + eps) * x + agg
            h = jax.nn.relu(h @ wa + ba) @ wb + bb
            return h
        src, dst = (edge_index[0], edge_index[1])
        n = x.shape[0]
        h = jax.nn.relu(_gin_conv(x, src, dst, eps1, w1a, b1a, w1b, b1b, n))
        h = _gin_conv(h, src, dst, eps2, w2a, b2a, w2b, b2b, n)
        return jax.nn.log_softmax(h, axis=1)

    def _L2_gnn_ref(x, edge_index, W, b):
        import jax, jax.numpy as jnp
        import numpy as np
        N_NODES = 125000
        n = x.shape[0]
        row, col = (edge_index[0], edge_index[1])
        h = x @ W
        deg = jax.ops.segment_sum(jnp.ones_like(col, dtype=h.dtype), col, num_segments=n) + 1.0
        dinv = jax.lax.rsqrt(deg)
        norm = dinv[row] * dinv[col]
        msgs = h[row] * norm[:, None]
        agg = jax.ops.segment_sum(msgs, col, num_segments=n)
        out = agg + h * (dinv * dinv)[:, None] + b
        return out

    def _L3_gnn_ref(node_attr, edge_attr, edge_vec, fc0_w1, fc0_b1, fc0_w2, fc0_b2, fc1_w1, fc1_b1, fc1_w2, fc1_b2, bn0_gs, bn0_bs, bn0_gv, bn1_gs, bn1_bs, edge_index):
        import jax, jax.numpy as jnp
        import numpy as np
        NS, NV = (16, 4)
        EPS = 1e-05
        N_NODES, N_EDGES = (5000, 50000)

        def _bn_scalar(x, g, b):
            m = x.mean(0)
            v = ((x - m) ** 2).mean(0)
            return (x - m) / jnp.sqrt(v + EPS) * g + b

        def _seg_mean(x, idx, n):
            s = jax.ops.segment_sum(x, idx, num_segments=n)
            c = jax.ops.segment_sum(jnp.ones((idx.shape[0],), x.dtype), idx, num_segments=n)
            return s / jnp.maximum(c, 1.0)[:, None]

        def _edge_weights(edge_attr, w1, b1, w2, b2):
            h = jax.nn.relu(edge_attr @ w1 + b1)
            return h @ w2 + b2

        def _forward(node_attr, edge_attr, edge_vec, fc0_w1, fc0_b1, fc0_w2, fc0_b2, fc1_w1, fc1_b1, fc1_w2, fc1_b2, bn0_gs, bn0_bs, bn0_gv, bn1_gs, bn1_bs, edge_index):
            N = node_attr.shape[0]
            E = edge_attr.shape[0]
            src, dst = (edge_index[0], edge_index[1])
            rhat = edge_vec / (jnp.linalg.norm(edge_vec, axis=-1, keepdims=True) + 1e-12)
            sh1 = rhat * float(np.sqrt(3.0))
            w = _edge_weights(edge_attr, fc0_w1, fc0_b1, fc0_w2, fc0_b2)
            wa = w[:, :NS * NS].reshape(E, NS, NS)
            wb = w[:, NS * NS:].reshape(E, NS, NV)
            x = node_attr[dst]
            inv = float(1.0 / np.sqrt(NS))
            msg_s = jnp.einsum('ei,eij->ej', x, wa) * inv
            msg_v = jnp.einsum('ei,eij,ec->ejc', x, wb, sh1) * inv
            msg = jnp.concatenate([msg_s, msg_v.reshape(E, NV * 3)], axis=-1)
            out = _seg_mean(msg, src, N)
            s0 = _bn_scalar(out[:, :NS], bn0_gs, bn0_bs)
            v0 = out[:, NS:].reshape(N, NV, 3)
            vn = jnp.sqrt((v0 ** 2).mean(axis=(0, 2)) + EPS)
            v0 = v0 / vn[None, :, None] * bn0_gv[None, :, None]
            w = _edge_weights(edge_attr, fc1_w1, fc1_b1, fc1_w2, fc1_b2)
            wa = w[:, :NS * NS].reshape(E, NS, NS)
            wb = w[:, NS * NS:].reshape(E, NV, NS)
            s = s0[dst]
            v = v0[dst]
            path_a = jnp.einsum('ei,eij->ej', s, wa)
            path_b = jnp.einsum('eic,ec,eij->ej', v, sh1, wb) * float(1.0 / np.sqrt(3.0))
            msg = (path_a + path_b) * float(1.0 / np.sqrt(NS + NV))
            node1 = _seg_mean(msg, src, N)
            return _bn_scalar(node1, bn1_gs, bn1_bs)
        return _forward(node_attr, edge_attr, edge_vec, fc0_w1, fc0_b1, fc0_w2, fc0_b2, fc1_w1, fc1_b1, fc1_w2, fc1_b2, bn0_gs, bn0_bs, bn0_gv, bn1_gs, bn1_bs, edge_index)
    edge_index = jnp.stack([src, dst])
    x = _layernorm(x + _L0_gnn_ref(x, edge_attr_8, node_vec1, L0_gnn_W_msg_tp, L0_gnn_W_msg_lin, L0_gnn_W_upd_tp, L0_gnn_W_upd_lin, edge_index), axis=-1)
    x = _layernorm(x + _L1_gnn_ref(x, edge_index, L1_gnn_eps1, L1_gnn_w1a, L1_gnn_b1a, L1_gnn_w1b, L1_gnn_b1b, L1_gnn_eps2, L1_gnn_w2a, L1_gnn_b2a, L1_gnn_w2b, L1_gnn_b2b), axis=-1)
    x = _layernorm(x + _L2_gnn_ref(x, edge_index, L2_gnn_W, L2_gnn_b), axis=-1)
    x = _layernorm(x + _L3_gnn_ref(x, edge_attr_48, edge_attr_3, L3_gnn_fc0_w1, L3_gnn_fc0_b1, L3_gnn_fc0_w2, L3_gnn_fc0_b2, L3_gnn_fc1_w1, L3_gnn_fc1_b1, L3_gnn_fc1_w2, L3_gnn_fc1_b2, L3_gnn_bn0_gs, L3_gnn_bn0_bs, L3_gnn_bn0_gv, L3_gnn_bn1_gs, L3_gnn_bn1_bs, edge_index), axis=-1)
    return x

_drawn_inputs = setup_inputs


def setup_inputs(seed=0):
    import zlib

    import numpy as np

    out = dict(_drawn_inputs(seed))
    spreads = {'L1_gnn_b1a': (0.0, 2.0),
     'L1_gnn_b1b': (0.0, 0.8),
     'L1_gnn_b2a': (0.0, 2.0),
     'L1_gnn_b2b': (0.0, 2.0),
     'L2_gnn_b': (0.0, 0.1),
     'L3_gnn_fc0_b1': (0.0, 0.1),
     'L3_gnn_fc0_b2': (0.0, 0.1),
     'L3_gnn_fc1_b1': (0.0, 0.1),
     'L3_gnn_fc1_b2': (0.0, 0.1),
     'L3_gnn_bn0_gs': (1.0, 0.2),
     'L3_gnn_bn0_bs': (0.0, 0.1),
     'L3_gnn_bn0_gv': (1.0, 0.2),
     'L3_gnn_bn1_gs': (1.0, 0.2),
     'L3_gnn_bn1_bs': (0.0, 0.1)}
    factors = {'edge_attr_8': 37.168, 'L0_gnn_W_msg_tp': 23.846, 'x': 2.789}
    for name, (base, spread) in spreads.items():
        noise = np.random.default_rng([zlib.crc32(name.encode()), seed]).standard_normal(out[name].shape)
        drawn = base * np.exp(spread * noise) if base else spread * noise
        out[name] = jnp.asarray(drawn.astype(out[name].dtype))
    for name, factor in factors.items():
        out[name] = (out[name] * factor).astype(out[name].dtype)
    return out
```

```python
from contextlib import ExitStack

import concourse.bass as bass
import numpy as np
from concourse import mybir

ALU = mybir.AluOpType
ACT = mybir.ActivationFunctionType
AX = mybir.AxisListType
F32 = mybir.dt.float32
BF16 = mybir.dt.bfloat16
I32 = mybir.dt.int32

P = 128
N_NODES = 12500
N_EDGES = 400000
F = 16
DE = 8
DH = 48
NV = 4
HI = 8
GROUP = HI * P
NG = -(-N_NODES // GROUP)
NBLK = NG * HI
NW = NBLK * F
NBKT = NG * NG
OHW = 176
EPP = N_EDGES // P
SUB = 25
GRP = 5
SLOTS = 5
NSUB = EPP // SUB
NT_MIN = (N_EDGES + NBKT * (P - 1)) // P
BT = 4
PADT = 4
SB = 8
NSL = 4
LOOP = NSL * SB
NT = -(-NT_MIN // LOOP) * LOOP
NTURN = NT // LOOP
NCHUNK = -(-NT // P)
KB = LOOP // BT
KS = SB // BT
PADLO = 256.0

C_SLO, C_SHI, C_DLO, C_DHI, C_R, C_A8, C_HA = 0, 1, 2, 3, 4, 8, 16
HW = DH + 1
C_HB = C_HA + HW
ROW = C_HB + HW
LEAD = 8

CONSTS = {}


def build_constants():
    p = np.arange(P)
    parts = {
        "ident": np.eye(P),
        "iota": np.tile(np.arange(P), (P, 1)),
        "bucket": np.tile(np.arange(OHW), (P, 1)),
        "before": (p[:, None] < p[None, :]),
        "notbefore": (p[:, None] >= p[None, :]),
        "fold": (p[:, None] % F == np.arange(F)[None, :]),
        "iota8": np.tile(np.arange(HI), (P, 1)),
        "lo": p[:, None],
        "blk": p[:, None] // F,
        "valid": (np.arange(NBLK)[None, :] * P + p[:, None] < N_NODES),
        "tau": np.arange(NCHUNK)[None, :] * P + p[:, None],
    }
    at = 0
    for name, a in parts.items():
        CONSTS[name] = (at, a.shape[1])
        at += a.shape[1]
    return np.concatenate([np.asarray(a, np.float32) for a in parts.values()], axis=1)


class Chain:

    def __init__(self, eng, sem):
        self.eng, self.sem, self.n = eng, sem, 0

    def __call__(self, ins):
        self.n += 1
        ins.then_inc(self.sem, 1)
        self.eng.wait_ge(self.sem, self.n)


class Kernel:

    def __init__(self, nc, ctx, ins, out):
        self.nc, self.ins, self.out, self.ctx = nc, ins, out, ctx
        self.sems = []
        self.rows_d = nc.dram_tensor("edge_rows", (P * NT, ROW), F32, kind="Internal").ap()
        self.idxT_d = nc.dram_tensor("idx_rows", (NTURN, 4 * LOOP * P), BF16, kind="Internal").ap()
        self.nat_d = nc.dram_tensor("idx_nat", (P, NT * 4), F32, kind="Internal").ap()
        self.offs_d = nc.dram_tensor("tile_offsets", (4, NCHUNK * P), I32, kind="Internal").ap()
        w = sum(n for _, n in CONSTS.values())
        self.consts = self.sb("consts", [P, w], F32)

    def c(self, name):
        at, n = CONSTS[name]
        return self.consts[:, at:at + n]

    def sb(self, name, shape, dt=F32, ctx=None):
        return (ctx or self.ctx).enter_context(self.nc.sbuf_tensor(name, shape, dt))

    def ps(self, ctx, name, shape, dt=F32):
        return ctx.enter_context(self.nc.psum_tensor(name, shape, dt))

    def sem(self, name):
        self.sems.append(self.nc.alloc_semaphore(name=name))
        return self.sems[-1]

    def end_phase(self):
        self.nc.all_engine_barrier()
        self.nc.clear_and_free_semaphores(self.sems)
        self.nc.all_engine_barrier()
        self.sems = []


def load_constants(K):
    nc = K.nc
    loaded = K.sem("consts_loaded")
    with nc.Block() as block:
        @block.sync
        def _(sp):
            sp.dma_start(K.consts[:], K.ins["consts"]).then_inc(loaded, 16)
            sp.wait_ge(loaded, 16)


def sort_edges(K):
    nc = K.nc
    with ExitStack() as ctx:
        def sb(name, shape, dt=F32):
            return K.sb(name, shape, dt, ctx)

        src_i = sb("src_i", [P, EPP], I32)
        dst_i = sb("dst_i", [P, EPP], I32)
        shi_i = sb("shi_i", [P, EPP], I32)
        dhi_i = sb("dhi_i", [P, EPP], I32)
        key = sb("key", [P, EPP], BF16)
        vec = sb("vec", [P, EPP, 3])
        buckets = sb("buckets", [P, OHW], BF16)
        before = sb("before", [P, P], BF16)
        notbefore = sb("notbefore", [P, P], BF16)
        ones = sb("ones", [P, P], BF16)
        onesrow = sb("onesrow", [NG, P])
        zeros = sb("zeros", [P, 512], BF16)
        zerof = sb("zerof", [P, NBKT])
        oh = sb("oh", [P, SUB, OHW], BF16)
        w1 = sb("w1", [HW, 2 * DH])
        cnt_i = sb("cnt_i", [P, NBKT], I32)
        tiles = sb("tiles", [P, NBKT])
        end = sb("end", [P, NBKT])
        start = sb("start", [P, GRP, NBKT])
        junk = sb("junk", [P, GRP, NBKT])
        counts = junk[0:NG]
        tb = sb("tb", [P, 4, NCHUNK])
        offs = sb("offs", [P, P], I32)
        pad = sb("pad", [P, PADT, ROW])
        rows = sb("rows", [P, SLOTS, SUB, ROW])
        attr = sb("attr", [P, SLOTS, SUB * DH])
        norm = attr[:].rearrange("p s c -> p (s c)")[:, 0:EPP]
        a8 = sb("a8", [P, SLOTS, SUB * DE])
        aT = sb("aT", [HW, GRP * P])
        both = oh[:].rearrange("p t b -> p (t b)")[:, 0:2 * SLOTS * SUB * NG].rearrange(
            "p (n s t g) -> p n s t g", n=2, s=SLOTS, t=SUB)
        ohs, ohd = both[:, 0], both[:, 1]
        pos = sb("pos", [P, SUB])
        pos_i = sb("pos_i", [P, SUB], I32)
        part_i = sb("part_i", [P, SUB], I32)
        tile_i = sb("tile_i", [P, SUB], I32)
        place = sb("place", [P, SLOTS, SUB], I32)
        count_ps = K.ps(ctx, "count_ps", [P, GRP, 512])
        counter = [count_ps[:, c, 0:NBKT] for c in range(GRP)]
        tp_ps = K.ps(ctx, "tp_ps", [P, 1024])
        h_ps = K.ps(ctx, "h_ps", [P, 512])
        hist_ps, off_ps = h_ps, tp_ps

        idx_loaded, vec_loaded, w_loaded = K.sem("s_idx_loaded"), K.sem("s_vec_loaded"), K.sem("s_w_loaded")
        pad_ready, es_filled = K.sem("s_pad_ready"), K.sem("s_es_filled")
        dve_chain, act_norm, norm2_ready = K.sem("s_dve_chain"), K.sem("s_act_norm"), K.sem("s_norm2_ready")
        hist_ready, hist_used, zero_done = K.sem("s_hist_ready"), K.sem("s_hist_used"), K.sem("s_zero_done")
        start_ready, offs_ready, offs_stored = K.sem("s_start_ready"), K.sem("s_offs_ready"), K.sem("s_offs_stored")
        oh_ready, p_ready, sel_done, rank_used = (K.sem("s_oh_ready"), K.sem("s_p_ready"), K.sem("s_sel_done"),
                                                  K.sem("s_rank_used"))
        attr_loaded, a8_used = K.sem("s_attr_loaded"), K.sem("s_a8_used")
        sp_go, pe_go, counts_ready, spread_ready = (K.sem("s_sp_go"), K.sem("s_pe_go"), K.sem("s_counts_ready"),
                                                    K.sem("s_spread_ready"))
        tp_ready, aT_ready, h_ready, h_used = (K.sem("s_tp_ready"), K.sem("s_aT_ready"), K.sem("s_h_ready"),
                                               K.sem("s_h_used"))
        place_ready, row_ready, pool_go = K.sem("s_place_ready"), K.sem("s_row_ready"), K.sem("s_pool_go")
        rowconst_ready, place_step, slot_free = K.sem("s_rowconst_ready"), K.sem("s_place_step"), K.sem("s_slot_free")
        groups_ready, offs_turned = K.sem("s_groups_ready"), K.sem("s_offs_turned")
        scattered = [K.sem(f"s_scattered{s}") for s in range(SLOTS)]
        NGRP = SUB // GRP
        LAG = 3

        def turns(eng, body):
            for s in range(SLOTS):
                body(s, s, True)
            with eng.Fori(1, NSUB // SLOTS) as turn:
                for s in range(SLOTS):
                    body(turn * SLOTS + s, s, False)

        block = ctx.enter_context(nc.Block())

        @block.sync
        def _(sp):
            sp.dma_start(src_i[:], K.ins["src"].rearrange("(p t) -> p t", p=P)).then_inc(idx_loaded, 16)
            sp.dma_start(dst_i[:], K.ins["dst"].rearrange("(p t) -> p t", p=P)).then_inc(idx_loaded, 16)
            sp.dma_start(vec[:].rearrange("p t c -> p (t c)"),
                         K.ins["edge_attr_3"].rearrange("(p t) c -> p (t c)", p=P)).then_inc(vec_loaded, 16)
            for n, fc in enumerate(("fc0", "fc1")):
                sp.dma_start(w1[0:DH, n * DH:(n + 1) * DH], K.ins[f"L3_gnn_{fc}_w1"]).then_inc(w_loaded, 16)
                sp.dma_start(w1[DH:HW, n * DH:(n + 1) * DH],
                             K.ins[f"L3_gnn_{fc}_b1"].rearrange("(a d) -> a d", a=1)).then_inc(w_loaded, 16)
            sp.wait_ge(pad_ready, 1)
            rows_v = K.rows_d.rearrange("(p t) c -> p (t c)", p=P)
            with sp.Fori(0, NT // PADT) as r:
                sp.dma_start(rows_v[:, bass.ds(r * (PADT * ROW), PADT * ROW)],
                             pad[:].rearrange("p t c -> p (t c)")).then_inc(es_filled, 16)
            sp.wait_ge(offs_ready, 1)
            sp.dma_start(K.offs_d.rearrange("k (c p) -> (k c) p", p=P), offs[0:4 * NCHUNK, :]).then_inc(offs_stored, 16)

            sp.wait_ge(rowconst_ready, 1)

            def load(q, s, first):
                if not first:
                    sp.wait_ge(tp_ready, (q - SLOTS + 1) * NGRP)
                    sp.wait_ge(a8_used, q - SLOTS + 1)
                    sp.sem_inc(sp_go, 1)
                sp.dma_start(attr[:, s, :], K.ins["edge_attr_48"].rearrange("(p t) c -> p (t c)", p=P)[
                    :, bass.ds(q * (SUB * DH), SUB * DH)]).then_inc(attr_loaded, 16)
                sp.dma_start(a8[:, s, :], K.ins["edge_attr_8"].rearrange("(p t) c -> p (t c)", p=P)[
                    :, bass.ds(q * (SUB * DE), SUB * DE)]).then_inc(attr_loaded, 16)
                sp.wait_ge(attr_loaded, q * 32 + 32)
                sp.sem_inc(sp_go, 1)
            turns(sp, load)
            sp.wait_ge(offs_stored, 16)

        @block.vector
        def _(v):
            step = Chain(v, dve_chain)
            step(v.memset(pad[:], 0.0))
            v.memset(pad[:, :, C_SLO:C_DLO + 1:2], PADLO).then_inc(pad_ready, 1)
            v.memset(ones[:], 1.0)
            v.memset(zeros[:], 0.0)
            v.memset(zerof[:], 0.0)
            v.memset(onesrow[:], 1.0)
            v.memset(aT[:], 1.0)
            v.tensor_copy(buckets[:], K.c("bucket"))
            v.tensor_copy(before[:], K.c("before"))
            step(v.tensor_copy(notbefore[:], K.c("notbefore")))
            v.sem_inc(zero_done, 1)
            v.wait_ge(idx_loaded, 32)
            v.tensor_scalar(shi_i[:], src_i[:], 10, None, ALU.logical_shift_right)
            step(v.tensor_scalar(dhi_i[:], dst_i[:], 10, None, ALU.logical_shift_right))
            step(v.scalar_tensor_tensor(key[:], shi_i[:], float(NG), dhi_i[:], ALU.mult, ALU.add))

            def hist(q, s, first):
                if not first:
                    v.wait_ge(hist_used, q - SLOTS + 1)
                iota = K.c("iota")[:, 0:NG].unsqueeze(1).to_broadcast([P, SUB, NG])
                for one, group in ((ohs, shi_i), (ohd, dhi_i)):
                    ins = v.tensor_tensor(one[:, s, :, :], group[:, bass.ds(q * SUB, SUB)].unsqueeze(2).to_broadcast(
                        [P, SUB, NG]), iota, ALU.is_equal)
                ins.then_inc(hist_ready, 1)
            turns(v, hist)
            v.wait_ge(hist_used, NSUB)

            v.tensor_scalar(shi_i[:], src_i[:], 7, HI - 1, ALU.logical_shift_right, ALU.bitwise_and)
            step(v.tensor_scalar(dhi_i[:], dst_i[:], 7, HI - 1, ALU.logical_shift_right, ALU.bitwise_and))
            v.tensor_scalar(src_i[:], src_i[:], P - 1, None, ALU.bitwise_and)
            step(v.tensor_scalar(dst_i[:], dst_i[:], P - 1, None, ALU.bitwise_and))
            v.wait_ge(vec_loaded, 16)
            square = rows[:].rearrange("p s t c -> p (s t c)")[:, 0:EPP]
            step(v.tensor_tensor(norm, vec[:, :, 0], vec[:, :, 0], ALU.mult))
            for c in (1, 2):
                step(v.tensor_tensor(square, vec[:, :, c], vec[:, :, c], ALU.mult))
                ins = v.tensor_tensor(norm, norm, square, ALU.add)
                step(ins)
            v.sem_inc(norm2_ready, 1)
            v.wait_ge(act_norm, 1)
            step(v.tensor_scalar(norm, norm, 1e-12, None, ALU.add))
            step(v.reciprocal(norm, norm))
            step(v.tensor_tensor(vec[:], vec[:], norm.unsqueeze(2).to_broadcast([P, EPP, 3]), ALU.mult))
            step(v.memset(rows[:], 0.0))
            step(v.memset(rows[:].rearrange("p s t c -> p (s t) c")[:, :, C_HA + DH:ROW:HW], 1.0))
            v.sem_inc(rowconst_ready, 1)

            for c in range(GRP):
                ins = v.tensor_tensor(counts[:, c, :].rearrange("p (s d) -> p s d", d=NG),
                                      hist_ps[0:NG, c * NG:(c + 1) * NG].unsqueeze(1).to_broadcast([NG, NG, NG]),
                                      K.c("ident")[0:NG, 0:NG].unsqueeze(2).to_broadcast([NG, NG, NG]), ALU.mult)
            step(ins)
            v.sem_inc(counts_ready, 1)
            v.wait_ge(spread_ready, 1)
            step(v.tensor_copy(start[:, 0, :], counter[0]))
            for c in range(1, GRP):
                step(v.tensor_tensor(start[:, 0, :], start[:, 0, :], counter[c], ALU.add))
            step(v.tensor_scalar(cnt_i[:], start[:, 0, :], float(P - 1), None, ALU.add))
            step(v.tensor_scalar(cnt_i[:], cnt_i[:], 7, None, ALU.logical_shift_right))
            step(v.tensor_copy(tiles[:], cnt_i[:]))
            step(v.tensor_tensor_scan(end[:], tiles[:], zerof[:], 0.0, ALU.add, ALU.add))
            step(v.tensor_tensor(start[:, 0, :], end[:], tiles[:], ALU.subtract))
            step(v.tensor_scalar(start[:, 0, :], start[:, 0, :], float(P), None, ALU.mult))
            for c in range(1, GRP):
                step(v.tensor_tensor(start[:, c, :], start[:, c - 1, :], counter[c - 1], ALU.add))
            v.sem_inc(start_ready, 1)

            def rank(q, s, first):
                for k in range(SUB):
                    if k % GRP == 0 and not first:
                        v.wait_ge(rank_used, q * SUB + (k + GRP - SUB))
                    if k % GRP == 0 and first and s > 0:
                        v.wait_ge(rank_used, q * SUB + k + GRP - SUB)
                    ins = v.tensor_scalar(oh[:, k, :], buckets[:], key[:, bass.ds(q * SUB + k, 1)], None, ALU.is_equal)
                    ins.then_inc(oh_ready, 1)
                for k in range(SUB):
                    v.wait_ge(p_ready, q * SUB + k + 1)
                    v.scalar_tensor_tensor(junk[:, k % GRP, :], counter[k % GRP], 1.0, oh[:, k, 0:NBKT], ALU.mult, ALU.mult,
                                           accum_out=pos[:, k:k + 1]).then_inc(sel_done, 1)
                v.wait_ge(sel_done, q * SUB + SUB)
                v.tensor_copy(pos_i[:], pos[:]).then_inc(place_step, 1)
                v.wait_ge(place_step, q * 3 + 1)
                v.tensor_scalar(part_i[:], pos_i[:], P - 1, None, ALU.bitwise_and)
                v.tensor_scalar(tile_i[:], pos_i[:], 7, None, ALU.logical_shift_right).then_inc(place_step, 1)
                v.wait_ge(place_step, q * 3 + 2)
                if not first:
                    v.wait_ge(slot_free, q - SLOTS + 1)
                v.scalar_tensor_tensor(place[:, s, :], part_i[:], float(NT), tile_i[:], ALU.mult,
                                       ALU.add).then_inc(place_step, 1)
                v.wait_ge(place_step, q * 3 + 3)
                v.sem_inc(place_ready, 1)

            def tile_groups():
                for c in range(NCHUNK):
                    step(v.tensor_scalar(junk[:, 0, :], end[:], K.c("tau")[:, c:c + 1], None, ALU.is_le, ALU.add,
                                         accum_out=tb[:, 1, c:c + 1]))
                    ins = v.tensor_scalar(junk[:, 0, 0:NG], end[:, NG - 1:NBKT:NG], K.c("tau")[:, c:c + 1], None, ALU.is_le,
                                          ALU.add, accum_out=tb[:, 0, c:c + 1])
                    step(ins)
                step(v.tensor_scalar(tb[:, 1, :], tb[:, 1, :], float(NBKT - 1), None, ALU.min))
                step(v.tensor_scalar(tb[:, 0, :], tb[:, 0, :], float(NG - 1), None, ALU.min))
                step(v.scalar_tensor_tensor(tb[:, 1, :], tb[:, 0, :], -float(NG), tb[:, 1, :], ALU.mult, ALU.add))
                step(v.tensor_scalar(tb[:, 2:4, :], tb[:, 0:2, :], float(HI), None, ALU.mult))
                step(v.tensor_scalar(tb[:, 0:2, :], tb[:, 0:2, :], float(P), None, ALU.mult))
                v.sem_inc(groups_ready, 1)
                v.wait_ge(offs_turned, 1)
                step(v.tensor_copy(offs[0:4 * NCHUNK, :], off_ps[0:4 * NCHUNK, 0:P]))
                v.sem_inc(offs_ready, 1)
            tile_groups()
            turns(v, rank)

        @block.scalar
        def _(act):
            act.wait_ge(norm2_ready, 1)
            nc.scalar.activation(norm, norm, ACT.Sqrt).then_inc(act_norm, 1)
            act.wait_ge(rowconst_ready, 1)

            def fill(q, s, first):
                if not first:
                    act.wait_ge(slot_free, q - SLOTS + 1)
                cols = bass.ds(q * SUB, SUB)
                for c, a in ((C_SLO, src_i), (C_SHI, shi_i), (C_DLO, dst_i), (C_DHI, dhi_i)):
                    nc.scalar.copy(rows[:, s, :, c], a[:, cols])
                nc.scalar.copy(rows[:, s, :, C_R:C_R + 3], vec[:, cols, :])
                act.wait_ge(attr_loaded, q * 32 + 32)
                nc.scalar.copy(rows[:, s, :, C_A8:C_A8 + DE],
                               a8[:, s, :].rearrange("p (t c) -> p t c", c=DE)).then_inc(a8_used, 1)
                for g in range(NGRP):
                    act.wait_ge(tp_ready, q * NGRP + g + 1)
                    nc.scalar.copy(aT[0:DH, :], tp_ps[0:DH, 0:GRP * P]).then_inc(aT_ready, 1)
                    act.wait_ge(h_ready, q * NGRP + g + 1)
                    nc.scalar.activation(
                        rows[:, s, g * GRP:(g + 1) * GRP, C_HA:ROW].rearrange("p t (n c) -> p t n c", n=2)[:, :, :, 0:DH],
                        h_ps[:, 0:GRP * 2 * DH].rearrange("p (t n c) -> p t n c", n=2, c=DH), ACT.Relu).then_inc(row_ready, 1)
            turns(act, fill)

        @block.tensor
        def _(pe):
            pe.wait_ge(zero_done, 1)
            pe.matmul(hist_ps[0:NG, :], zeros[:, 0:NG], zeros[:], start=True, stop=False, skip_group_check=True)

            def hist(q, s, first):
                pe.wait_ge(hist_ready, q + 1)
                for k in range(SUB):
                    c = k % GRP
                    ins = pe.matmul(hist_ps[0:NG, c * NG:(c + 1) * NG], ohs[:, s, k, :], ohd[:, s, k, :],
                                    start=False, stop=False, skip_group_check=True)
                ins.then_inc(hist_used, 1)
            turns(pe, hist)

            def clear_counters():
                for bank in range(GRP):
                    pe.matmul(count_ps[:, bank, :], ones[:], zeros[:], start=True, stop=False, skip_group_check=True)
            pe.wait_ge(counts_ready, 1)
            clear_counters()
            for c in range(GRP):
                ins = pe.matmul(counter[c], onesrow[:], counts[:, c, :], start=False, stop=False, skip_group_check=True)
            ins.then_inc(spread_ready, 1)
            pe.wait_ge(start_ready, 1)
            clear_counters()
            for c in range(GRP):
                pe.matmul(counter[c], onesrow[0:1, :], start[0:1, c, :], start=False, stop=False, skip_group_check=True)
            pe.wait_ge(groups_ready, 1)
            pe.transpose(off_ps[0:4 * NCHUNK, 0:P], tb[:].rearrange("p k c -> p (k c)"), K.c("ident")).then_inc(offs_turned, 1)
            pe.wait_ge(offs_ready, 1)
            pe.wait_ge(w_loaded, 64)

            def rank(q, s, first):
                for k in range(SUB + LAG):
                    if k < SUB:
                        if k % GRP == 0:
                            turn_attributes(q, s, k // GRP, first)
                        pe.wait_ge(oh_ready, q * SUB + k + 1)
                        pe.matmul(counter[k % GRP], before[:], oh[:, k, 0:NBKT], start=False, stop=False,
                                  skip_group_check=True).then_inc(p_ready, 1)
                        if k % GRP == 2:
                            hidden(q, s, k // GRP, first)
                    if k >= LAG:
                        pe.wait_ge(sel_done, q * SUB + k - LAG + 1)
                        pe.matmul(counter[(k - LAG) % GRP], notbefore[:], oh[:, k - LAG, 0:NBKT], start=False, stop=False,
                                  skip_group_check=True).then_inc(rank_used, 1)

            def turn_attributes(q, s, g, first):
                if g == 0:
                    pe.wait_ge(attr_loaded, q * 32 + 32)
                    pe.sem_inc(pe_go, 1)
                if not (first and s == 0 and g == 0):
                    pe.wait_ge(aT_ready, q * NGRP + g)
                    pe.sem_inc(pe_go, 1)
                for i in range(GRP):
                    k = g * GRP + i
                    ins = pe.transpose(tp_ps[0:DH, i * P:(i + 1) * P], attr[:, s, k * DH:(k + 1) * DH], K.c("ident"))
                ins.then_inc(tp_ready, 1)

            def hidden(q, s, g, first):
                pe.wait_ge(aT_ready, q * NGRP + g + 1)
                if not (first and s == 0 and g == 0):
                    pe.wait_ge(row_ready, q * NGRP + g)
                for i in range(GRP):
                    ins = pe.matmul(h_ps[:, i * 2 * DH:(i + 1) * 2 * DH], aT[:, i * P:(i + 1) * P], w1[:],
                                    start=True, stop=True)
                ins.then_inc(h_ready, 1)
            turns(pe, rank)

        @block.gpsimd
        def _(pool):
            pool.wait_ge(es_filled, NT // PADT * 16)

            def scatter(q, s, first):
                pool.wait_ge(row_ready, q * NGRP + NGRP)
                pool.sem_inc(pool_go, 1)
                pool.wait_ge(place_ready, q + 1)
                pool.sem_inc(pool_go, 1)
                for k in range(SUB):
                    pool.indirect_dma_start(K.rows_d, bass.IndirectOffsetOnAxis(place[:, s, k:k + 1], axis=0),
                                            rows[:, s, k, :], None).then_inc(scattered[s], 16)
                    if k == 5 and not (first and s < 1):
                        b = (s - 1) % SLOTS
                        turn = q if first else None
                        landed(q, b)
                        pool.sem_inc(slot_free, 1)

            def landed(q, b):
                if isinstance(q, int):
                    pool.wait_ge(scattered[b], 16 * SUB * ((q - 1) // SLOTS + 1))
                else:
                    pool.wait_ge(scattered[b], count[b])

            for s in range(SLOTS):
                scatter(s, s, True)
            with pool.Fori(1, NSUB // SLOTS) as turn:
                count = [(turn + 1) * (16 * SUB)] * (SLOTS - 1) + [turn * (16 * SUB)]
                for s in range(SLOTS):
                    scatter(turn * SLOTS + s, s, False)
            for s in range(SLOTS):
                pool.wait_ge(scattered[s], NSUB // SLOTS * 16 * SUB)


def unpack_indices(K):
    nc = K.nc
    R = 4
    with ExitStack() as ctx:
        nat = K.sb("nat", [P, NT, 4], F32, ctx)
        turned = K.sb("turned", [P, R, P], BF16, ctx)
        stage = K.sb("stage", [P, R, 4, LOOP], BF16, ctx)
        ident = K.sb("ident", [P, P], BF16, ctx)
        turn_ps = K.ps(ctx, "turn_ps", [P, R, 1024], BF16)
        staged, ident_ready = K.sem("u_staged"), K.sem("u_ident_ready")
        nat_loaded = [K.sem(f"u_nat_loaded{c}") for c in range(4)]
        nat_stored, rows_stored = K.sem("u_nat_stored"), [K.sem(f"u_rows_stored{r}") for r in range(R)]
        turn_ready, copied, row_free, act_go, pe_go, sp_go = (K.sem("u_turn_ready"), K.sem("u_copied"), K.sem("u_row_free"),
                                                       K.sem("u_act_go"), K.sem("u_pe_go"), K.sem("u_sp_go"))
        cut = [0, 3 * LOOP, 28 * LOOP, 60 * LOOP, NT]
        rows_v = K.rows_d.rearrange("(p t) c -> p t c", p=P)

        def turns(eng, body):
            whole = NTURN // R
            for r in range(R):
                body(r, r, True)
            with eng.Fori(1, whole) as n:
                for r in range(R):
                    body(n * R + r, r, False)
            for r in range(NTURN - whole * R):
                body(whole * R + r, r, False)

        block = ctx.enter_context(nc.Block())

        @block.sync
        def _(sp):
            for c in range(4):
                sp.dma_start(nat[:, cut[c]:cut[c + 1], :], rows_v[:, cut[c]:cut[c + 1], 0:4]).then_inc(nat_loaded[c], 16)
            for c in range(4):
                sp.wait_ge(nat_loaded[c], 16)
            sp.dma_start(K.nat_d, nat[:].rearrange("p t c -> p (t c)")).then_inc(nat_stored, 16)

            def store(q, r, first):
                sp.wait_ge(copied, q + 1)
                sp.dma_start(K.idxT_d[bass.ds(q, 1)].rearrange("o (k e) -> (o k) e", e=P), turned[:, r, :]).then_inc(rows_stored[r], 16)
            turns(sp, store)
            sp.wait_ge(nat_stored, 16)
            for r in range(R):
                sp.wait_ge(rows_stored[r], 16 * len(range(r, NTURN, R)))

        @block.tensor
        def _(pe):
            pe.wait_ge(ident_ready, 1)

            def turn(q, r, first):
                pe.wait_ge(staged, q + 1)
                if not first:
                    pe.wait_ge(copied, q - R + 1)
                    pe.sem_inc(pe_go, 1)
                pe.transpose(turn_ps[:, r, 0:P], stage[:, r, :, :].rearrange("p c t -> p (c t)"),
                             ident[:]).then_inc(turn_ready, 1)
            turns(pe, turn)

        @block.vector
        def _(v):
            v.tensor_copy(ident[:], K.c("ident")).then_inc(ident_ready, 1)
            for c in range(4):
                v.wait_ge(nat_loaded[c], 16)

            def put(q, r, first):
                if not first:
                    v.wait_ge(turn_ready, q - R + 1)
                v.tensor_copy(stage[:, r, :, :], nat[:, bass.ds(q * LOOP, LOOP), :].rearrange(
                    "p t c -> p c t")).then_inc(staged, 1)
            turns(v, put)

        @block.scalar
        def _(act):
            def copy(q, r, first):
                act.wait_ge(turn_ready, q + 1)
                if not first:
                    use = q - r if isinstance(q, int) else None
                    act.wait_ge(rows_stored[r], stored(q, r))
                nc.scalar.copy(turned[:, r, :], turn_ps[:, r, 0:P]).then_inc(copied, 1)

            def stored(q, r):
                return q // R * 16 if isinstance(q, int) else uses[0] * 16
            uses = [None]
            whole = NTURN // R
            for r in range(R):
                copy(r, r, True)
            with act.Fori(1, whole) as n:
                uses[0] = n
                for r in range(R):
                    copy(n * R + r, r, False)
            for r in range(NTURN - whole * R):
                copy(whole * R + r, r, False)


class Batch:

    def __init__(self, turn, k):
        at = 0 if turn is None else turn
        self.n, self.i, self.use = at * KB + k, at * NSL + k // KS, at + k // KB
        self.k = k % KB
        self.h, self.b = self.k // KS, self.k % KS
        self.last = turn is None and k == NTURN * KB - 1


def run_batches(eng, stages):
    n_batches = NTURN * KB

    def at(turn, m):
        for lag, stage in stages:
            if turn is not None or 0 <= m - lag < n_batches:
                stage(Batch(turn, m - lag))
    for m in range(KB):
        at(None, m)
    with eng.Fori(1, NTURN) as turn:
        for m in range(KB):
            at(turn, m)
    for m in range(n_batches, n_batches + max(lag for lag, _ in stages)):
        at(None, m)


def edge_pass(K, name, gather, scatter, kind, tables, acc_out, cnt_out=None):
    nc = K.nc
    last = kind in ("scalar", "vector", "both")
    G = 1 if last else 2
    RM, RO, RZ = 4, 4, 2
    NTAB = len(tables)
    WCOLS = {"scalar": (0, F * F), "vector": (F * F, F * F + F * NV), "both": (0, (F + NV) * F)}.get(kind, (0, 0))
    WN = WCOLS[1] - WCOLS[0]
    NLOAD = 3 if kind == "copy" else 4
    NQ = {"scalar": F, "vector": F, "both": F + NV}.get(kind, 0)
    with ExitStack() as ctx:
        def sb(n, shape, dt=F32):
            return K.sb(f"{name}_{n}", shape, dt, ctx)

        def sem(n):
            return K.sem(f"{name}_{n}")

        idxb = sb("idxb", [P, NSL, 2, SB * P], BF16)
        natb = sb("natb", [P, NSL, SB, 4])
        offb = sb("offb", [1, NSL, 4, SB], I32)
        ohT = sb("ohT", [P, NSL, SB * P], BF16)
        ohlo = sb("ohlo", [P, NSL, SB, P])
        ohhi = sb("ohhi", [P, NSL, SB, HI])
        masked = sb("masked", [P, RM, NTAB, BT * P])
        msg = sb("msg", [P, RO, BT, F])
        outer = sb("outer", [P, RO, BT, HI, F])
        zero = sb("zero", [P, 512], BF16)
        if kind != "copy":
            rows = sb("rows", [P, NSL, SB, ROW])
        if kind == "product":
            prod = sb("prod", [P, BT, DE, F])
            tsum = sb("tsum", [P, RO, BT, F])
        if last:
            hT = sb("hT", [HW, RZ, BT * P])
            z = sb("z", [P, RZ, BT, NTAB * F])
            zz = sb("zz", [P, RZ, BT, F + NV])
            prod = sb("prod", [P, BT, WN])
            dot = sb("dot", [P, BT, NV, 3])
            mv = sb("mv", [P, BT, NV])
        acc = K.ps(ctx, f"{name}_acc", [P, 4 * 512])
        gps = K.ps(ctx, f"{name}_gps", [P, G, 512])
        if last:
            turn_ps = K.ps(ctx, f"{name}_turn", [P, 512])
            w_ps = K.ps(ctx, f"{name}_w", [P, 2, 512])
            fold_ps = turn_ps
        else:
            fold_ps = K.ps(ctx, f"{name}_fold", [P, 512])
            if cnt_out is not None:
                cnt_ps = K.ps(ctx, f"{name}_cnt", [P, 512])

        loaded = [sem(f"loaded{h}") for h in range(NSL)]
        zero_ready, pe_go, flushed = sem("zero_ready"), sem("pe_go"), sem("flushed")
        oh_ready, gathered, masks, folded, messages, outers, scattered = (
            sem("oh_ready"), sem("gathered"), sem("masks"), sem("folded"), sem("messages"), sem("outers"), sem("scattered"))
        if kind != "copy":
            dve_step, sums = sem("dve_step"), sem("sums")
        if last:
            turned, hT_ready, z_ready, weights, contracted = (sem("turned"), sem("hT_ready"), sem("z_ready"),
                                                              sem("weights"), sem("contracted"))

        def done(eng, s, n):
            eng.wait_ge(s, n + LEAD)

        def arrived(eng, B):
            eng.wait_ge(loaded[B.h], B.use * (16 * NLOAD) + 16 * NLOAD)

        block = ctx.enter_context(nc.Block())

        @block.sync
        def _(sp):
            def load(i, h, turn, first):
                if not first:
                    done(sp, scattered, i * KS - (NSL - 1) * KS)
                sp.dma_start(idxb[:, h, :, :], K.idxT_d[bass.ds(turn, 1), :].rearrange(
                    "o (k e) -> (o k) e", k=4)[2 * gather:2 * gather + 2, h * SB * P:(h + 1) * SB * P].partition_broadcast(P)
                    ).then_inc(loaded[h], 16)
                sp.dma_start(natb[:, h, :, :].rearrange("p t c -> p (t c)"),
                             K.nat_d[:, bass.ds(i * (SB * 4), SB * 4)]).then_inc(loaded[h], 16)
                sp.dma_start(offb[0:1, h, :, :], K.offs_d[:, bass.ds(i * SB, SB)].unsqueeze(0)).then_inc(loaded[h], 16)
                if kind != "copy":
                    sp.dma_start(rows[:, h, :, :].rearrange("p t c -> p (t c)"),
                                 K.rows_d.rearrange("(p t) c -> p (t c)", p=P)[:, bass.ds(i * (SB * ROW), SB * ROW)]
                                 ).then_inc(loaded[h], 16)
            for h in range(NSL):
                load(h, h, 0, True)
            with sp.Fori(1, NTURN) as turn:
                for h in range(NSL):
                    load(turn * NSL + h, h, turn, False)

        @block.tensor
        def _(pe):
            for s in (gathered, folded, scattered) + ((turned, weights) if last else ()):
                pe.sem_inc(s, LEAD)
            pe.wait_ge(zero_ready, 1)
            for bank in range(4):
                pe.matmul(acc[:, bank * 512:(bank + 1) * 512], zero[:, 0:P], zero[:], start=True, stop=False,
                          skip_group_check=True)
            if cnt_out is not None:
                pe.matmul(cnt_ps[:], zero[:, 0:P], zero[:], start=True, stop=False, skip_group_check=True)

            def offsets(B, row):
                return nc.values_load_multi_w_load_instructions(
                    offb[0:1, B.h, row, B.b * BT:(B.b + 1) * BT], engines=(mybir.EngineType.PE,), min_val=0,
                    max_val=(NG - 1) * (P if row < 2 else HI), skip_runtime_bounds_check_because="made on the chip, clamped")[1]

            def gather_blocks(B, tab):
                if tab == 0:
                    arrived(pe, B)
                    done(pe, oh_ready, B.i + 1)
                done(pe, masks, B.n * NTAB + tab + 1 - G)
                pe.sem_inc(pe_go, 1)
                for t, off in enumerate(offsets(B, gather)):
                    for part in range(3):
                        ins = pe.matmul(gps[:, B.k % G, t * P:(t + 1) * P], tables[tab][:, part, bass.ds(off, P)],
                                        ohT[:, B.h, (B.b * BT + t) * P:(B.b * BT + t + 1) * P],
                                        start=(part == 0), stop=(part == 2))
                ins.then_inc(gathered, 1)

            def turn_hidden(B):
                at = C_HA if kind != "both" else C_HB
                done(pe, z_ready, B.n - 1)
                done(pe, hT_ready, B.n)
                pe.sem_inc(pe_go, 1)
                for t in range(BT):
                    ins = pe.transpose(turn_ps[0:HW, t * P:(t + 1) * P], rows[:, B.h, B.b * BT + t, at:at + HW],
                                       K.c("ident"))
                ins.then_inc(turned, 1)

            def fold(B):
                done(pe, masks, (B.n + 1) * NTAB)
                if last:
                    done(pe, hT_ready, B.n + (1 if B.last else 2))
                else:
                    done(pe, messages if kind == "copy" else sums, B.n)
                for t in range(BT):
                    for tab in range(NTAB):
                        m = masked[:, B.k % RM, tab, t * P:(t + 1) * P]
                        if kind == "product":
                            ins = pe.matmul(fold_ps[:, t * P:(t + 1) * P], m, K.w_msg[:], start=True, stop=True)
                        else:
                            at = (t * NTAB + tab) * F
                            ins = pe.matmul(fold_ps[:, at:at + F], m, K.c("fold"), start=True, stop=True)
                ins.then_inc(folded, 1)

            def edge_weights(B):
                for t in range(BT):
                    done(pe, contracted, B.n * BT + t - 1)
                    if t == 0:
                        done(pe, hT_ready, B.n + 1)
                    pe.matmul(w_ps[:, t % 2, 0:WN], hT[:, B.k % RZ, t * P:(t + 1) * P],
                              K.w2[0 if kind != "both" else 1][:, WCOLS[0]:WCOLS[1]], start=True,
                              stop=True).then_inc(weights, 1)

            def scatter_sums(B):
                done(pe, outers, B.n + 1)
                pe.sem_inc(pe_go, 1)
                offs = offsets(B, scatter)
                for t, off in enumerate(offs):
                    ins = pe.matmul(acc[:, bass.ds(off, P)], ohlo[:, B.h, B.b * BT + t, :],
                                    outer[:, B.k % RO, t, :, :].rearrange("p a f -> p (a f)"),
                                    start=False, stop=False, skip_group_check=True)
                if cnt_out is not None:
                    for t, off in enumerate(offsets(B, 2 + scatter)):
                        ins = pe.matmul(cnt_ps[:, bass.ds(off, HI)], ohlo[:, B.h, B.b * BT + t, :],
                                        ohhi[:, B.h, B.b * BT + t, :], start=False, stop=False, skip_group_check=True)
                ins.then_inc(scattered, 1)

            if last:
                stages = [(0, lambda B: gather_blocks(B, 0)), (0, turn_hidden), (3, scatter_sums)]
                if NTAB == 2:
                    stages.append((0, lambda B: gather_blocks(B, 1)))
                stages += [(1, fold), (1, edge_weights)]
            else:
                stages = [(0, lambda B: gather_blocks(B, 0)), (1, fold), (3, scatter_sums)]
            run_batches(pe, stages)

        @block.vector
        def _(v):
            for s in (oh_ready, masks) + ((sums, dve_step) if kind != "copy" else ()) + ((contracted, messages) if last else ()):
                v.sem_inc(s, LEAD)
            if kind == "vector":
                v.memset(msg[:], 0.0)
            v.memset(zero[:], 0.0).then_inc(zero_ready, 1)
            v.wait_ge(zero_ready, 1)

            def one_hots(i, h, use):
                done(v, scattered, i * KS - (NSL - 1) * KS)
                v.wait_ge(loaded[h], use * (16 * NLOAD) + 16 * NLOAD)
                v.tensor_tensor(ohhi[:, h, :, :], natb[:, h, :, 2 * scatter + 1].unsqueeze(2).to_broadcast([P, SB, HI]),
                                K.c("iota8").unsqueeze(1).to_broadcast([P, SB, HI]), ALU.is_equal)
                v.tensor_scalar(ohT[:, h, :], idxb[:, h, 0, :], K.c("lo"), None, ALU.is_equal)
                for t in range(SB):
                    ins = v.tensor_scalar(ohlo[:, h, t, :], K.c("iota"), natb[:, h, t, 2 * scatter:2 * scatter + 1], None,
                                          ALU.is_equal)
                ins.then_inc(oh_ready, 1)

            def make_one_hots(B):
                if B.b == 0:
                    one_hots(B.i, B.h, B.use)

            def mask(B, tab):
                done(v, gathered, B.n * NTAB + tab + 1)
                done(v, folded, B.n - RM + 1)
                v.scalar_tensor_tensor(masked[:, B.k % RM, tab, :], idxb[:, B.h, 1, B.b * BT * P:(B.b + 1) * BT * P],
                                       K.c("blk"), gps[:, B.k % G, :], ALU.is_equal, ALU.mult).then_inc(masks, 1)

            def product(B):
                done(v, folded, B.n + 1)
                done(v, sums, B.n)
                a8 = rows[:, B.h, B.b * BT:(B.b + 1) * BT, C_A8:C_A8 + DE]
                v.tensor_tensor(prod[:], fold_ps[:].rearrange("p (t j f) -> p t j f", t=BT, j=DE),
                                a8.unsqueeze(3).to_broadcast([P, BT, DE, F]), ALU.mult).then_inc(dve_step, 1)
                done(v, dve_step, B.n + 1)
                done(v, messages, B.n - RO + 1)
                v.tensor_reduce(tsum[:, B.k % RO, :, :], prod[:].rearrange("p t j f -> p t f j"), AX.X,
                                ALU.add).then_inc(sums, 1)

            def contract(B):
                done(v, z_ready, B.n + 1)
                done(v, sums, B.n)
                zsrc = z[:, B.k % RZ, :, :]
                if kind == "both":
                    r = rows[:, B.h, B.b * BT:(B.b + 1) * BT, C_R:C_R + 3]
                    v.tensor_copy(zz[:, B.k % RZ, :, 0:F], z[:, B.k % RZ, :, 0:F])
                    v.tensor_tensor(dot[:], z[:, B.k % RZ, :, F:F + 3 * NV].rearrange("p t (j c) -> p t j c", c=3),
                                    r.unsqueeze(2).to_broadcast([P, BT, NV, 3]), ALU.mult).then_inc(dve_step, 1)
                    done(v, dve_step, 2 * B.n + 1)
                    v.tensor_reduce(zz[:, B.k % RZ, :, F:F + NV], dot[:], AX.X, ALU.add).then_inc(dve_step, 1)
                    done(v, dve_step, 2 * B.n + 2)
                    zsrc = zz[:, B.k % RZ, :, :]
                nj = WN // NQ
                for t in range(BT):
                    done(v, weights, B.n * BT + t + 1)
                    v.tensor_tensor(prod[:, t, :].rearrange("p (q j) -> p q j", j=nj),
                                    w_ps[:, t % 2, 0:WN].rearrange("p (q j) -> p q j", j=nj),
                                    zsrc[:, t, :].unsqueeze(2).to_broadcast([P, NQ, nj]), ALU.mult).then_inc(contracted, 1)
                done(v, contracted, B.n * BT + BT)
                done(v, outers, B.n - RO + 1)
                view = prod[:].rearrange("p t (q j) -> p t j q", j=nj)
                if kind == "vector":
                    v.tensor_reduce(mv[:], view, AX.X, ALU.add).then_inc(sums, 1)
                    done(v, sums, B.n + 1)
                    v.tensor_tensor(msg[:, B.k % RO, :, 0:3 * NV].rearrange("p t (j c) -> p t j c", c=3),
                                    mv[:].unsqueeze(3).to_broadcast([P, BT, NV, 3]),
                                    rows[:, B.h, B.b * BT:(B.b + 1) * BT, C_R:C_R + 3].unsqueeze(2).to_broadcast(
                                        [P, BT, NV, 3]), ALU.mult).then_inc(messages, 1)
                    done(v, messages, B.n + 1)
                else:
                    v.tensor_reduce(msg[:, B.k % RO, :, :], view, AX.X, ALU.add).then_inc(messages, 1)
                    done(v, messages, B.n + 1)
                    v.sem_inc(sums, 1)

            stages = [(KS, lambda B: mask(B, 0))]
            if NTAB == 2:
                stages.append((KS, lambda B: mask(B, 1)))
            if kind == "product":
                stages += [(KS + 1, product)]
            if last:
                stages += [(KS + 1, contract)]
            stages += [(0, make_one_hots)]
            run_batches(v, stages)
            done(v, scattered, NTURN * KB)
            ins = v.tensor_copy(acc_out[:], acc[:, 0:NW])
            if cnt_out is not None:
                ins.then_inc(flushed, 1)
                ins = v.tensor_copy(cnt_out[:], cnt_ps[:, 0:NBLK])
            ins.then_inc(flushed, 1)

        @block.scalar
        def _(act):
            if last:
                act.sem_inc(hT_ready, LEAD)
                act.sem_inc(z_ready, LEAD)

                def take_hidden(B):
                    done(act, turned, B.n + 1)
                    done(act, weights, (B.n - RZ + 1) * BT)
                    nc.scalar.copy(hT[:, B.k % RZ, :], turn_ps[0:HW, :]).then_inc(hT_ready, 1)

                def take_rows(B):
                    done(act, folded, B.n + 1)
                    done(act, sums, B.n - RZ + 1)
                    nc.scalar.copy(z[:, B.k % RZ, :, :].rearrange("p t f -> p (t f)"),
                                   fold_ps[:, 0:BT * NTAB * F]).then_inc(z_ready, 1)
                run_batches(act, [(0, take_hidden), (1, take_rows)])
            else:
                act.sem_inc(messages, LEAD)

                def message(B):
                    done(act, outers, B.n - RO + 1)
                    if kind == "copy":
                        done(act, folded, B.n + 1)
                        nc.scalar.copy(msg[:, B.k % RO, :, :].rearrange("p t f -> p (t f)"),
                                       fold_ps[:, 0:BT * F]).then_inc(messages, 1)
                    else:
                        done(act, sums, B.n + 1)
                        nc.scalar.activation(msg[:, B.k % RO, :, :], tsum[:, B.k % RO, :, :], ACT.Silu,
                                             scale=float(1.0 / np.sqrt(F * DE))).then_inc(messages, 1)
                run_batches(act, [(0, message)])

        @block.gpsimd
        def _(pool):
            pool.sem_inc(outers, LEAD)

            def spread(B):
                done(pool, messages, B.n + 1)
                done(pool, scattered, B.n - RO + 1)
                nc.gpsimd.tensor_tensor(
                    outer[:, B.k % RO, :, :, :],
                    ohhi[:, B.h, B.b * BT:(B.b + 1) * BT, :].unsqueeze(3).to_broadcast([P, BT, HI, F]),
                    msg[:, B.k % RO, :, :].unsqueeze(2).to_broadcast([P, BT, HI, F]), ALU.mult).then_inc(outers, 1)
            run_batches(pool, [(0, spread)])



BDS = ["L0_gnn_W_msg_lin", "L0_gnn_W_upd_lin", "L1_gnn_w1a", "L1_gnn_w1b", "L1_gnn_w2a", "L1_gnn_w2b", "L2_gnn_W"]
VECS = ["L1_gnn_b1a", "L1_gnn_b1b", "L1_gnn_b2a", "L1_gnn_b2b", "L2_gnn_b", "L3_gnn_bn0_gs", "L3_gnn_bn0_bs",
        "L3_gnn_bn1_gs", "L3_gnn_bn1_bs", "L3_gnn_bn0_gv", "L1_gnn_eps1", "L1_gnn_eps2"]
EPS = 1e-5


def setup_nodes(K):
    nc = K.nc
    K.x = K.sb("x", [P, NBLK, F])
    K.acc = K.sb("acc", [P, NW])
    K.keep = K.sb("keep", [P, NBLK, F])
    K.src_count = K.sb("src_count", [P, NBLK])
    K.dst_count = K.sb("dst_count", [P, NBLK])
    K.tab = [K.sb(f"tab{n}", [P, 3, NW], BF16) for n in range(2)]
    K.bd = K.sb("bd", [P, len(BDS), P])
    K.vecs = K.sb("vecs", [P, len(VECS), F])
    K.w_msg = K.sb("w_msg", [P, DE * F])
    K.w_upd = K.sb("w_upd", [P, HI, F * F])
    K.w2 = [K.sb(f"w2_{n}", [HW, (F + NV) * F]) for n in range(2)]
    cleared, loaded, loaded2 = K.sem("n_cleared"), K.sem("n_loaded"), K.sem("n_loaded2")
    whole = N_NODES // P
    jobs = []
    for w, n in enumerate(BDS):
        jobs += [(K.bd[F * k:F * k + F, w, F * k:F * k + F], K.ins[n]) for k in range(HI)]
    for k in range(HI):
        jobs.append((K.w_msg[F * k:F * k + F, :], K.ins["L0_gnn_W_msg_tp"].rearrange("i j h -> i (j h)")))
        jobs.append((K.w_upd[F * k:F * k + F, k, :], K.ins["L0_gnn_W_upd_tp"].rearrange("i h k -> i (h k)")))
    for w, n in enumerate(VECS):
        a = K.ins[n]
        jobs.append((K.vecs[:, w, 0:a.shape[0]], a.partition_broadcast(P)))
    for n in range(2):
        jobs.append((K.w2[n][0:DH, :], K.ins[f"L3_gnn_fc{n}_w2"]))
        jobs.append((K.w2[n][DH:HW, :], K.ins[f"L3_gnn_fc{n}_b2"].rearrange("(a d) -> a d", a=1)))
    jobs.append((K.x[:, 0:whole, :], K.ins["x"][0:whole * P].rearrange("(b p) f -> p b f", p=P)))
    jobs.append((K.x[0:N_NODES - whole * P, whole, :], K.ins["x"][whole * P:N_NODES]))
    with nc.Block() as block:
        @block.vector
        def _(v):
            v.memset(K.bd[:], 0.0)
            v.memset(K.w_upd[:], 0.0)
            v.memset(K.vecs[:], 0.0)
            v.memset(K.x[:], 0.0).then_inc(cleared, 1)

        @block.sync
        def _(sp):
            sp.wait_ge(cleared, 1)
            for dst, src in jobs[0::2]:
                sp.dma_start(dst, src).then_inc(loaded, 16)
            sp.wait_ge(loaded, 16 * len(jobs[0::2]))

        @block.scalar
        def _(act):
            act.wait_ge(cleared, 1)
            for dst, src in jobs[1::2]:
                act.dma_start(dst, src).then_inc(loaded2, 16)
            act.wait_ge(loaded2, 16 * len(jobs[1::2]))


class Nodes:

    def __init__(self, K, name, linears=(), functions=(), totals=0, update=False):
        self.K, self.nc, self.name = K, K.nc, name
        self.linears, self.functions, self.totals, self.update = linears, functions, totals, update
        self.ctx = ExitStack()

    def __enter__(self):
        K, n, ctx = self.K, self.name, self.ctx
        self.y = K.sb(f"{n}_y", [P, NBLK, F], F32, ctx)
        self.sq = K.sb(f"{n}_sq", [P, NBLK, F], F32, ctx)
        self.s = K.sb(f"{n}_s", [P, NBLK], F32, ctx)
        self.r = K.sb(f"{n}_r", [P, NBLK], F32, ctx)
        self.part = K.sb(f"{n}_part", [P, F], F32, ctx)
        self.stat = K.sb(f"{n}_stat", [P, 4, F], F32, ctx)
        self.xT = K.sb(f"{n}_xT", [P, NW], F32, ctx)
        self.ones = K.sb(f"{n}_ones", [P, P], F32, ctx)
        self.turn_ps = K.ps(ctx, f"{n}_turn_ps", [P, 4 * 512])
        self.lin_ps = K.ps(ctx, f"{n}_lin_ps", [P, 4 * 512])
        self.dve = K.sem(f"{n}_dve")
        self.lin_in, self.lin_out = K.sem(f"{n}_lin_in"), K.sem(f"{n}_lin_out")
        self.turned, self.taken = K.sem(f"{n}_turned"), K.sem(f"{n}_taken")
        self.func_in, self.func_out = K.sem(f"{n}_func_in"), K.sem(f"{n}_func_out")
        self.tot_in, self.tot_out = K.sem(f"{n}_tot_in"), K.sem(f"{n}_tot_out")
        self.n_lin = self.n_func = self.n_tot = 0
        self.block = ctx.enter_context(self.nc.Block())
        return self

    def __exit__(self, *e):
        return self.ctx.__exit__(*e)

    def linear(self):
        self.n_lin += 1
        self.v.sem_inc(self.lin_in, 1)
        self.v.wait_ge(self.lin_out, self.n_lin)
        return self.lin_ps[:, 0:NW].rearrange("p (b f) -> p b f", f=F)

    def function(self):
        self.n_func += 1
        self.v.sem_inc(self.func_in, 1)
        self.v.wait_ge(self.func_out, self.n_func)

    def total(self):
        self.n_tot += 1
        self.v.sem_inc(self.tot_in, 1)
        self.v.wait_ge(self.tot_out, self.n_tot)
        return self.lin_ps[:, 0:F]

    def start_vector(self, v):
        self.v, self.step = v, Chain(v, self.dve)
        self.step(v.memset(self.ones[:], 1.0))

    def vec(self, name, n=F):
        return self.K.vecs[:, VECS.index(name), 0:n]

    def row(self, name):
        return self.vec(name).unsqueeze(1).to_broadcast([P, NBLK, F])

    def each(self, a):
        return a[:].unsqueeze(2).to_broadcast([P, NBLK, F])

    def split(self, tab, a):
        v, step, flat = self.v, self.step, a.rearrange("p b f -> p (b f)")
        rest = self.sq[:].rearrange("p b f -> p (b f)")
        step(v.tensor_copy(tab[:, 0, :], flat))
        step(v.tensor_tensor(rest, flat, tab[:, 0, :], ALU.subtract))
        step(v.tensor_copy(tab[:, 1, :], rest))
        step(v.tensor_tensor(rest, rest, tab[:, 1, :], ALU.subtract))
        step(v.tensor_copy(tab[:, 2, :], rest))

    def layernorm(self, out):
        v, step = self.v, self.step
        step(v.tensor_reduce(self.s[:], self.y[:], AX.X, ALU.add))
        step(v.tensor_scalar(self.s[:], self.s[:], 1.0 / F, None, ALU.mult))
        step(v.tensor_tensor(self.y[:], self.y[:], self.each(self.s), ALU.subtract))
        step(v.tensor_tensor(self.sq[:], self.y[:], self.y[:], ALU.mult))
        step(v.tensor_reduce(self.r[:], self.sq[:], AX.X, ALU.add))
        step(v.tensor_scalar(self.r[:], self.r[:], 1.0 / F, EPS, ALU.mult, ALU.add))
        self.function()
        step(v.reciprocal(self.r[:], self.r[:]))
        step(v.tensor_tensor(out, self.y[:], self.each(self.r), ALU.mult))

    def run_tensor(self, pe):
        K = self.K
        for k, (src, w) in enumerate(self.linears):
            pe.wait_ge(self.lin_in, k + 1)
            flat = src.rearrange("p b f -> p (b f)")
            for g in range(NG):
                ins = pe.transpose(self.turn_ps[:, g * P:(g + 1) * P], flat[:, g * P:(g + 1) * P], K.c("ident"))
            ins.then_inc(self.turned, 1)
            pe.wait_ge(self.taken, k + 1)
            if w is None:
                self.update_products(pe)
                continue
            for g in range(NG):
                ins = pe.matmul(self.lin_ps[:, g * P:(g + 1) * P], self.xT[:, g * P:(g + 1) * P], K.bd[:, BDS.index(w), :],
                                start=True, stop=True)
            ins.then_inc(self.lin_out, 1)
        for k in range(self.totals):
            pe.wait_ge(self.tot_in, k + 1)
            pe.matmul(self.lin_ps[:, 0:F], self.ones[:], self.part[:], start=True, stop=True).then_inc(self.tot_out, 1)

    def run_scalar(self, act):
        lin = func = 0
        for f in self.functions:
            if f is None:
                lin += 1
                act.wait_ge(self.turned, lin)
                self.nc.scalar.copy(self.xT[:], self.turn_ps[:, 0:NW]).then_inc(self.taken, 1)
            else:
                func += 1
                act.wait_ge(self.func_in, func)
                out, in_, name, scale = f
                self.nc.scalar.activation(out, in_, name, scale=scale).then_inc(self.func_out, 1)

    def engines(self, lead):
        @self.block.vector
        def _(v):
            self.start_vector(v)
            lead(v)

        @self.block.tensor
        def _(pe):
            pe.wait_ge(self.dve, 1)
            self.run_tensor(pe)

        @self.block.scalar
        def _(act):
            self.run_scalar(act)


def sqrt_r(N):
    return (N.r[:], N.r[:], ACT.Sqrt, 1.0)


def acc_nodes(K):
    return K.acc[:].rearrange("p (b f) -> p b f", f=F)


def first_table(K):
    with Nodes(K, "n0") as N:
        N.engines(lambda v: N.split(K.tab[0], K.x[:]))


def update_first(K):
    nc = K.nc
    lin_norm, upd_norm = 1.0 / np.sqrt(F), 1.0 / np.sqrt(F * F)
    with Nodes(K, "n1") as N:
        agg = K.sb("n1_agg", [P, NBLK, F], F32, N.ctx)
        prod = K.sb("n1_prod", [P, 4, F, F], F32, N.ctx)
        upd_ready, upd_used = K.sem("n1_upd_ready"), K.sem("n1_upd_used")
        half = HI // 2

        def bank(n):
            return N.lin_ps[:, n % 2 * 1024:n % 2 * 1024 + half * F * F]

        def update_products(pe):
            for n in range(2 * NG):
                if n >= 2:
                    pe.wait_ge(upd_used, n - 1)
                for k in range(half):
                    ins = pe.matmul(bank(n)[:, k * F * F:(k + 1) * F * F], N.xT[:, n // 2 * P:(n // 2 + 1) * P],
                                    K.w_upd[:, n % 2 * half + k, :], start=True, stop=True)
                ins.then_inc(upd_ready, 1)
        N.update_products = update_products
        N.linears = [(acc_nodes(K), "L0_gnn_W_msg_lin"), (K.x[:], None), (N.y[:], "L0_gnn_W_upd_lin")]
        N.functions = [None, None, (N.y[:], N.y[:], ACT.Silu, float(lin_norm * upd_norm)), None, sqrt_r(N)]

        def lead(v):
            step = N.step
            step(v.tensor_copy(agg[:], N.linear()))
            N.n_lin += 1
            v.sem_inc(N.lin_in, 1)
            for n in range(2 * NG):
                v.wait_ge(upd_ready, n + 1)
                blocks = slice(n * half, (n + 1) * half)
                v.tensor_tensor(prod[:], bank(n).rearrange("p (b h k) -> p b h k", h=F, k=F),
                                agg[:, blocks, :].unsqueeze(3).to_broadcast([P, half, F, F]), ALU.mult).then_inc(upd_used, 1)
                v.wait_ge(upd_used, n + 1)
                step(v.tensor_reduce(N.y[:, blocks, :], prod[:].rearrange("p b h k -> p b k h"), AX.X, ALU.add))
            N.n_lin -= 1
            N.function()
            u = N.linear()
            step(v.scalar_tensor_tensor(N.y[:], K.x[:], 2.0 / lin_norm, u, ALU.mult, ALU.add))
            step(v.tensor_scalar(N.y[:], N.y[:], float(lin_norm), None, ALU.mult))
            N.layernorm(K.x[:])
            N.split(K.tab[0], K.x[:])
        N.engines(lead)


def gin(K, N, v, x, eps, wa, wb):
    step = N.step
    step(v.tensor_scalar(N.s[:, 0:1], N.vec(eps, 1), 1.0, None, ALU.add))
    flat = x.rearrange("p b f -> p (b f)")
    step(v.scalar_tensor_tensor(N.y[:].rearrange("p b f -> p (b f)"), flat, N.s[:, 0:1], K.acc[:], ALU.mult, ALU.add))
    step(v.tensor_tensor(N.y[:], N.linear(), N.row(wa), ALU.add))
    step(v.tensor_scalar(N.y[:], N.y[:], 0.0, None, ALU.max))
    step(v.tensor_tensor(N.y[:], N.linear(), N.row(wb), ALU.add))


def gin_first(K):
    with Nodes(K, "n2") as N:
        N.linears = [(N.y[:], "L1_gnn_w1a"), (N.y[:], "L1_gnn_w1b")]
        N.functions = [None, None]

        def lead(v):
            gin(K, N, v, K.x[:], "L1_gnn_eps1", "L1_gnn_b1a", "L1_gnn_b1b")
            N.step(v.tensor_scalar(K.keep[:], N.y[:], 0.0, None, ALU.max))
            N.split(K.tab[0], K.keep[:])
        N.engines(lead)


def gin_second(K):
    with Nodes(K, "n3") as N:
        dinv = K.dst_count
        N.linears = [(N.y[:], "L1_gnn_w2a"), (N.y[:], "L1_gnn_w2b"), (K.x[:], "L2_gnn_W")]
        N.functions = [None, None, (N.sq[:], N.y[:], ACT.Exp, 1.0), (N.s[:], N.s[:], ACT.Ln, 1.0), sqrt_r(N),
                       (dinv[:], dinv[:], ACT.Sqrt, 1.0), None]

        def lead(v):
            step = N.step
            gin(K, N, v, K.keep[:], "L1_gnn_eps2", "L1_gnn_b2a", "L1_gnn_b2b")
            step(v.tensor_reduce(N.s[:], N.y[:], AX.X, ALU.max))
            step(v.tensor_tensor(N.y[:], N.y[:], N.each(N.s), ALU.subtract))
            N.function()
            step(v.tensor_reduce(N.s[:], N.sq[:], AX.X, ALU.add))
            N.function()
            step(v.tensor_tensor(N.y[:], N.y[:], N.each(N.s), ALU.subtract))
            step(v.tensor_tensor(N.y[:], N.y[:], K.x[:], ALU.add))
            N.layernorm(K.x[:])
            step(v.tensor_scalar(dinv[:], dinv[:], 1.0, None, ALU.add))
            N.function()
            step(v.reciprocal(dinv[:], dinv[:]))
            step(v.tensor_tensor(K.keep[:], N.linear(), N.each(dinv), ALU.mult))
            N.split(K.tab[0], K.keep[:])
        N.engines(lead)


def gcn(K):
    with Nodes(K, "n4") as N:
        N.functions = [sqrt_r(N)]

        def lead(v):
            step = N.step
            step(v.tensor_tensor(N.y[:], acc_nodes(K), K.keep[:], ALU.add))
            step(v.tensor_tensor(N.y[:], N.y[:], N.each(K.dst_count), ALU.mult))
            step(v.tensor_tensor(N.y[:], N.y[:], N.row("L2_gnn_b"), ALU.add))
            step(v.tensor_tensor(N.y[:], N.y[:], K.x[:], ALU.add))
            N.layernorm(K.x[:])
            N.split(K.tab[0], K.x[:])
        N.engines(lead)


def batch_norm(K, N, v, a, gain, bias, which):
    step = N.step
    mean, scale = N.stat[:, 0, :], N.stat[:, 1, :]
    valid = K.c("valid").unsqueeze(2).to_broadcast([P, NBLK, F])

    def over_nodes(x, out, bias):
        step(v.tensor_reduce(N.part[:], x.rearrange("p b f -> p f b"), AX.X, ALU.add))
        step(v.tensor_scalar(out, N.total(), 1.0 / N_NODES, bias, ALU.mult, ALU.add))

    def spread(x):
        return x.unsqueeze(1).to_broadcast([P, NBLK, F])
    over_nodes(a, mean, 0.0)
    step(v.tensor_tensor(a, a, spread(mean), ALU.subtract))
    step(v.tensor_tensor(N.sq[:], a, a, ALU.mult))
    step(v.tensor_tensor(N.sq[:], N.sq[:], valid, ALU.mult))
    over_nodes(N.sq[:], scale, EPS)
    N.function()
    step(v.reciprocal(scale, scale))
    step(v.tensor_tensor(scale, scale, N.vec(gain), ALU.mult))
    step(v.tensor_tensor(a, a, spread(scale), ALU.mult))
    step(v.tensor_tensor(a, a, spread(N.vec(bias)), ALU.add))


def sqrt_stat(N, k):
    return (N.stat[:, k, :], N.stat[:, k, :], ACT.Sqrt, 1.0)


def mean_of(K, N, v, factor):
    N.step(v.tensor_scalar(N.r[:], K.src_count[:], 1.0, None, ALU.max))
    N.step(v.reciprocal(N.r[:], N.r[:]))
    N.step(v.tensor_scalar(N.r[:], N.r[:], float(factor), None, ALU.mult))


def norm_first(K):
    with Nodes(K, "n6", totals=3) as N:
        N.functions = [sqrt_stat(N, 1), sqrt_stat(N, 2)]

        def lead(v):
            step = N.step
            mean_of(K, N, v, 1.0 / np.sqrt(F))
            step(v.tensor_tensor(N.y[:], K.keep[:], N.each(N.r), ALU.mult))
            batch_norm(K, N, v, N.y[:], "L3_gnn_bn0_gs", "L3_gnn_bn0_bs", 0)
            N.split(K.tab[0], N.y[:])
            step(v.tensor_scalar(N.r[:], N.r[:], float(np.sqrt(3.0)), None, ALU.mult))
            step(v.tensor_tensor(N.y[:], acc_nodes(K), N.each(N.r), ALU.mult))
            step(v.tensor_tensor(N.sq[:], N.y[:], N.y[:], ALU.mult))
            step(v.tensor_reduce(N.part[:], N.sq[:].rearrange("p b f -> p f b"), AX.X, ALU.add))
            tot = N.total()
            scale = N.stat[:, 2, 0:NV]
            step(v.memset(N.stat[:, 2, :], 1.0))
            step(v.tensor_reduce(scale, tot[:, 0:3 * NV].rearrange("p (j c) -> p j c", c=3), AX.X, ALU.add))
            step(v.tensor_scalar(scale, scale, 1.0 / (3 * N_NODES), EPS, ALU.mult, ALU.add))
            N.function()
            step(v.reciprocal(scale, scale))
            step(v.tensor_tensor(scale, scale, N.vec("L3_gnn_bn0_gv", NV), ALU.mult))
            step(v.memset(N.stat[:, 3, :], 0.0))
            step(v.tensor_copy(N.stat[:, 3, 0:3 * NV].rearrange("p (j c) -> p j c", c=3),
                               scale.unsqueeze(2).to_broadcast([P, NV, 3])))
            step(v.tensor_tensor(N.y[:], N.y[:], N.stat[:, 3, :].unsqueeze(1).to_broadcast([P, NBLK, F]), ALU.mult))
            N.split(K.tab[1], N.y[:])
        N.engines(lead)


def finish(K):
    whole = N_NODES // P
    with Nodes(K, "n7", totals=2) as N:
        N.functions = [sqrt_stat(N, 1), sqrt_r(N)]
        stored = K.sem("n7_stored")

        def lead(v):
            step = N.step
            mean_of(K, N, v, 1.0 / np.sqrt(F + NV))
            step(v.tensor_tensor(N.y[:], acc_nodes(K), N.each(N.r), ALU.mult))
            batch_norm(K, N, v, N.y[:], "L3_gnn_bn1_gs", "L3_gnn_bn1_bs", 0)
            step(v.tensor_tensor(N.y[:], N.y[:], K.x[:], ALU.add))
            N.layernorm(K.keep[:])
            v.sem_inc(N.lin_in, 1)
        N.engines(lead)

        @N.block.sync
        def _(sp):
            sp.wait_ge(N.lin_in, 1)
            sp.dma_start(K.out[0:whole * P].rearrange("(b p) f -> p b f", p=P), K.keep[:, 0:whole, :]).then_inc(stored, 16)
            sp.dma_start(K.out[whole * P:N_NODES], K.keep[0:N_NODES - whole * P, whole, :]).then_inc(stored, 16)
            sp.wait_ge(stored, 32)


SRC, DST = 0, 1


def program(nc, ins, out):
    with ExitStack() as ctx:
        K = Kernel(nc, ctx, ins, out)
        load_constants(K)
        K.end_phase()
        sort_edges(K)
        K.end_phase()
        unpack_indices(K)
        K.end_phase()
        setup_nodes(K)
        K.end_phase()
        first_table(K)
        K.end_phase()
        edge_pass(K, "e0", DST, SRC, "product", [K.tab[0]], K.acc, K.src_count)
        K.end_phase()
        update_first(K)
        K.end_phase()
        edge_pass(K, "e1", SRC, DST, "copy", [K.tab[0]], K.acc, K.dst_count)
        K.end_phase()
        gin_first(K)
        K.end_phase()
        edge_pass(K, "e2", SRC, DST, "copy", [K.tab[0]], K.acc)
        K.end_phase()
        gin_second(K)
        K.end_phase()
        edge_pass(K, "e3", SRC, DST, "copy", [K.tab[0]], K.acc)
        K.end_phase()
        gcn(K)
        K.end_phase()
        edge_pass(K, "e4", DST, SRC, "scalar", [K.tab[0]], K.keep[:].rearrange("p b f -> p (b f)"))
        K.end_phase()
        edge_pass(K, "e5", DST, SRC, "vector", [K.tab[0]], K.acc)
        K.end_phase()
        norm_first(K)
        K.end_phase()
        edge_pass(K, "e6", DST, SRC, "both", K.tab, K.acc)
        K.end_phase()
        finish(K)
        K.end_phase()


_INS = ["x", "src", "dst", "edge_attr_3", "edge_attr_48", "edge_attr_8",
        "L0_gnn_W_msg_tp", "L0_gnn_W_msg_lin", "L0_gnn_W_upd_tp", "L0_gnn_W_upd_lin",
        "L1_gnn_eps1", "L1_gnn_w1a", "L1_gnn_b1a", "L1_gnn_w1b", "L1_gnn_b1b",
        "L1_gnn_eps2", "L1_gnn_w2a", "L1_gnn_b2a", "L1_gnn_w2b", "L1_gnn_b2b", "L2_gnn_W", "L2_gnn_b",
        "L3_gnn_fc0_w1", "L3_gnn_fc0_b1", "L3_gnn_fc0_w2", "L3_gnn_fc0_b2",
        "L3_gnn_fc1_w1", "L3_gnn_fc1_b1", "L3_gnn_fc1_w2", "L3_gnn_fc1_b2",
        "L3_gnn_bn0_gs", "L3_gnn_bn0_bs", "L3_gnn_bn0_gv", "L3_gnn_bn1_gs", "L3_gnn_bn1_bs"]


def kernel(**inputs):
    import concourse.bacc as bacc
    from concourse.bass_utils import run_bass_kernel_spmd

    nc = bacc.Bacc("TRN2", target_bir_lowering=False, num_devices=1)
    arrays = {"in_consts": build_constants()}
    for name in _INS:
        a = np.ascontiguousarray(inputs[name])
        arrays[f"in_{name}"] = a.reshape(1) if a.ndim == 0 else a
    ins = {n[3:]: nc.dram_tensor(n, a.shape, mybir.dt.from_np(a.dtype), kind="ExternalInput").ap()
           for n, a in arrays.items()}
    out = nc.dram_tensor("out", (N_NODES, F), F32, kind="ExternalOutput").ap()
    program(nc, ins, out)
    r = run_bass_kernel_spmd(nc, [arrays], core_ids=[0])
    return r.results[0]["out"]
```

```python
from contextlib import ExitStack

import concourse.bass as bass
import numpy as np
from concourse import mybir

ALU = mybir.AluOpType
ACT = mybir.ActivationFunctionType
AX = mybir.AxisListType
F32 = mybir.dt.float32
BF16 = mybir.dt.bfloat16
I32 = mybir.dt.int32

P = 128
N_NODES = 12500
N_EDGES = 400000
F = 16
DE = 8
DH = 48
NV = 4
HI = 8
GROUP = HI * P
NG = -(-N_NODES // GROUP)
NBLK = NG * HI
NW = NBLK * F
NBKT = NG * NG
OHW = 176
EPP = N_EDGES // P
SUB = 25
GRP = 5
SLOTS = 5
NSUB = EPP // SUB
PAIR = 2
NT_MIN = (N_EDGES + NBKT * (PAIR * P - 1)) // P
BT = 4
PADT = 4
SB = 8
NSL = 4
LOOP = NSL * SB
NT = -(-NT_MIN // LOOP) * LOOP
NTURN = NT // LOOP
NPAIR = NT // PAIR
NCHUNK = -(-NPAIR // P)
KB = LOOP // BT
KS = SB // BT
PADLO = 256.0

C_SLO, C_SHI, C_DLO, C_DHI, C_R, C_A8, C_HA = 0, 1, 2, 3, 4, 8, 16
HW = DH + 1
C_HB = C_HA + HW
ROW = C_HB + HW
OFFP = 32
NSB = NT // SB
SPAIR = SB // PAIR
SLAG = 2
SRC, DST = 0, 1
LEAD = 16

CONSTS = {}


def build_constants():
    p = np.arange(P)
    parts = {
        "ident": np.eye(P),
        "iota": np.tile(np.arange(P), (P, 1)),
        "bucket": np.tile(np.arange(OHW), (P, 1)),
        "before": (p[:, None] < p[None, :]),
        "notbefore": (p[:, None] >= p[None, :]),
        "fold": (p[:, None] % F == np.arange(F)[None, :]),
        "iota8": np.tile(np.arange(HI), (P, 1)),
        "lo": p[:, None],
        "one": np.ones((P, 1)),
        "blk": p[:, None] // F,
        "valid": (np.arange(NBLK)[None, :] * P + p[:, None] < N_NODES),
        "tau": PAIR * (np.arange(NCHUNK)[None, :] * P + p[:, None]),
    }
    at = 0
    for name, a in parts.items():
        CONSTS[name] = (at, a.shape[1])
        at += a.shape[1]
    return np.concatenate([np.asarray(a, np.float32) for a in parts.values()], axis=1)


class Chain:

    def __init__(self, eng, sem):
        self.eng, self.sem, self.n = eng, sem, 0

    def __call__(self, ins):
        self.n += 1
        ins.then_inc(self.sem, 1)
        self.eng.wait_ge(self.sem, self.n)


class Kernel:

    def __init__(self, nc, ctx, ins, out):
        self.nc, self.ins, self.out, self.ctx = nc, ins, out, ctx
        self.sems = []
        self.rows_d = nc.dram_tensor("edge_rows", (P * NT, ROW), F32, kind="Internal").ap()
        self.idxT_d = nc.dram_tensor("idx_rows", (NTURN, 4 * LOOP * P), BF16, kind="Internal").ap()
        self.nat_d = nc.dram_tensor("idx_nat", (P, NT * 4), F32, kind="Internal").ap()
        self.vec_d = nc.dram_tensor("vector_messages", (P, NT * 3 * NV), F32, kind="Internal").ap()
        self.offs_d = nc.dram_tensor("tile_offsets", (2, NCHUNK * P), I32, kind="Internal").ap()
        w = sum(n for _, n in CONSTS.values())
        self.consts = self.sb("consts", [P, w], F32)

    def c(self, name):
        at, n = CONSTS[name]
        return self.consts[:, at:at + n]

    def sb(self, name, shape, dt=F32, ctx=None):
        return (ctx or self.ctx).enter_context(self.nc.sbuf_tensor(name, shape, dt))

    def ps(self, ctx, name, shape, dt=F32):
        return ctx.enter_context(self.nc.psum_tensor(name, shape, dt))

    def sem(self, name):
        self.sems.append(self.nc.alloc_semaphore(name=name))
        return self.sems[-1]

    def end_phase(self):
        self.nc.all_engine_barrier()
        self.nc.clear_and_free_semaphores(self.sems)
        self.nc.all_engine_barrier()
        self.sems = []


def load_constants(K):
    nc = K.nc
    loaded = K.sem("consts_loaded")
    with nc.Block() as block:
        @block.sync
        def _(sp):
            sp.dma_start(K.consts[:], K.ins["consts"]).then_inc(loaded, 16)
            sp.wait_ge(loaded, 16)


def sort_edges(K):
    nc = K.nc
    with ExitStack() as ctx:
        def sb(name, shape, dt=F32):
            return K.sb(name, shape, dt, ctx)

        src_i = sb("src_i", [P, EPP], I32)
        dst_i = sb("dst_i", [P, EPP], I32)
        shi_i = sb("shi_i", [P, EPP], I32)
        dhi_i = sb("dhi_i", [P, EPP], I32)
        key = sb("key", [P, EPP], BF16)
        vec = sb("vec", [P, EPP, 3])
        buckets = sb("buckets", [P, OHW], BF16)
        before = sb("before", [P, P], BF16)
        notbefore = sb("notbefore", [P, P], BF16)
        ones = sb("ones", [P, P], BF16)
        onesrow = sb("onesrow", [NG, P])
        zeros = sb("zeros", [P, 512], BF16)
        zerof = sb("zerof", [P, NBKT])
        oh = sb("oh", [P, SUB, OHW], BF16)
        w1 = sb("w1", [HW, 2 * DH])
        cnt_i = sb("cnt_i", [P, NBKT], I32)
        tiles = sb("tiles", [P, NBKT])
        end = sb("end", [P, NBKT])
        start = sb("start", [P, GRP, NBKT])
        junk = sb("junk", [P, GRP, NBKT])
        counts = junk[0:NG]
        tb = sb("tb", [P, 2, NCHUNK])
        offs = sb("offs", [P, P], I32)
        pad = sb("pad", [P, PADT, ROW])
        rows = sb("rows", [P, SLOTS, SUB, ROW])
        attr = sb("attr", [P, SLOTS, SUB * DH])
        norm = attr[:].rearrange("p s c -> p (s c)")[:, 0:EPP]
        a8 = sb("a8", [P, SLOTS, SUB * DE])
        aT = sb("aT", [HW, GRP * P])
        both = oh[:].rearrange("p t b -> p (t b)")[:, 0:2 * SLOTS * SUB * NG].rearrange(
            "p (n s t g) -> p n s t g", n=2, s=SLOTS, t=SUB)
        ohs, ohd = both[:, 0], both[:, 1]
        pos = sb("pos", [P, SUB])
        pos_i = sb("pos_i", [P, SUB], I32)
        part_i = sb("part_i", [P, SUB], I32)
        tile_i = sb("tile_i", [P, SUB], I32)
        place = sb("place", [P, SLOTS, SUB], I32)
        count_ps = K.ps(ctx, "count_ps", [P, GRP, 512])
        counter = [count_ps[:, c, 0:NBKT] for c in range(GRP)]
        tp_ps = K.ps(ctx, "tp_ps", [P, 1024])
        h_ps = K.ps(ctx, "h_ps", [P, 512])
        hist_ps, off_ps = h_ps, tp_ps

        idx_loaded, vec_loaded, w_loaded = K.sem("s_idx_loaded"), K.sem("s_vec_loaded"), K.sem("s_w_loaded")
        pad_ready, es_filled = K.sem("s_pad_ready"), K.sem("s_es_filled")
        dve_chain, act_norm, norm2_ready = K.sem("s_dve_chain"), K.sem("s_act_norm"), K.sem("s_norm2_ready")
        hist_ready, hist_used, zero_done = K.sem("s_hist_ready"), K.sem("s_hist_used"), K.sem("s_zero_done")
        start_ready, offs_ready, offs_stored = K.sem("s_start_ready"), K.sem("s_offs_ready"), K.sem("s_offs_stored")
        oh_ready, p_ready, sel_done, rank_used = (K.sem("s_oh_ready"), K.sem("s_p_ready"), K.sem("s_sel_done"),
                                                  K.sem("s_rank_used"))
        attr_loaded, a8_used = K.sem("s_attr_loaded"), K.sem("s_a8_used")
        sp_go, pe_go, counts_ready, spread_ready = (K.sem("s_sp_go"), K.sem("s_pe_go"), K.sem("s_counts_ready"),
                                                    K.sem("s_spread_ready"))
        tp_ready, aT_ready, h_ready, h_used = (K.sem("s_tp_ready"), K.sem("s_aT_ready"), K.sem("s_h_ready"),
                                               K.sem("s_h_used"))
        place_ready, row_ready, pool_go = K.sem("s_place_ready"), K.sem("s_row_ready"), K.sem("s_pool_go")
        rowconst_ready, place_step, slot_free = K.sem("s_rowconst_ready"), K.sem("s_place_step"), K.sem("s_slot_free")
        groups_ready, offs_turned = K.sem("s_groups_ready"), K.sem("s_offs_turned")
        scattered = [K.sem(f"s_scattered{s}") for s in range(SLOTS)]
        NGRP = SUB // GRP
        LAG = 3

        def turns(eng, body):
            for s in range(SLOTS):
                body(s, s, True)
            with eng.Fori(1, NSUB // SLOTS) as turn:
                for s in range(SLOTS):
                    body(turn * SLOTS + s, s, False)

        block = ctx.enter_context(nc.Block())

        @block.sync
        def _(sp):
            sp.dma_start(src_i[:], K.ins["src"].rearrange("(p t) -> p t", p=P)).then_inc(idx_loaded, 16)
            sp.dma_start(dst_i[:], K.ins["dst"].rearrange("(p t) -> p t", p=P)).then_inc(idx_loaded, 16)
            sp.dma_start(vec[:].rearrange("p t c -> p (t c)"),
                         K.ins["edge_attr_3"].rearrange("(p t) c -> p (t c)", p=P)).then_inc(vec_loaded, 16)
            for n, fc in enumerate(("fc0", "fc1")):
                sp.dma_start(w1[0:DH, n * DH:(n + 1) * DH], K.ins[f"L3_gnn_{fc}_w1"]).then_inc(w_loaded, 16)
                sp.dma_start(w1[DH:HW, n * DH:(n + 1) * DH],
                             K.ins[f"L3_gnn_{fc}_b1"].rearrange("(a d) -> a d", a=1)).then_inc(w_loaded, 16)
            sp.wait_ge(pad_ready, 1)
            rows_v = K.rows_d.rearrange("(p t) c -> p (t c)", p=P)
            with sp.Fori(0, NT // PADT) as r:
                sp.dma_start(rows_v[:, bass.ds(r * (PADT * ROW), PADT * ROW)],
                             pad[:].rearrange("p t c -> p (t c)")).then_inc(es_filled, 16)
            sp.wait_ge(offs_ready, 1)
            sp.dma_start(K.offs_d.rearrange("k (c p) -> (k c) p", p=P), offs[0:2 * NCHUNK, :]).then_inc(offs_stored, 16)

            sp.wait_ge(rowconst_ready, 1)

            def load(q, s, first):
                if not first:
                    sp.wait_ge(tp_ready, (q - SLOTS + 1) * NGRP)
                    sp.wait_ge(a8_used, q - SLOTS + 1)
                    sp.sem_inc(sp_go, 1)
                sp.dma_start(attr[:, s, :], K.ins["edge_attr_48"].rearrange("(p t) c -> p (t c)", p=P)[
                    :, bass.ds(q * (SUB * DH), SUB * DH)]).then_inc(attr_loaded, 16)
                sp.dma_start(a8[:, s, :], K.ins["edge_attr_8"].rearrange("(p t) c -> p (t c)", p=P)[
                    :, bass.ds(q * (SUB * DE), SUB * DE)]).then_inc(attr_loaded, 16)
                sp.wait_ge(attr_loaded, q * 32 + 32)
                sp.sem_inc(sp_go, 1)
            turns(sp, load)
            sp.wait_ge(offs_stored, 16)

        @block.vector
        def _(v):
            step = Chain(v, dve_chain)
            step(v.memset(pad[:], 0.0))
            v.memset(pad[:, :, C_SLO:C_DLO + 1:2], PADLO).then_inc(pad_ready, 1)
            v.memset(ones[:], 1.0)
            v.memset(zeros[:], 0.0)
            v.memset(zerof[:], 0.0)
            v.memset(onesrow[:], 1.0)
            v.memset(aT[:], 1.0)
            v.tensor_copy(buckets[:], K.c("bucket"))
            v.tensor_copy(before[:], K.c("before"))
            step(v.tensor_copy(notbefore[:], K.c("notbefore")))
            v.sem_inc(zero_done, 1)
            v.wait_ge(idx_loaded, 32)
            v.tensor_scalar(shi_i[:], src_i[:], 10, None, ALU.logical_shift_right)
            step(v.tensor_scalar(dhi_i[:], dst_i[:], 10, None, ALU.logical_shift_right))
            step(v.scalar_tensor_tensor(key[:], shi_i[:], float(NG), dhi_i[:], ALU.mult, ALU.add))

            def hist(q, s, first):
                if not first:
                    v.wait_ge(hist_used, q - SLOTS + 1)
                iota = K.c("iota")[:, 0:NG].unsqueeze(1).to_broadcast([P, SUB, NG])
                for one, group in ((ohs, shi_i), (ohd, dhi_i)):
                    ins = v.tensor_tensor(one[:, s, :, :], group[:, bass.ds(q * SUB, SUB)].unsqueeze(2).to_broadcast(
                        [P, SUB, NG]), iota, ALU.is_equal)
                ins.then_inc(hist_ready, 1)
            turns(v, hist)
            v.wait_ge(hist_used, NSUB)

            v.tensor_scalar(shi_i[:], src_i[:], 7, HI - 1, ALU.logical_shift_right, ALU.bitwise_and)
            step(v.tensor_scalar(dhi_i[:], dst_i[:], 7, HI - 1, ALU.logical_shift_right, ALU.bitwise_and))
            v.tensor_scalar(src_i[:], src_i[:], P - 1, None, ALU.bitwise_and)
            step(v.tensor_scalar(dst_i[:], dst_i[:], P - 1, None, ALU.bitwise_and))
            v.wait_ge(vec_loaded, 16)
            square = rows[:].rearrange("p s t c -> p (s t c)")[:, 0:EPP]
            step(v.tensor_tensor(norm, vec[:, :, 0], vec[:, :, 0], ALU.mult))
            for c in (1, 2):
                step(v.tensor_tensor(square, vec[:, :, c], vec[:, :, c], ALU.mult))
                ins = v.tensor_tensor(norm, norm, square, ALU.add)
                step(ins)
            v.sem_inc(norm2_ready, 1)
            v.wait_ge(act_norm, 1)
            step(v.tensor_scalar(norm, norm, 1e-12, None, ALU.add))
            step(v.reciprocal(norm, norm))
            step(v.tensor_tensor(vec[:], vec[:], norm.unsqueeze(2).to_broadcast([P, EPP, 3]), ALU.mult))
            step(v.memset(rows[:], 0.0))
            step(v.memset(rows[:].rearrange("p s t c -> p (s t) c")[:, :, C_HA + DH:ROW:HW], 1.0))
            v.sem_inc(rowconst_ready, 1)

            for c in range(GRP):
                ins = v.tensor_tensor(counts[:, c, :].rearrange("p (s d) -> p s d", d=NG),
                                      hist_ps[0:NG, c * NG:(c + 1) * NG].unsqueeze(1).to_broadcast([NG, NG, NG]),
                                      K.c("ident")[0:NG, 0:NG].unsqueeze(2).to_broadcast([NG, NG, NG]), ALU.mult)
            step(ins)
            v.sem_inc(counts_ready, 1)
            v.wait_ge(spread_ready, 1)
            step(v.tensor_copy(start[:, 0, :], counter[0]))
            for c in range(1, GRP):
                step(v.tensor_tensor(start[:, 0, :], start[:, 0, :], counter[c], ALU.add))
            step(v.tensor_scalar(cnt_i[:], start[:, 0, :], float(PAIR * P - 1), None, ALU.add))
            step(v.tensor_scalar(cnt_i[:], cnt_i[:], 8, None, ALU.logical_shift_right))
            step(v.tensor_scalar(tiles[:], cnt_i[:], float(PAIR), None, ALU.mult))
            step(v.tensor_tensor_scan(end[:], tiles[:], zerof[:], 0.0, ALU.add, ALU.add))
            step(v.tensor_tensor(start[:, 0, :], end[:], tiles[:], ALU.subtract))
            step(v.tensor_scalar(start[:, 0, :], start[:, 0, :], float(P), None, ALU.mult))
            for c in range(1, GRP):
                step(v.tensor_tensor(start[:, c, :], start[:, c - 1, :], counter[c - 1], ALU.add))
            v.sem_inc(start_ready, 1)

            def rank(q, s, first):
                for k in range(SUB):
                    if k % GRP == 0 and not first:
                        v.wait_ge(rank_used, q * SUB + (k + GRP - SUB))
                    if k % GRP == 0 and first and s > 0:
                        v.wait_ge(rank_used, q * SUB + k + GRP - SUB)
                    ins = v.tensor_scalar(oh[:, k, :], buckets[:], key[:, bass.ds(q * SUB + k, 1)], None, ALU.is_equal)
                    ins.then_inc(oh_ready, 1)
                for k in range(SUB):
                    v.wait_ge(p_ready, q * SUB + k + 1)
                    v.scalar_tensor_tensor(junk[:, k % GRP, :], counter[k % GRP], 1.0, oh[:, k, 0:NBKT], ALU.mult, ALU.mult,
                                           accum_out=pos[:, k:k + 1]).then_inc(sel_done, 1)
                v.wait_ge(sel_done, q * SUB + SUB)
                v.tensor_copy(pos_i[:], pos[:]).then_inc(place_step, 1)
                v.wait_ge(place_step, q * 3 + 1)
                v.tensor_scalar(part_i[:], pos_i[:], P - 1, None, ALU.bitwise_and)
                v.tensor_scalar(tile_i[:], pos_i[:], 7, None, ALU.logical_shift_right).then_inc(place_step, 1)
                v.wait_ge(place_step, q * 3 + 2)
                if not first:
                    v.wait_ge(slot_free, q - SLOTS + 1)
                v.scalar_tensor_tensor(place[:, s, :], part_i[:], float(NT), tile_i[:], ALU.mult,
                                       ALU.add).then_inc(place_step, 1)
                v.wait_ge(place_step, q * 3 + 3)
                v.sem_inc(place_ready, 1)

            def tile_groups():
                for c in range(NCHUNK):
                    step(v.tensor_scalar(junk[:, 0, :], end[:], K.c("tau")[:, c:c + 1], None, ALU.is_le, ALU.add,
                                         accum_out=tb[:, 1, c:c + 1]))
                    ins = v.tensor_scalar(junk[:, 0, 0:NG], end[:, NG - 1:NBKT:NG], K.c("tau")[:, c:c + 1], None, ALU.is_le,
                                          ALU.add, accum_out=tb[:, 0, c:c + 1])
                    step(ins)
                step(v.tensor_scalar(tb[:, 1, :], tb[:, 1, :], float(NBKT - 1), None, ALU.min))
                step(v.tensor_scalar(tb[:, 0, :], tb[:, 0, :], float(NG - 1), None, ALU.min))
                step(v.scalar_tensor_tensor(tb[:, 1, :], tb[:, 0, :], -float(NG), tb[:, 1, :], ALU.mult, ALU.add))
                step(v.tensor_scalar(tb[:], tb[:], float(HI), None, ALU.mult))
                v.sem_inc(groups_ready, 1)
                v.wait_ge(offs_turned, 1)
                step(v.tensor_copy(offs[0:2 * NCHUNK, :], off_ps[0:2 * NCHUNK, 0:P]))
                v.sem_inc(offs_ready, 1)
            tile_groups()
            turns(v, rank)

        @block.scalar
        def _(act):
            act.wait_ge(norm2_ready, 1)
            nc.scalar.activation(norm, norm, ACT.Sqrt).then_inc(act_norm, 1)
            act.wait_ge(rowconst_ready, 1)

            def fill(q, s, first):
                if not first:
                    act.wait_ge(slot_free, q - SLOTS + 1)
                cols = bass.ds(q * SUB, SUB)
                for c, a in ((C_SLO, src_i), (C_SHI, shi_i), (C_DLO, dst_i), (C_DHI, dhi_i)):
                    nc.scalar.copy(rows[:, s, :, c], a[:, cols])
                nc.scalar.copy(rows[:, s, :, C_R:C_R + 3], vec[:, cols, :])
                act.wait_ge(attr_loaded, q * 32 + 32)
                nc.scalar.copy(rows[:, s, :, C_A8:C_A8 + DE],
                               a8[:, s, :].rearrange("p (t c) -> p t c", c=DE)).then_inc(a8_used, 1)
                for g in range(NGRP):
                    act.wait_ge(tp_ready, q * NGRP + g + 1)
                    nc.scalar.copy(aT[0:DH, :], tp_ps[0:DH, 0:GRP * P]).then_inc(aT_ready, 1)
                    act.wait_ge(h_ready, q * NGRP + g + 1)
                    nc.scalar.activation(
                        rows[:, s, g * GRP:(g + 1) * GRP, C_HA:ROW].rearrange("p t (n c) -> p t n c", n=2)[:, :, :, 0:DH],
                        h_ps[:, 0:GRP * 2 * DH].rearrange("p (t n c) -> p t n c", n=2, c=DH), ACT.Relu).then_inc(row_ready, 1)
            turns(act, fill)

        @block.tensor
        def _(pe):
            pe.wait_ge(zero_done, 1)
            pe.matmul(hist_ps[0:NG, :], zeros[:, 0:NG], zeros[:], start=True, stop=False, skip_group_check=True)

            def hist(q, s, first):
                pe.wait_ge(hist_ready, q + 1)
                for k in range(SUB):
                    c = k % GRP
                    ins = pe.matmul(hist_ps[0:NG, c * NG:(c + 1) * NG], ohs[:, s, k, :], ohd[:, s, k, :],
                                    start=False, stop=False, skip_group_check=True)
                ins.then_inc(hist_used, 1)
            turns(pe, hist)

            def clear_counters():
                for bank in range(GRP):
                    pe.matmul(count_ps[:, bank, :], ones[:], zeros[:], start=True, stop=False, skip_group_check=True)
            pe.wait_ge(counts_ready, 1)
            clear_counters()
            for c in range(GRP):
                ins = pe.matmul(counter[c], onesrow[:], counts[:, c, :], start=False, stop=False, skip_group_check=True)
            ins.then_inc(spread_ready, 1)
            pe.wait_ge(start_ready, 1)
            clear_counters()
            for c in range(GRP):
                pe.matmul(counter[c], onesrow[0:1, :], start[0:1, c, :], start=False, stop=False, skip_group_check=True)
            pe.wait_ge(groups_ready, 1)
            pe.transpose(off_ps[0:2 * NCHUNK, 0:P], tb[:].rearrange("p k c -> p (k c)"), K.c("ident")).then_inc(offs_turned, 1)
            pe.wait_ge(offs_ready, 1)
            pe.wait_ge(w_loaded, 64)

            def rank(q, s, first):
                for k in range(SUB + LAG):
                    if k < SUB:
                        if k % GRP == 0:
                            turn_attributes(q, s, k // GRP, first)
                        pe.wait_ge(oh_ready, q * SUB + k + 1)
                        pe.matmul(counter[k % GRP], before[:], oh[:, k, 0:NBKT], start=False, stop=False,
                                  skip_group_check=True).then_inc(p_ready, 1)
                        if k % GRP == 2:
                            hidden(q, s, k // GRP, first)
                    if k >= LAG:
                        pe.wait_ge(sel_done, q * SUB + k - LAG + 1)
                        pe.matmul(counter[(k - LAG) % GRP], notbefore[:], oh[:, k - LAG, 0:NBKT], start=False, stop=False,
                                  skip_group_check=True).then_inc(rank_used, 1)

            def turn_attributes(q, s, g, first):
                if g == 0:
                    pe.wait_ge(attr_loaded, q * 32 + 32)
                    pe.sem_inc(pe_go, 1)
                if not (first and s == 0 and g == 0):
                    pe.wait_ge(aT_ready, q * NGRP + g)
                    pe.sem_inc(pe_go, 1)
                for i in range(GRP):
                    k = g * GRP + i
                    ins = pe.transpose(tp_ps[0:DH, i * P:(i + 1) * P], attr[:, s, k * DH:(k + 1) * DH], K.c("ident"))
                ins.then_inc(tp_ready, 1)

            def hidden(q, s, g, first):
                pe.wait_ge(aT_ready, q * NGRP + g + 1)
                if not (first and s == 0 and g == 0):
                    pe.wait_ge(row_ready, q * NGRP + g)
                for i in range(GRP):
                    ins = pe.matmul(h_ps[:, i * 2 * DH:(i + 1) * 2 * DH], aT[:, i * P:(i + 1) * P], w1[:],
                                    start=True, stop=True)
                ins.then_inc(h_ready, 1)
            turns(pe, rank)

        @block.gpsimd
        def _(pool):
            pool.wait_ge(es_filled, NT // PADT * 16)

            def scatter(q, s, first):
                pool.wait_ge(row_ready, q * NGRP + NGRP)
                pool.sem_inc(pool_go, 1)
                pool.wait_ge(place_ready, q + 1)
                pool.sem_inc(pool_go, 1)
                for k in range(SUB):
                    pool.indirect_dma_start(K.rows_d, bass.IndirectOffsetOnAxis(place[:, s, k:k + 1], axis=0),
                                            rows[:, s, k, :], None).then_inc(scattered[s], 16)
                    if k == 5 and not (first and s < 1):
                        b = (s - 1) % SLOTS
                        turn = q if first else None
                        landed(q, b)
                        pool.sem_inc(slot_free, 1)

            def landed(q, b):
                if isinstance(q, int):
                    pool.wait_ge(scattered[b], 16 * SUB * ((q - 1) // SLOTS + 1))
                else:
                    pool.wait_ge(scattered[b], count[b])

            for s in range(SLOTS):
                scatter(s, s, True)
            with pool.Fori(1, NSUB // SLOTS) as turn:
                count = [(turn + 1) * (16 * SUB)] * (SLOTS - 1) + [turn * (16 * SUB)]
                for s in range(SLOTS):
                    scatter(turn * SLOTS + s, s, False)
            for s in range(SLOTS):
                pool.wait_ge(scattered[s], NSUB // SLOTS * 16 * SUB)


def unpack_indices(K):
    nc = K.nc
    R = 4
    with ExitStack() as ctx:
        nat = K.sb("nat", [P, NT, 4], F32, ctx)
        turned = K.sb("turned", [P, R, P], BF16, ctx)
        stage = K.sb("stage", [P, R, 4, LOOP], BF16, ctx)
        ident = K.sb("ident", [P, P], BF16, ctx)
        turn_ps = K.ps(ctx, "turn_ps", [P, R, 1024], BF16)
        staged, ident_ready = K.sem("u_staged"), K.sem("u_ident_ready")
        nat_loaded = [K.sem(f"u_nat_loaded{c}") for c in range(4)]
        nat_stored, rows_stored = K.sem("u_nat_stored"), [K.sem(f"u_rows_stored{r}") for r in range(R)]
        turn_ready, copied, row_free, act_go, pe_go, sp_go = (K.sem("u_turn_ready"), K.sem("u_copied"), K.sem("u_row_free"),
                                                       K.sem("u_act_go"), K.sem("u_pe_go"), K.sem("u_sp_go"))
        cut = [0, 3 * LOOP, 28 * LOOP, 60 * LOOP, NT]
        rows_v = K.rows_d.rearrange("(p t) c -> p t c", p=P)

        def turns(eng, body):
            whole = NTURN // R
            for r in range(R):
                body(r, r, True)
            with eng.Fori(1, whole) as n:
                for r in range(R):
                    body(n * R + r, r, False)
            for r in range(NTURN - whole * R):
                body(whole * R + r, r, False)

        block = ctx.enter_context(nc.Block())

        @block.sync
        def _(sp):
            for c in range(4):
                sp.dma_start(nat[:, cut[c]:cut[c + 1], :], rows_v[:, cut[c]:cut[c + 1], 0:4]).then_inc(nat_loaded[c], 16)
            for c in range(4):
                sp.wait_ge(nat_loaded[c], 16)
            sp.dma_start(K.nat_d, nat[:].rearrange("p t c -> p (t c)")).then_inc(nat_stored, 16)

            def store(q, r, first):
                sp.wait_ge(copied, q + 1)
                sp.dma_start(K.idxT_d[bass.ds(q, 1)].rearrange("o (k e) -> (o k) e", e=P), turned[:, r, :]).then_inc(rows_stored[r], 16)
            turns(sp, store)
            sp.wait_ge(nat_stored, 16)
            for r in range(R):
                sp.wait_ge(rows_stored[r], 16 * len(range(r, NTURN, R)))

        @block.tensor
        def _(pe):
            pe.wait_ge(ident_ready, 1)

            def turn(q, r, first):
                pe.wait_ge(staged, q + 1)
                if not first:
                    pe.wait_ge(copied, q - R + 1)
                    pe.sem_inc(pe_go, 1)
                pe.transpose(turn_ps[:, r, 0:P], stage[:, r, :, :].rearrange("p c t -> p (c t)"),
                             ident[:]).then_inc(turn_ready, 1)
            turns(pe, turn)

        @block.vector
        def _(v):
            v.tensor_copy(ident[:], K.c("ident")).then_inc(ident_ready, 1)
            for c in range(4):
                v.wait_ge(nat_loaded[c], 16)

            def put(q, r, first):
                if not first:
                    v.wait_ge(turn_ready, q - R + 1)
                v.tensor_copy(stage[:, r, :, :], nat[:, bass.ds(q * LOOP, LOOP), :].rearrange(
                    "p t c -> p c t")).then_inc(staged, 1)
            turns(v, put)

        @block.scalar
        def _(act):
            def copy(q, r, first):
                act.wait_ge(turn_ready, q + 1)
                if not first:
                    use = q - r if isinstance(q, int) else None
                    act.wait_ge(rows_stored[r], stored(q, r))
                nc.scalar.copy(turned[:, r, :], turn_ps[:, r, 0:P]).then_inc(copied, 1)

            def stored(q, r):
                return q // R * 16 if isinstance(q, int) else uses[0] * 16
            uses = [None]
            whole = NTURN // R
            for r in range(R):
                copy(r, r, True)
            with act.Fori(1, whole) as n:
                uses[0] = n
                for r in range(R):
                    copy(n * R + r, r, False)
            for r in range(NTURN - whole * R):
                copy(whole * R + r, r, False)


class Batch:

    def __init__(self, turn, k):
        at = 0 if turn is None else turn
        self.n, self.i, self.use = at * KB + k, at * NSL + k // KS, at + k // KB
        self.k = k % KB
        self.h, self.b = self.k // KS, self.k % KS
        self.first = turn is None and k < KB


def run_batches(eng, stages):
    n_batches = NTURN * KB

    def at(turn, m):
        for lag, stage in stages:
            if turn is not None or 0 <= m - lag < n_batches:
                stage(Batch(turn, m - lag))
    for m in range(KB):
        at(None, m)
    with eng.Fori(1, NTURN) as turn:
        for m in range(KB):
            at(turn, m)
    for m in range(n_batches, n_batches + max(lag for lag, _ in stages)):
        at(None, m)


def edge_pass(K, name, gather, scatter, kind, tables, acc_out, cnt_out=None):
    nc = K.nc
    last, gathers = kind in ("first", "second"), kind != "stored"
    turned_rows = kind == "product"
    G = 1 if last else 2
    RM, RO, RZ = 4, 4, 4
    NTAB = len(tables)
    WN = (F + NV) * F
    NQ = F if kind == "first" else F + NV
    NJ = WN // NQ
    HB = KB // 2
    SHORT = 3 * NV if kind == "stored" else F
    has_rows = kind in ("product", "first", "second")
    NLOAD = {"copy": 2, "stored": 2}.get(kind, 3)
    with ExitStack() as ctx:
        def sb(n, shape, dt=F32):
            return K.sb(f"{name}_{n}", shape, dt, ctx)

        def sem(n):
            return K.sem(f"{name}_{n}")

        natb = sb("natb", [P, NSL, SB, 4])
        ohlo = sb("ohlo", [P, KB, BT, P])
        ohhi = sb("ohhi", [P, KB, BT, HI])
        outer = sb("outer", [P, RO, BT, HI, F])
        zero = sb("zero", [P, 512], BF16)
        if gathers:
            NIDX = 2 if turned_rows else 1
            idxb = sb("idxb", [P, NSL, NIDX, SB * P], BF16)
            ohg = sb("ohg", [P, KB, BT, HI])
            far = sb("far", [P, 2, BT, P])
            ohT = sb("ohT", [P, KB, BT * P], BF16)
            masked = sb("masked", [P, RM, NTAB, BT * P])
            msg = sb("msg", [P, RO, BT, NJ if last else F])
        else:
            msg = sb("msg", [P, NSL * KS, BT, 3 * NV])
        if has_rows:
            rows = sb("rows", [P, NSL, SB, ROW])
        if kind == "product":
            prod = sb("prod", [P, 2, BT, DE * F])
            tsum = sb("tsum", [P, RO, BT, F])
        if last:
            hT = sb("hT", [HW, RZ, BT * P])
            z = sb("z", [P, RZ, BT, NQ])
            zv = sb("zv", [P, BT, F])
            prod = sb("prod", [P, 2, BT, WN])
            dot = sb("dot", [P, BT, NV, 3])
            vecs = sb("vecs", [P, 2, HB * BT, 3 * NV])
        acc = K.ps(ctx, f"{name}_acc", [P, 4 * 512])
        if gathers:
            gps = K.ps(ctx, f"{name}_gps", [P, G, 512])
        if last:
            turn_ps = K.ps(ctx, f"{name}_turn", [P, 512])
            w_ps = K.ps(ctx, f"{name}_w", [P, 2, 512])
        elif turned_rows:
            fold_ps = K.ps(ctx, f"{name}_fold", [P, 512])
        if cnt_out is not None:
            cnt_ps = K.ps(ctx, f"{name}_cnt", [P, 512])

        loaded = [sem(f"loaded{h}") for h in range(NSL)]
        zero_ready, sp_go, pe_go, flushed = sem("zero_ready"), sem("sp_go"), sem("pe_go"), sem("flushed")
        oh_ready, outers, scattered = sem("oh_ready"), sem("outers"), sem("scattered")
        places = sem("places") if gathers else oh_ready
        if gathers:
            place_step = sem("place_step")
            gathered, masks, folded, messages = sem("gathered"), sem("masks"), sem("folded"), sem("messages")
        if has_rows:
            dve_step, pool_go = sem("dve_step"), sem("pool_go")
        if gathers:
            pool_step, fold_step, halved = sem("pool_step"), sem("fold_step"), sem("halved")
        if kind == "product":
            sums = sem("sums")
        if last:
            turned, hT_ready, weights, contracted = sem("turned"), sem("hT_ready"), sem("weights"), sem("contracted")
        if kind == "first":
            vec_stored, vec_ready = [sem(f"vec_stored{u}") for u in range(2)], sem("vec_ready")
        used = {"copy": masks, "product": dve_step if has_rows else None}.get(kind, outers) if gathers else outers

        def done(eng, s, n):
            eng.wait_ge(s, n + LEAD)

        block = ctx.enter_context(nc.Block())

        @block.sync
        def _(sp):
            def load(i, h, turn, first):
                if not first:
                    done(sp, used, (i - NSL + 1) * KS)
                    done(sp, places, (i - NSL + 1) * KS)
                    sp.sem_inc(sp_go, 1)
                sp.dma_start(natb[:, h, :, :].rearrange("p t c -> p (t c)"),
                             K.nat_d[:, bass.ds(i * (SB * 4), SB * 4)]).then_inc(loaded[h], 16)
                if gathers:
                    sp.dma_start(idxb[:, h, :, :], K.idxT_d[bass.ds(turn, 1), :].rearrange(
                        "o (k e) -> (o k) e", k=4)[2 * gather:2 * gather + NIDX, h * SB * P:(h + 1) * SB * P
                                                   ].partition_broadcast(P)).then_inc(loaded[h], 16)
                else:
                    sp.dma_start(msg[:, h * KS:(h + 1) * KS, :, :].rearrange("p b t c -> p (b t c)"),
                                 K.vec_d[:, bass.ds(i * (SB * 3 * NV), SB * 3 * NV)]).then_inc(loaded[h], 16)
                if has_rows:
                    sp.dma_start(rows[:, h, :, :].rearrange("p t c -> p (t c)"),
                                 K.rows_d.rearrange("(p t) c -> p (t c)", p=P)[:, bass.ds(i * (SB * ROW), SB * ROW)]
                                 ).then_inc(loaded[h], 16)

            def store(turn, u):
                sp.wait_ge(vec_ready, turn * 2 + u + 1)
                sp.dma_start(K.vec_d[:, bass.ds(turn * LOOP * 3 * NV + u * (HB * BT * 3 * NV), HB * BT * 3 * NV)],
                             vecs[:, u, :, :].rearrange("p t c -> p (t c)")).then_inc(vec_stored[u], 16)
            for h in range(NSL):
                load(h, h, 0, True)
            with sp.Fori(1, NTURN) as turn:
                for h in range(NSL):
                    load(turn * NSL + h, h, turn, False)
                    if kind == "first" and h % 2 == 1:
                        store(turn - 1, h // 2)
            if kind == "first":
                for u in range(2):
                    store(NTURN - 1, u)
                for u in range(2):
                    sp.wait_ge(vec_stored[u], 16 * NTURN)

        @block.tensor
        def _(pe):
            for s in (scattered,) + ((gathered,) if gathers else ()) + ((folded,) if turned_rows else ()) + ((turned, weights) if last else ()):
                pe.sem_inc(s, LEAD)
            pe.wait_ge(zero_ready, 1 if gathers else 2)
            for bank in range(4):
                pe.matmul(acc[:, bank * 512:(bank + 1) * 512], zero[:, 0:P], zero[:], start=True, stop=False,
                          skip_group_check=True)
            if cnt_out is not None:
                pe.matmul(cnt_ps[:], zero[:, 0:P], zero[:], start=True, stop=False, skip_group_check=True)
            regs = {}
            base = (gather if gathers else 1 - scatter) * OFFP

            def offsets(entry, sides):
                vals = nc.values_load_multi_w_load_instructions(
                    K.offs[base:base + 1, bass.ds(entry, 1), sides, :].rearrange("o i s k -> o (i s k)"),
                    engines=(mybir.EngineType.PE,), min_val=0, max_val=NBLK - HI,
                    skip_runtime_bounds_check_because="made on the chip, clamped")[1]
                regs["gather"], regs["scatter"] = vals[:SPAIR], vals[-SPAIR:]

            def load_offsets(B):
                if B.b == 0:
                    early = isinstance(B.i, int) and B.i < SLAG
                    offsets(B.i, slice(0, 1 if early else 2))

            def pair(B, side):
                n = BT // PAIR
                return regs[side][B.b * n:(B.b + 1) * n]

            def gather_blocks(B, tab):
                if tab == 0:
                    load_offsets(B)
                    done(pe, oh_ready, B.n + 1)
                done(pe, masks, B.n * NTAB + tab + 1 - G)
                pe.sem_inc(pe_go, 1)
                offs = pair(B, "gather")
                for t in range(0, BT, PAIR if turned_rows else 1):
                    cols = slice(t * P, (t + (PAIR if turned_rows else 1)) * P)
                    for part in range(3):
                        one_hot = ohT[:, B.k, cols]
                        blocks = tables[tab][:, part, bass.ds(offs[t // PAIR] * F, P)]
                        if turned_rows:
                            ins = pe.matmul(gps[:, B.k % G, cols], blocks, one_hot, start=(part == 0), stop=(part == 2))
                        else:
                            ins = pe.matmul(gps[:, B.k % G, cols], one_hot, blocks, start=(part == 0), stop=(part == 2))
                ins.then_inc(gathered, 1)

            def turn_hidden(B):
                at = C_HA if kind == "first" else C_HB
                done(pe, hT_ready, B.n)
                pe.sem_inc(pe_go, 1)
                for t in range(BT):
                    ins = pe.transpose(turn_ps[0:HW, t * P:(t + 1) * P], rows[:, B.h, B.b * BT + t, at:at + HW],
                                       K.c("ident"))
                ins.then_inc(turned, 1)

            def fold(B):
                done(pe, masks, B.n + 1)
                done(pe, dve_step, B.n)
                for t in range(BT):
                    ins = pe.matmul(fold_ps[:, t * P:(t + 1) * P], masked[:, B.k % RM, 0, t * P:(t + 1) * P], K.w_msg[:],
                                    start=True, stop=True)
                ins.then_inc(folded, 1)

            def edge_weights(B, tiles):
                if 0 in tiles:
                    done(pe, hT_ready, B.n + 1)
                for t in tiles:
                    done(pe, contracted, B.n * BT + t - 1)
                    pe.matmul(w_ps[:, t % 2, 0:WN], hT[:, B.k % RZ, t * P:(t + 1) * P],
                              K.w2[0 if kind == "first" else 1][:], start=True, stop=True).then_inc(weights, 1)

            def scatter_sums(B):
                late = isinstance(B.n, int) and B.n + SLAG * KS >= NTURN * KB
                if B.b == 0 and (late or not gathers):
                    offsets(B.i + SLAG, slice(1, 2))
                done(pe, places, B.n + 1)
                done(pe, outers, B.n + 1)
                pe.sem_inc(pe_go, 1)
                offs = pair(B, "scatter")
                for t in range(BT):
                    ins = pe.matmul(acc[:, bass.ds(offs[t // PAIR] * F, P)], ohlo[:, B.k, t, :],
                                    outer[:, B.k % RO, t, :, :].rearrange("p a f -> p (a f)"),
                                    start=False, stop=False, skip_group_check=True)
                if cnt_out is not None:
                    for t in range(BT):
                        ins = pe.matmul(cnt_ps[:, bass.ds(offs[t // PAIR], HI)], ohlo[:, B.k, t, :],
                                        ohhi[:, B.k, t, :], start=False, stop=False, skip_group_check=True)
                ins.then_inc(scattered, 1)

            if not gathers:
                stages = [(0, scatter_sums)]
            else:
                stages = [(0, lambda B: gather_blocks(B, 0))]
                if last:
                    stages.append((0, turn_hidden))
                if turned_rows:
                    stages.append((1, fold))
                if last:
                    stages.append((2, lambda B: edge_weights(B, range(0, 2))))
                if NTAB == 2:
                    stages.append((0, lambda B: gather_blocks(B, 1)))
                else:
                    stages.append((SLAG * KS, scatter_sums))
                if last:
                    stages.append((2, lambda B: edge_weights(B, range(2, BT))))
                if NTAB == 2:
                    stages.append((SLAG * KS, scatter_sums))
            run_batches(pe, stages)

        @block.vector
        def _(v):
            for s in (oh_ready,) + ((masks,) if gathers else ()) + ((dve_step,) if kind == "product" else ()) + (
                    (contracted,) if last else ()) + ((halved,) if gathers and not turned_rows else ()):
                v.sem_inc(s, LEAD)
            if not gathers:
                v.memset(outer[:], 0.0).then_inc(zero_ready, 1)
                v.wait_ge(zero_ready, 1)
            v.memset(zero[:], 0.0).then_inc(zero_ready, 1)
            v.wait_ge(zero_ready, 1 if gathers else 2)

            def one_hots(B):
                done(v, scattered, B.n - KB + 1)
                if B.b == 0:
                    v.wait_ge(loaded[B.h], B.use * (16 * NLOAD) + 16 * NLOAD)
                tiles = slice(B.b * BT, (B.b + 1) * BT)
                ins = v.tensor_tensor(ohhi[:, B.k, :, :], natb[:, B.h, tiles, 2 * scatter + 1].unsqueeze(2).to_broadcast(
                    [P, BT, HI]), K.c("iota8").unsqueeze(1).to_broadcast([P, BT, HI]), ALU.is_equal)
                if gathers:
                    if not turned_rows:
                        v.tensor_tensor(ohg[:, B.k, :, :], natb[:, B.h, tiles, 2 * gather + 1].unsqueeze(2).to_broadcast(
                            [P, BT, HI]), K.c("iota8").unsqueeze(1).to_broadcast([P, BT, HI]), ALU.is_equal)
                    ins = v.tensor_scalar(ohT[:, B.k, :], idxb[:, B.h, 0, B.b * BT * P:(B.b + 1) * BT * P], K.c("lo"), None,
                                          ALU.is_equal)
                else:
                    for t in range(BT):
                        ins = v.tensor_scalar(ohlo[:, B.k, t, :], K.c("iota"),
                                              natb[:, B.h, B.b * BT + t, 2 * scatter:2 * scatter + 1], None, ALU.is_equal)
                ins.then_inc(oh_ready, 1)

            def mask(B, tab):
                done(v, gathered, B.n * NTAB + tab + 1)
                done(v, folded, B.n - RM + 1)
                if turned_rows:
                    ins = v.scalar_tensor_tensor(masked[:, B.k % RM, tab, :],
                                                 idxb[:, B.h, NIDX - 1, B.b * BT * P:(B.b + 1) * BT * P], K.c("blk"),
                                                 gps[:, B.k % G, :], ALU.is_equal, ALU.mult)
                else:
                    ins = v.tensor_tensor(masked[:, B.k % RM, tab, :].rearrange("p (b f) -> p b f", f=F),
                                          gps[:, B.k % G, :].rearrange("p (b f) -> p b f", f=F),
                                          ohg[:, B.k, :, :].rearrange("p t a -> p (t a)").unsqueeze(2).to_broadcast(
                                              [P, BT * HI, F]), ALU.mult)
                ins.then_inc(masks, 1)
                if kind == "copy":
                    done(v, masks, B.n + 1)
                    b = masked[:, B.k % RM, tab, :].rearrange("p (t b f) -> p t b f", b=HI, f=F)
                    v.tensor_tensor(b[:, :, 0:4, :], b[:, :, 0:4, :], b[:, :, 4:8, :], ALU.add).then_inc(halved, 1)

            def product(B):
                done(v, folded, B.n + 1)
                done(v, sums, B.n - 1)
                a8 = rows[:, B.h, B.b * BT:(B.b + 1) * BT, C_A8:C_A8 + DE]
                v.tensor_tensor(prod[:, B.k % 2, :, :].rearrange("p t (j f) -> p t j f", j=DE),
                                fold_ps[:].rearrange("p (t j f) -> p t j f", t=BT, j=DE),
                                a8.unsqueeze(3).to_broadcast([P, BT, DE, F]), ALU.mult).then_inc(dve_step, 1)

            def contract(B):
                done(v, folded, B.n + 1)
                done(v, weights, B.n * BT + 1)
                done(v, messages, B.n - 1)
                multiply(B, range(0, 2))

            def multiply(B, tiles):
                a = prod[:, B.k % 2, :, :].rearrange("p t (q j) -> p t q j", j=NJ)
                for t in tiles:
                    if t > 0:
                        done(v, weights, B.n * BT + t + 1)
                    v.tensor_tensor(a[:, t, :, :], w_ps[:, t % 2, 0:WN].rearrange("p (q j) -> p q j", j=NJ),
                                    z[:, B.k % RZ, t, :].unsqueeze(2).to_broadcast([P, NQ, NJ]), ALU.mult
                                    ).then_inc(contracted, 1)

            def contract_rest(B):
                multiply(B, range(2, BT))
                done(v, contracted, B.n * BT + BT)
                a = prod[:, B.k % 2, :, :].rearrange("p t (q j) -> p t q j", j=NJ)
                half = NQ // 2
                v.tensor_tensor(a[:, :, 0:half, :], a[:, :, 0:half, :], a[:, :, half:NQ, :], ALU.add).then_inc(halved, 1)

            stages = [(KS, lambda B: mask(B, 0))] if gathers else []
            stages.append((0, one_hots))
            if kind == "product":
                stages.append((KS + 1, product))
            if last:
                stages.append((KS + 2, contract))
            if NTAB == 2:
                stages.append((KS, lambda B: mask(B, 1)))
            if last:
                stages.append((KS + 2, contract_rest))
            run_batches(v, stages)
            done(v, scattered, NTURN * KB)
            ins = v.tensor_copy(acc_out[:], acc[:, 0:NW])
            if cnt_out is not None:
                ins.then_inc(flushed, 1)
                ins = v.tensor_copy(cnt_out[:], cnt_ps[:, 0:NBLK])
            ins.then_inc(flushed, 1)

        @block.scalar
        def _(act):
            if not gathers:
                return
            for s in (places, place_step) + ((hT_ready,) if last else (messages,) if turned_rows else ()):
                act.sem_inc(s, LEAD)

            def make_places(B):
                if B.b == 0:
                    act.wait_ge(loaded[B.h], B.use * (16 * NLOAD) + 16 * NLOAD)
                done(act, places, B.n - 1)
                for t in range(BT):
                    ins = nc.scalar.activation(far[:, B.k % 2, t, :], K.c("iota"), ACT.Abs, scale=-1.0,
                                               bias=natb[:, B.h, B.b * BT + t, 2 * scatter:2 * scatter + 1])
                ins.then_inc(place_step, 1)
                done(act, place_step, B.n + 1)
                done(act, scattered, B.n - KB + 1)
                nc.scalar.activation(ohlo[:, B.k, :, :], far[:, B.k % 2, :, :], ACT.Relu, scale=-1.0,
                                     bias=K.c("one")).then_inc(places, 1)

            def take_hidden(B):
                done(act, turned, B.n + 1)
                done(act, weights, (B.n - RZ + 1) * BT)
                nc.scalar.copy(hT[:, B.k % RZ, :], turn_ps[0:HW, :]).then_inc(hT_ready, 1)

            def message(B):
                done(act, outers, B.n - RO + 1)
                done(act, sums, B.n + 1)
                nc.scalar.activation(msg[:, B.k % RO, :, :], tsum[:, B.k % RO, :, :], ACT.Silu,
                                     scale=float(1.0 / np.sqrt(F * DE))).then_inc(messages, 1)
            run_batches(act, ([(KS, take_hidden)] if last else [(KS + 1, message)] if turned_rows else []) + [(0, make_places)])

        @block.gpsimd
        def _(pool):
            pool.sem_inc(outers, LEAD)
            for s in ((messages, folded) if last else (sums,) if turned_rows else (folded, messages) if gathers else ()) + (
                    (pool_step, fold_step) if gathers else ()):
                pool.sem_inc(s, LEAD)
            if not gathers:
                pool.wait_ge(zero_ready, 1)

            def add(out, a, b):
                return nc.gpsimd.tensor_tensor(out, a, b, ALU.add)

            def fold_blocks(B):
                a = masked[:, B.k % RM, :, :].rearrange("p n (t b f) -> p n t b f", b=HI, f=F)
                count, n = {"copy": 1, "first": 2, "second": 8}[kind], 0

                def step(ins):
                    nonlocal n
                    n += 1
                    ins.then_inc(fold_step, 1)
                    done(pool, fold_step, B.n * count + n)
                if last:
                    done(pool, contracted, (B.n - RZ + 1) * BT)
                for tab in range(NTAB):
                    b = a[:, tab]
                    if last:
                        done(pool, masks, B.n * NTAB + tab + 1)
                        step(add(b[:, :, 0:4, :], b[:, :, 0:4, :], b[:, :, 4:8, :]))
                    else:
                        done(pool, halved, B.n + 1)
                    step(add(b[:, :, 0:2, :], b[:, :, 0:2, :], b[:, :, 2:4, :]))
                    if tab == 1:
                        r = rows[:, B.h, B.b * BT:(B.b + 1) * BT, C_R:C_R + 3].unsqueeze(2).to_broadcast([P, BT, NV, 3])
                        v3 = zv[:, :, 0:3 * NV].rearrange("p t (j c) -> p t j c", c=3)
                        step(add(zv[:], b[:, :, 0, :], b[:, :, 1, :]))
                        step(nc.gpsimd.tensor_tensor(v3, v3, r, ALU.mult))
                        step(add(v3[:, :, :, 0], v3[:, :, :, 0], v3[:, :, :, 1]))
                        add(z[:, B.k % RZ, :, F:F + NV], v3[:, :, :, 0], v3[:, :, :, 2]).then_inc(folded, 1)
                    elif last:
                        ins = add(z[:, B.k % RZ, :, 0:F], b[:, :, 0, :], b[:, :, 1, :])
                        if NTAB == 2:
                            step(ins)
                        else:
                            ins.then_inc(folded, 1)
                    else:
                        done(pool, outers, B.n - RO + 1)
                        add(msg[:, B.k % RO, :, :], b[:, :, 0, :], b[:, :, 1, :]).then_inc(messages, 1)
                        done(pool, messages, B.n + 1)
                        pool.sem_inc(folded, 1)

            def rest_of_sum(B):
                a = prod[:, B.k % 2, :, :].rearrange("p t (q j) -> p t q j", j=F if kind == "product" else NJ)
                if kind == "product":
                    steps, q, out = 2, DE, tsum[:, B.k % RO, :, :]
                    done(pool, dve_step, B.n + 1)
                    done(pool, messages, B.n - RO + 1)
                else:
                    steps, q, out = 3, NQ // 2, msg[:, B.k % RO, :, :]
                    done(pool, halved, B.n + 1)
                n = 0

                def step(ins):
                    nonlocal n
                    n += 1
                    ins.then_inc(pool_step, 1)
                    done(pool, pool_step, B.n * steps + n)
                while q > 2:
                    half = q // 2
                    if q == 5:
                        step(add(a[:, :, 0, :], a[:, :, 0, :], a[:, :, 4, :]))
                    step(add(a[:, :, 0:half, :], a[:, :, 0:half, :], a[:, :, half:2 * half, :]))
                    q = half
                add(out, a[:, :, 0, :], a[:, :, 1, :]).then_inc(sums if kind == "product" else messages, 1)
                if kind == "first":
                    u = B.k // HB
                    done(pool, messages, B.n + 1)
                    if B.k % HB == 0 and not B.first:
                        pool.wait_ge(vec_stored[u], B.use * 16)
                        pool.sem_inc(pool_go, 1)
                    r = rows[:, B.h, B.b * BT:(B.b + 1) * BT, C_R:C_R + 3].unsqueeze(2).to_broadcast([P, BT, NV, 3])
                    step(nc.gpsimd.tensor_tensor(
                        vecs[:, u, B.k % HB * BT:(B.k % HB + 1) * BT, :].rearrange("p t (j c) -> p t j c", c=3),
                        msg[:, B.k % RO, :, F:F + NV].unsqueeze(3).to_broadcast([P, BT, NV, 3]), r, ALU.mult))
                    if B.k % HB == HB - 1:
                        pool.sem_inc(vec_ready, 1)

            def spread(B):
                done(pool, messages if gathers else oh_ready, B.n + 1)
                done(pool, scattered, B.n - RO + 1)
                m = msg[:, B.k % RO if gathers else B.k, :, 0:SHORT]
                nc.gpsimd.tensor_tensor(
                    outer[:, B.k % RO, :, :, 0:SHORT],
                    ohhi[:, B.k, :, :].unsqueeze(3).to_broadcast([P, BT, HI, SHORT]),
                    m.unsqueeze(2).to_broadcast([P, BT, HI, SHORT]), ALU.mult).then_inc(outers, 1)
            if kind == "product":
                run_batches(pool, [(0, rest_of_sum), (1, spread)])
            elif last:
                run_batches(pool, [(0, fold_blocks), (2, rest_of_sum), (2, spread)])
            elif gathers:
                run_batches(pool, [(0, fold_blocks), (0, spread)])
            else:
                run_batches(pool, [(0, spread)])


BDS = ["L0_gnn_W_msg_lin", "L0_gnn_W_upd_lin", "L1_gnn_w1a", "L1_gnn_w1b", "L1_gnn_w2a", "L1_gnn_w2b", "L2_gnn_W"]
VECS = ["L1_gnn_b1a", "L1_gnn_b1b", "L1_gnn_b2a", "L1_gnn_b2b", "L2_gnn_b", "L3_gnn_bn0_gs", "L3_gnn_bn0_bs",
        "L3_gnn_bn1_gs", "L3_gnn_bn1_bs", "L3_gnn_bn0_gv", "L1_gnn_eps1", "L1_gnn_eps2"]
EPS = 1e-5


def setup_nodes(K):
    nc = K.nc
    K.x = K.sb("x", [P, NBLK, F])
    K.acc = K.sb("acc", [P, NW])
    K.keep = K.sb("keep", [P, NBLK, F])
    K.src_count = K.sb("src_count", [P, NBLK])
    K.dst_count = K.sb("dst_count", [P, NBLK])
    K.tab = [K.sb(f"tab{n}", [P, 3, NW], BF16) for n in range(2)]
    K.bd = K.sb("bd", [P, len(BDS), P])
    K.vecs = K.sb("vecs", [P, len(VECS), F])
    K.w_msg = K.sb("w_msg", [P, DE * F])
    K.w_upd = K.sb("w_upd", [P, HI, F * F])
    K.offs = K.sb("offs_rows", [OFFP + 1, NSB + SLAG, 2, SPAIR], I32)
    K.w2 = [K.sb(f"w2_{n}", [HW, (F + NV) * F]) for n in range(2)]
    cleared, loaded, loaded2 = K.sem("n_cleared"), K.sem("n_loaded"), K.sem("n_loaded2")
    whole = N_NODES // P
    jobs = []
    for w, n in enumerate(BDS):
        jobs += [(K.bd[F * k:F * k + F, w, F * k:F * k + F], K.ins[n]) for k in range(HI)]
    for k in range(HI):
        jobs.append((K.w_msg[F * k:F * k + F, :], K.ins["L0_gnn_W_msg_tp"].rearrange("i j h -> i (j h)")))
        jobs.append((K.w_upd[F * k:F * k + F, k, :], K.ins["L0_gnn_W_upd_tp"].rearrange("i h k -> i (h k)")))
    for w, n in enumerate(VECS):
        a = K.ins[n]
        jobs.append((K.vecs[:, w, 0:a.shape[0]], a.partition_broadcast(P)))
    w0 = K.w2[0][:].rearrange("k (i j) -> k i j", j=F + NV)
    for rows, src in ((slice(0, DH), K.ins["L3_gnn_fc0_w2"]), (slice(DH, HW), K.ins["L3_gnn_fc0_b2"].rearrange("(a d) -> a d", a=1))):
        jobs.append((w0[rows, :, 0:F], src[:, 0:F * F].rearrange("k (i j) -> k i j", j=F)))
        jobs.append((w0[rows, :, F:F + NV], src[:, F * F:].rearrange("k (i j) -> k i j", j=NV)))
    jobs.append((K.w2[1][0:DH, :], K.ins["L3_gnn_fc1_w2"]))
    jobs.append((K.w2[1][DH:HW, :], K.ins["L3_gnn_fc1_b2"].rearrange("(a d) -> a d", a=1)))
    for side in (SRC, DST):
        pairs = K.offs_d[side:side + 1, 0:NPAIR].rearrange("o (i k) -> o i k", k=SPAIR)
        at, other = side * OFFP, (1 - side) * OFFP
        jobs.append((K.offs[at:at + 1, 0:NSB, 0, :], pairs))
        jobs.append((K.offs[other:other + 1, SLAG:NSB + SLAG, 1, :], pairs))
    jobs.append((K.x[:, 0:whole, :], K.ins["x"][0:whole * P].rearrange("(b p) f -> p b f", p=P)))
    jobs.append((K.x[0:N_NODES - whole * P, whole, :], K.ins["x"][whole * P:N_NODES]))
    with nc.Block() as block:
        @block.vector
        def _(v):
            v.memset(K.bd[:], 0.0)
            v.memset(K.w_upd[:], 0.0)
            v.memset(K.vecs[:], 0.0)
            v.memset(K.x[:], 0.0).then_inc(cleared, 1)

        @block.sync
        def _(sp):
            sp.wait_ge(cleared, 1)
            for dst, src in jobs[0::2]:
                sp.dma_start(dst, src).then_inc(loaded, 16)
            sp.wait_ge(loaded, 16 * len(jobs[0::2]))

        @block.scalar
        def _(act):
            act.wait_ge(cleared, 1)
            for dst, src in jobs[1::2]:
                act.dma_start(dst, src).then_inc(loaded2, 16)
            act.wait_ge(loaded2, 16 * len(jobs[1::2]))


class Nodes:

    def __init__(self, K, name, linears=(), functions=(), totals=0, update=False):
        self.K, self.nc, self.name = K, K.nc, name
        self.linears, self.functions, self.totals, self.update = linears, functions, totals, update
        self.ctx = ExitStack()

    def __enter__(self):
        K, n, ctx = self.K, self.name, self.ctx
        self.y = K.sb(f"{n}_y", [P, NBLK, F], F32, ctx)
        self.sq = K.sb(f"{n}_sq", [P, NBLK, F], F32, ctx)
        self.s = K.sb(f"{n}_s", [P, NBLK], F32, ctx)
        self.r = K.sb(f"{n}_r", [P, NBLK], F32, ctx)
        self.part = K.sb(f"{n}_part", [P, F], F32, ctx)
        self.stat = K.sb(f"{n}_stat", [P, 4, F], F32, ctx)
        self.xT = K.sb(f"{n}_xT", [P, NW], F32, ctx)
        self.ones = K.sb(f"{n}_ones", [P, P], F32, ctx)
        self.turn_ps = K.ps(ctx, f"{n}_turn_ps", [P, 4 * 512])
        self.lin_ps = K.ps(ctx, f"{n}_lin_ps", [P, 4 * 512])
        self.dve = K.sem(f"{n}_dve")
        self.lin_in, self.lin_out = K.sem(f"{n}_lin_in"), K.sem(f"{n}_lin_out")
        self.turned, self.taken = K.sem(f"{n}_turned"), K.sem(f"{n}_taken")
        self.func_in, self.func_out = K.sem(f"{n}_func_in"), K.sem(f"{n}_func_out")
        self.tot_in, self.tot_out = K.sem(f"{n}_tot_in"), K.sem(f"{n}_tot_out")
        self.n_lin = self.n_func = self.n_tot = 0
        self.block = ctx.enter_context(self.nc.Block())
        return self

    def __exit__(self, *e):
        return self.ctx.__exit__(*e)

    def linear(self):
        self.n_lin += 1
        self.v.sem_inc(self.lin_in, 1)
        self.v.wait_ge(self.lin_out, self.n_lin)
        return self.lin_ps[:, 0:NW].rearrange("p (b f) -> p b f", f=F)

    def function(self):
        self.n_func += 1
        self.v.sem_inc(self.func_in, 1)
        self.v.wait_ge(self.func_out, self.n_func)

    def total(self):
        self.n_tot += 1
        self.v.sem_inc(self.tot_in, 1)
        self.v.wait_ge(self.tot_out, self.n_tot)
        return self.lin_ps[:, 0:F]

    def start_vector(self, v):
        self.v, self.step = v, Chain(v, self.dve)
        self.step(v.memset(self.ones[:], 1.0))

    def vec(self, name, n=F):
        return self.K.vecs[:, VECS.index(name), 0:n]

    def row(self, name):
        return self.vec(name).unsqueeze(1).to_broadcast([P, NBLK, F])

    def each(self, a):
        return a[:].unsqueeze(2).to_broadcast([P, NBLK, F])

    def split(self, tab, a):
        v, step, flat = self.v, self.step, a.rearrange("p b f -> p (b f)")
        rest = self.sq[:].rearrange("p b f -> p (b f)")
        step(v.tensor_copy(tab[:, 0, :], flat))
        step(v.tensor_tensor(rest, flat, tab[:, 0, :], ALU.subtract))
        step(v.tensor_copy(tab[:, 1, :], rest))
        step(v.tensor_tensor(rest, rest, tab[:, 1, :], ALU.subtract))
        step(v.tensor_copy(tab[:, 2, :], rest))

    def layernorm(self, out):
        v, step = self.v, self.step
        step(v.tensor_reduce(self.s[:], self.y[:], AX.X, ALU.add))
        step(v.tensor_scalar(self.s[:], self.s[:], 1.0 / F, None, ALU.mult))
        step(v.tensor_tensor(self.y[:], self.y[:], self.each(self.s), ALU.subtract))
        step(v.tensor_tensor(self.sq[:], self.y[:], self.y[:], ALU.mult))
        step(v.tensor_reduce(self.r[:], self.sq[:], AX.X, ALU.add))
        step(v.tensor_scalar(self.r[:], self.r[:], 1.0 / F, EPS, ALU.mult, ALU.add))
        self.function()
        step(v.reciprocal(self.r[:], self.r[:]))
        step(v.tensor_tensor(out, self.y[:], self.each(self.r), ALU.mult))

    def run_tensor(self, pe):
        K = self.K
        for k, (src, w) in enumerate(self.linears):
            pe.wait_ge(self.lin_in, k + 1)
            flat = src.rearrange("p b f -> p (b f)")
            for g in range(NG):
                ins = pe.transpose(self.turn_ps[:, g * P:(g + 1) * P], flat[:, g * P:(g + 1) * P], K.c("ident"))
            ins.then_inc(self.turned, 1)
            pe.wait_ge(self.taken, k + 1)
            if w is None:
                self.update_products(pe)
                continue
            for g in range(NG):
                ins = pe.matmul(self.lin_ps[:, g * P:(g + 1) * P], self.xT[:, g * P:(g + 1) * P], K.bd[:, BDS.index(w), :],
                                start=True, stop=True)
            ins.then_inc(self.lin_out, 1)
        for k in range(self.totals):
            pe.wait_ge(self.tot_in, k + 1)
            pe.matmul(self.lin_ps[:, 0:F], self.ones[:], self.part[:], start=True, stop=True).then_inc(self.tot_out, 1)

    def run_scalar(self, act):
        lin = func = 0
        for f in self.functions:
            if f is None:
                lin += 1
                act.wait_ge(self.turned, lin)
                self.nc.scalar.copy(self.xT[:], self.turn_ps[:, 0:NW]).then_inc(self.taken, 1)
            else:
                func += 1
                act.wait_ge(self.func_in, func)
                out, in_, name, scale = f
                self.nc.scalar.activation(out, in_, name, scale=scale).then_inc(self.func_out, 1)

    def engines(self, lead):
        @self.block.vector
        def _(v):
            self.start_vector(v)
            lead(v)

        @self.block.tensor
        def _(pe):
            pe.wait_ge(self.dve, 1)
            self.run_tensor(pe)

        @self.block.scalar
        def _(act):
            self.run_scalar(act)


def sqrt_r(N):
    return (N.r[:], N.r[:], ACT.Sqrt, 1.0)


def acc_nodes(K):
    return K.acc[:].rearrange("p (b f) -> p b f", f=F)


def first_table(K):
    with Nodes(K, "n0") as N:
        N.engines(lambda v: N.split(K.tab[0], K.x[:]))


def update_first(K):
    nc = K.nc
    lin_norm, upd_norm = 1.0 / np.sqrt(F), 1.0 / np.sqrt(F * F)
    with Nodes(K, "n1") as N:
        agg = K.sb("n1_agg", [P, NBLK, F], F32, N.ctx)
        prod = K.sb("n1_prod", [P, 4, F, F], F32, N.ctx)
        upd_ready, upd_used = K.sem("n1_upd_ready"), K.sem("n1_upd_used")
        half = HI // 2

        def bank(n):
            return N.lin_ps[:, n % 2 * 1024:n % 2 * 1024 + half * F * F]

        def update_products(pe):
            for n in range(2 * NG):
                if n >= 2:
                    pe.wait_ge(upd_used, n - 1)
                for k in range(half):
                    ins = pe.matmul(bank(n)[:, k * F * F:(k + 1) * F * F], N.xT[:, n // 2 * P:(n // 2 + 1) * P],
                                    K.w_upd[:, n % 2 * half + k, :], start=True, stop=True)
                ins.then_inc(upd_ready, 1)
        N.update_products = update_products
        N.linears = [(acc_nodes(K), "L0_gnn_W_msg_lin"), (K.x[:], None), (N.y[:], "L0_gnn_W_upd_lin")]
        N.functions = [None, None, (N.y[:], N.y[:], ACT.Silu, float(lin_norm * upd_norm)), None, sqrt_r(N)]

        def lead(v):
            step = N.step
            step(v.tensor_copy(agg[:], N.linear()))
            N.n_lin += 1
            v.sem_inc(N.lin_in, 1)
            for n in range(2 * NG):
                v.wait_ge(upd_ready, n + 1)
                blocks = slice(n * half, (n + 1) * half)
                v.tensor_tensor(prod[:], bank(n).rearrange("p (b h k) -> p b h k", h=F, k=F),
                                agg[:, blocks, :].unsqueeze(3).to_broadcast([P, half, F, F]), ALU.mult).then_inc(upd_used, 1)
                v.wait_ge(upd_used, n + 1)
                step(v.tensor_reduce(N.y[:, blocks, :], prod[:].rearrange("p b h k -> p b k h"), AX.X, ALU.add))
            N.n_lin -= 1
            N.function()
            u = N.linear()
            step(v.scalar_tensor_tensor(N.y[:], K.x[:], 2.0 / lin_norm, u, ALU.mult, ALU.add))
            step(v.tensor_scalar(N.y[:], N.y[:], float(lin_norm), None, ALU.mult))
            N.layernorm(K.x[:])
            N.split(K.tab[0], K.x[:])
        N.engines(lead)


def gin(K, N, v, x, eps, wa, wb):
    step = N.step
    step(v.tensor_scalar(N.s[:, 0:1], N.vec(eps, 1), 1.0, None, ALU.add))
    flat = x.rearrange("p b f -> p (b f)")
    step(v.scalar_tensor_tensor(N.y[:].rearrange("p b f -> p (b f)"), flat, N.s[:, 0:1], K.acc[:], ALU.mult, ALU.add))
    step(v.tensor_tensor(N.y[:], N.linear(), N.row(wa), ALU.add))
    step(v.tensor_scalar(N.y[:], N.y[:], 0.0, None, ALU.max))
    step(v.tensor_tensor(N.y[:], N.linear(), N.row(wb), ALU.add))


def gin_first(K):
    with Nodes(K, "n2") as N:
        N.linears = [(N.y[:], "L1_gnn_w1a"), (N.y[:], "L1_gnn_w1b")]
        N.functions = [None, None]

        def lead(v):
            gin(K, N, v, K.x[:], "L1_gnn_eps1", "L1_gnn_b1a", "L1_gnn_b1b")
            N.step(v.tensor_scalar(K.keep[:], N.y[:], 0.0, None, ALU.max))
            N.split(K.tab[0], K.keep[:])
        N.engines(lead)


def gin_second(K):
    with Nodes(K, "n3") as N:
        dinv = K.dst_count
        N.linears = [(N.y[:], "L1_gnn_w2a"), (N.y[:], "L1_gnn_w2b"), (K.x[:], "L2_gnn_W")]
        N.functions = [None, None, (N.sq[:], N.y[:], ACT.Exp, 1.0), (N.s[:], N.s[:], ACT.Ln, 1.0), sqrt_r(N),
                       (dinv[:], dinv[:], ACT.Sqrt, 1.0), None]

        def lead(v):
            step = N.step
            gin(K, N, v, K.keep[:], "L1_gnn_eps2", "L1_gnn_b2a", "L1_gnn_b2b")
            step(v.tensor_reduce(N.s[:], N.y[:], AX.X, ALU.max))
            step(v.tensor_tensor(N.y[:], N.y[:], N.each(N.s), ALU.subtract))
            N.function()
            step(v.tensor_reduce(N.s[:], N.sq[:], AX.X, ALU.add))
            N.function()
            step(v.tensor_tensor(N.y[:], N.y[:], N.each(N.s), ALU.subtract))
            step(v.tensor_tensor(N.y[:], N.y[:], K.x[:], ALU.add))
            N.layernorm(K.x[:])
            step(v.tensor_scalar(dinv[:], dinv[:], 1.0, None, ALU.add))
            N.function()
            step(v.reciprocal(dinv[:], dinv[:]))
            step(v.tensor_tensor(K.keep[:], N.linear(), N.each(dinv), ALU.mult))
            N.split(K.tab[0], K.keep[:])
        N.engines(lead)


def gcn(K):
    with Nodes(K, "n4") as N:
        N.functions = [sqrt_r(N)]

        def lead(v):
            step = N.step
            step(v.tensor_tensor(N.y[:], acc_nodes(K), K.keep[:], ALU.add))
            step(v.tensor_tensor(N.y[:], N.y[:], N.each(K.dst_count), ALU.mult))
            step(v.tensor_tensor(N.y[:], N.y[:], N.row("L2_gnn_b"), ALU.add))
            step(v.tensor_tensor(N.y[:], N.y[:], K.x[:], ALU.add))
            N.layernorm(K.x[:])
            N.split(K.tab[0], K.x[:])
        N.engines(lead)


def batch_norm(K, N, v, a, gain, bias, which):
    step = N.step
    mean, scale = N.stat[:, 0, :], N.stat[:, 1, :]
    valid = K.c("valid").unsqueeze(2).to_broadcast([P, NBLK, F])

    def over_nodes(x, out, bias):
        step(v.tensor_reduce(N.part[:], x.rearrange("p b f -> p f b"), AX.X, ALU.add))
        step(v.tensor_scalar(out, N.total(), 1.0 / N_NODES, bias, ALU.mult, ALU.add))

    def spread(x):
        return x.unsqueeze(1).to_broadcast([P, NBLK, F])
    over_nodes(a, mean, 0.0)
    step(v.tensor_tensor(a, a, spread(mean), ALU.subtract))
    step(v.tensor_tensor(N.sq[:], a, a, ALU.mult))
    step(v.tensor_tensor(N.sq[:], N.sq[:], valid, ALU.mult))
    over_nodes(N.sq[:], scale, EPS)
    N.function()
    step(v.reciprocal(scale, scale))
    step(v.tensor_tensor(scale, scale, N.vec(gain), ALU.mult))
    step(v.tensor_tensor(a, a, spread(scale), ALU.mult))
    step(v.tensor_tensor(a, a, spread(N.vec(bias)), ALU.add))


def sqrt_stat(N, k):
    return (N.stat[:, k, :], N.stat[:, k, :], ACT.Sqrt, 1.0)


def mean_of(K, N, v, factor):
    N.step(v.tensor_scalar(N.r[:], K.src_count[:], 1.0, None, ALU.max))
    N.step(v.reciprocal(N.r[:], N.r[:]))
    N.step(v.tensor_scalar(N.r[:], N.r[:], float(factor), None, ALU.mult))


def norm_first(K):
    with Nodes(K, "n6", totals=3) as N:
        N.functions = [sqrt_stat(N, 1), sqrt_stat(N, 2)]

        def lead(v):
            step = N.step
            mean_of(K, N, v, 1.0 / np.sqrt(F))
            step(v.tensor_tensor(N.y[:], K.keep[:], N.each(N.r), ALU.mult))
            batch_norm(K, N, v, N.y[:], "L3_gnn_bn0_gs", "L3_gnn_bn0_bs", 0)
            N.split(K.tab[0], N.y[:])
            step(v.tensor_scalar(N.r[:], N.r[:], float(np.sqrt(3.0)), None, ALU.mult))
            step(v.tensor_tensor(N.y[:], acc_nodes(K), N.each(N.r), ALU.mult))
            step(v.tensor_tensor(N.sq[:], N.y[:], N.y[:], ALU.mult))
            step(v.tensor_reduce(N.part[:], N.sq[:].rearrange("p b f -> p f b"), AX.X, ALU.add))
            tot = N.total()
            scale = N.stat[:, 2, 0:NV]
            step(v.memset(N.stat[:, 2, :], 1.0))
            step(v.tensor_reduce(scale, tot[:, 0:3 * NV].rearrange("p (j c) -> p j c", c=3), AX.X, ALU.add))
            step(v.tensor_scalar(scale, scale, 1.0 / (3 * N_NODES), EPS, ALU.mult, ALU.add))
            N.function()
            step(v.reciprocal(scale, scale))
            step(v.tensor_tensor(scale, scale, N.vec("L3_gnn_bn0_gv", NV), ALU.mult))
            step(v.memset(N.stat[:, 3, :], 0.0))
            step(v.tensor_copy(N.stat[:, 3, 0:3 * NV].rearrange("p (j c) -> p j c", c=3),
                               scale.unsqueeze(2).to_broadcast([P, NV, 3])))
            step(v.tensor_tensor(N.y[:], N.y[:], N.stat[:, 3, :].unsqueeze(1).to_broadcast([P, NBLK, F]), ALU.mult))
            N.split(K.tab[1], N.y[:])
        N.engines(lead)


def finish(K):
    whole = N_NODES // P
    with Nodes(K, "n7", totals=2) as N:
        N.functions = [sqrt_stat(N, 1), sqrt_r(N)]
        stored = K.sem("n7_stored")

        def lead(v):
            step = N.step
            mean_of(K, N, v, 1.0 / np.sqrt(F + NV))
            step(v.tensor_tensor(N.y[:], acc_nodes(K), N.each(N.r), ALU.mult))
            batch_norm(K, N, v, N.y[:], "L3_gnn_bn1_gs", "L3_gnn_bn1_bs", 0)
            step(v.tensor_tensor(N.y[:], N.y[:], K.x[:], ALU.add))
            N.layernorm(K.keep[:])
            v.sem_inc(N.lin_in, 1)
        N.engines(lead)

        @N.block.sync
        def _(sp):
            sp.wait_ge(N.lin_in, 1)
            sp.dma_start(K.out[0:whole * P].rearrange("(b p) f -> p b f", p=P), K.keep[:, 0:whole, :]).then_inc(stored, 16)
            sp.dma_start(K.out[whole * P:N_NODES], K.keep[0:N_NODES - whole * P, whole, :]).then_inc(stored, 16)
            sp.wait_ge(stored, 32)


def program(nc, ins, out):
    with ExitStack() as ctx:
        K = Kernel(nc, ctx, ins, out)
        load_constants(K)
        K.end_phase()
        sort_edges(K)
        K.end_phase()
        unpack_indices(K)
        K.end_phase()
        setup_nodes(K)
        K.end_phase()
        first_table(K)
        K.end_phase()
        edge_pass(K, "e0", DST, SRC, "product", [K.tab[0]], K.acc, K.src_count)
        K.end_phase()
        update_first(K)
        K.end_phase()
        edge_pass(K, "e1", SRC, DST, "copy", [K.tab[0]], K.acc, K.dst_count)
        K.end_phase()
        gin_first(K)
        K.end_phase()
        edge_pass(K, "e2", SRC, DST, "copy", [K.tab[0]], K.acc)
        K.end_phase()
        gin_second(K)
        K.end_phase()
        edge_pass(K, "e3", SRC, DST, "copy", [K.tab[0]], K.acc)
        K.end_phase()
        gcn(K)
        K.end_phase()
        edge_pass(K, "e4", DST, SRC, "first", [K.tab[0]], K.keep[:].rearrange("p b f -> p (b f)"))
        K.end_phase()
        edge_pass(K, "e5", None, SRC, "stored", [], K.acc)
        K.end_phase()
        norm_first(K)
        K.end_phase()
        edge_pass(K, "e6", DST, SRC, "second", K.tab, K.acc)
        K.end_phase()
        finish(K)
        K.end_phase()


_INS = ["x", "src", "dst", "edge_attr_3", "edge_attr_48", "edge_attr_8",
        "L0_gnn_W_msg_tp", "L0_gnn_W_msg_lin", "L0_gnn_W_upd_tp", "L0_gnn_W_upd_lin",
        "L1_gnn_eps1", "L1_gnn_w1a", "L1_gnn_b1a", "L1_gnn_w1b", "L1_gnn_b1b",
        "L1_gnn_eps2", "L1_gnn_w2a", "L1_gnn_b2a", "L1_gnn_w2b", "L1_gnn_b2b", "L2_gnn_W", "L2_gnn_b",
        "L3_gnn_fc0_w1", "L3_gnn_fc0_b1", "L3_gnn_fc0_w2", "L3_gnn_fc0_b2",
        "L3_gnn_fc1_w1", "L3_gnn_fc1_b1", "L3_gnn_fc1_w2", "L3_gnn_fc1_b2",
        "L3_gnn_bn0_gs", "L3_gnn_bn0_bs", "L3_gnn_bn0_gv", "L3_gnn_bn1_gs", "L3_gnn_bn1_bs"]


def kernel(**inputs):
    import concourse.bacc as bacc
    from concourse.bass_utils import run_bass_kernel_spmd

    nc = bacc.Bacc("TRN2", target_bir_lowering=False, num_devices=1)
    arrays = {"in_consts": build_constants()}
    for name in _INS:
        a = np.ascontiguousarray(inputs[name])
        arrays[f"in_{name}"] = a.reshape(1) if a.ndim == 0 else a
    ins = {n[3:]: nc.dram_tensor(n, a.shape, mybir.dt.from_np(a.dtype), kind="ExternalInput").ap()
           for n, a in arrays.items()}
    out = nc.dram_tensor("out", (N_NODES, F), F32, kind="ExternalOutput").ap()
    program(nc, ins, out)
    r = run_bass_kernel_spmd(nc, [arrays], core_ids=[0])
    return r.results[0]["out"]
```

```python
from contextlib import ExitStack

import concourse.bass as bass
import numpy as np
from concourse import mybir

ALU = mybir.AluOpType
ACT = mybir.ActivationFunctionType
AX = mybir.AxisListType
F32 = mybir.dt.float32
BF16 = mybir.dt.bfloat16
I32 = mybir.dt.int32

P = 128
N_NODES = 12500
N_EDGES = 400000
F = 16
DE = 8
DH = 48
NV = 4
HI = 8
GROUP = HI * P
NG = -(-N_NODES // GROUP)
NBLK = NG * HI
NW = NBLK * F
NBKT = NG * NG
OHW = 176
EPP = N_EDGES // P
SUB = 25
GRP = 5
SLOTS = 5
NSUB = EPP // SUB
PAIR = 2
NT_MIN = (N_EDGES + NBKT * (PAIR * P - 1)) // P
BT = 4
PADT = 8
SB = 8
NSL = 4
LOOP = NSL * SB
NT = -(-NT_MIN // LOOP) * LOOP
NTURN = NT // LOOP
NPAIR = NT // PAIR
NCHUNK = -(-NPAIR // P)
KB = LOOP // BT
KS = SB // BT
PADLO = 256.0

C_SLO, C_SHI, C_DLO, C_DHI, C_R, C_A8, C_HA = 0, 1, 2, 3, 4, 8, 16
HW = DH + 1
C_HB = C_HA + HW
ROW = C_HB + HW
OFFP = 32
NSB = NT // SB
SPAIR = SB // PAIR
SLAG = 2
SRC, DST = 0, 1
BANK = 512
CW = P + HI
CG = BANK // CW
LEAD = 16

CONSTS = {}


def build_constants():
    p = np.arange(P)
    parts = {
        "ident": np.eye(P),
        "iota": np.tile(np.arange(P), (P, 1)),
        "bucket": np.tile(np.arange(OHW), (P, 1)),
        "before": (p[:, None] < p[None, :]),
        "notbefore": (p[:, None] >= p[None, :]),
        "iota8": np.tile(np.arange(HI), (P, 1)),
        "lo": p[:, None],
        "one": np.ones((P, 1)),
        "blk": p[:, None] // F,
        "valid": (np.arange(NBLK)[None, :] * P + p[:, None] < N_NODES),
        "tau": PAIR * (np.arange(NCHUNK)[None, :] * P + p[:, None]),
    }
    at = 0
    for name, a in parts.items():
        CONSTS[name] = (at, a.shape[1])
        at += a.shape[1]
    return np.concatenate([np.asarray(a, np.float32) for a in parts.values()], axis=1)


class Chain:

    def __init__(self, eng, sem):
        self.eng, self.sem, self.n = eng, sem, 0

    def __call__(self, ins):
        self.n += 1
        ins.then_inc(self.sem, 1)
        self.eng.wait_ge(self.sem, self.n)


class Kernel:

    def __init__(self, nc, ctx, ins, out):
        self.nc, self.ins, self.out, self.ctx = nc, ins, out, ctx
        self.sems = []
        self.rows_d = nc.dram_tensor("edge_rows", (P * NT, ROW), F32, kind="Internal").ap()
        self.idxT_d = nc.dram_tensor("idx_rows", (NTURN, 4 * LOOP * P), BF16, kind="Internal").ap()
        self.nat_d = nc.dram_tensor("idx_nat", (P, NT * 4), F32, kind="Internal").ap()
        self.vec_d = nc.dram_tensor("vector_messages", (P, NT * 3 * NV), F32, kind="Internal").ap()
        self.offs_d = nc.dram_tensor("tile_offsets", (4, NCHUNK * P), I32, kind="Internal").ap()
        w = sum(n for _, n in CONSTS.values())
        self.consts = self.sb("consts", [P, w], F32)

    def c(self, name):
        at, n = CONSTS[name]
        return self.consts[:, at:at + n]

    def sb(self, name, shape, dt=F32, ctx=None):
        return (ctx or self.ctx).enter_context(self.nc.sbuf_tensor(name, shape, dt))

    def ps(self, ctx, name, shape, dt=F32):
        return ctx.enter_context(self.nc.psum_tensor(name, shape, dt))

    def sem(self, name):
        self.sems.append(self.nc.alloc_semaphore(name=name))
        return self.sems[-1]

    def end_phase(self):
        self.nc.all_engine_barrier()
        self.nc.clear_and_free_semaphores(self.sems)
        self.nc.all_engine_barrier()
        self.sems = []


def load_constants(K):
    nc = K.nc
    loaded = K.sem("consts_loaded")
    with nc.Block() as block:
        @block.sync
        def _(sp):
            sp.dma_start(K.consts[:], K.ins["consts"]).then_inc(loaded, 16)
            sp.wait_ge(loaded, 16)


def sort_edges(K):
    nc = K.nc
    with ExitStack() as ctx:
        def sb(name, shape, dt=F32):
            return K.sb(name, shape, dt, ctx)

        src_i = sb("src_i", [P, EPP], I32)
        dst_i = sb("dst_i", [P, EPP], I32)
        shi_i = sb("shi_i", [P, EPP], I32)
        dhi_i = sb("dhi_i", [P, EPP], I32)
        key = sb("key", [P, EPP], BF16)
        vec = sb("vec", [P, EPP, 3])
        buckets = sb("buckets", [P, OHW], BF16)
        before = sb("before", [P, P], BF16)
        notbefore = sb("notbefore", [P, P], BF16)
        ones = sb("ones", [P, P], BF16)
        onesrow = sb("onesrow", [NG, P])
        zeros = sb("zeros", [P, 512], BF16)
        zerof = sb("zerof", [P, NBKT])
        oh = sb("oh", [P, SUB, OHW], BF16)
        w1 = sb("w1", [HW, 2 * DH])
        cnt_i = sb("cnt_i", [P, NBKT], I32)
        tiles = sb("tiles", [P, NBKT])
        end = sb("end", [P, NBKT])
        start = sb("start", [P, GRP, NBKT])
        junk = sb("junk", [P, GRP, NBKT])
        counts = junk[0:NG]
        tb = sb("tb", [P, 4, NCHUNK])
        offs = sb("offs", [P, P], I32)
        pad = sb("pad", [P, PADT, ROW])
        rows = sb("rows", [P, SLOTS, SUB, ROW])
        attr = sb("attr", [P, SLOTS, SUB * DH])
        norm = attr[:].rearrange("p s c -> p (s c)")[:, 0:EPP]
        a8 = sb("a8", [P, SLOTS, SUB * DE])
        aT = sb("aT", [HW, GRP * P])
        both = oh[:].rearrange("p t b -> p (t b)")[:, 0:2 * SLOTS * SUB * NG].rearrange(
            "p (n s t g) -> p n s t g", n=2, s=SLOTS, t=SUB)
        ohs, ohd = both[:, 0], both[:, 1]
        pos = sb("pos", [P, SUB])
        pos_i = sb("pos_i", [P, SUB], I32)
        part_i = sb("part_i", [P, SUB], I32)
        tile_i = sb("tile_i", [P, SUB], I32)
        place = sb("place", [P, SLOTS, SUB], I32)
        count_ps = K.ps(ctx, "count_ps", [P, GRP, 512])
        counter = [count_ps[:, c, 0:NBKT] for c in range(GRP)]
        tp_ps = K.ps(ctx, "tp_ps", [P, 1024])
        h_ps = K.ps(ctx, "h_ps", [P, 512])
        hist_ps, off_ps = h_ps, tp_ps

        idx_loaded, vec_loaded, w_loaded = K.sem("s_idx_loaded"), K.sem("s_vec_loaded"), K.sem("s_w_loaded")
        pad_ready, es_filled = K.sem("s_pad_ready"), K.sem("s_es_filled")
        dve_chain, act_norm, norm2_ready = K.sem("s_dve_chain"), K.sem("s_act_norm"), K.sem("s_norm2_ready")
        hist_ready, hist_used, zero_done = K.sem("s_hist_ready"), K.sem("s_hist_used"), K.sem("s_zero_done")
        start_ready, offs_ready, offs_stored = K.sem("s_start_ready"), K.sem("s_offs_ready"), K.sem("s_offs_stored")
        oh_ready, p_ready, sel_done, rank_used = (K.sem("s_oh_ready"), K.sem("s_p_ready"), K.sem("s_sel_done"),
                                                  K.sem("s_rank_used"))
        attr_loaded, a8_used = K.sem("s_attr_loaded"), K.sem("s_a8_used")
        sp_go, pe_go, counts_ready, spread_ready = (K.sem("s_sp_go"), K.sem("s_pe_go"), K.sem("s_counts_ready"),
                                                    K.sem("s_spread_ready"))
        tp_ready, aT_ready, h_ready = K.sem("s_tp_ready"), K.sem("s_aT_ready"), K.sem("s_h_ready")
        place_ready, row_ready, pool_go = K.sem("s_place_ready"), K.sem("s_row_ready"), K.sem("s_pool_go")
        rowconst_ready, place_step, slot_free = K.sem("s_rowconst_ready"), K.sem("s_place_step"), K.sem("s_slot_free")
        groups_ready, offs_turned = K.sem("s_groups_ready"), K.sem("s_offs_turned")
        scattered = [K.sem(f"s_scattered{s}") for s in range(SLOTS)]
        NGRP = SUB // GRP
        LAG = 3

        def turns(eng, body):
            for s in range(SLOTS):
                body(s, s, True)
            with eng.Fori(1, NSUB // SLOTS) as turn:
                for s in range(SLOTS):
                    body(turn * SLOTS + s, s, False)

        block = ctx.enter_context(nc.Block())

        @block.sync
        def _(sp):
            sp.dma_start(src_i[:], K.ins["src"].rearrange("(p t) -> p t", p=P)).then_inc(idx_loaded, 16)
            sp.dma_start(dst_i[:], K.ins["dst"].rearrange("(p t) -> p t", p=P)).then_inc(idx_loaded, 16)
            sp.dma_start(vec[:].rearrange("p t c -> p (t c)"),
                         K.ins["edge_attr_3"].rearrange("(p t) c -> p (t c)", p=P)).then_inc(vec_loaded, 16)
            for n, fc in enumerate(("fc0", "fc1")):
                sp.dma_start(w1[0:DH, n * DH:(n + 1) * DH], K.ins[f"L3_gnn_{fc}_w1"]).then_inc(w_loaded, 16)
                sp.dma_start(w1[DH:HW, n * DH:(n + 1) * DH],
                             K.ins[f"L3_gnn_{fc}_b1"].rearrange("(a d) -> a d", a=1)).then_inc(w_loaded, 16)
            sp.wait_ge(pad_ready, 1)
            rows_v = K.rows_d.rearrange("(p t) c -> p (t c)", p=P)
            with sp.Fori(0, NT // PADT) as r:
                sp.dma_start(rows_v[:, bass.ds(r * (PADT * ROW), PADT * ROW)],
                             pad[:].rearrange("p t c -> p (t c)")).then_inc(es_filled, 16)
            sp.wait_ge(offs_ready, 1)
            sp.dma_start(K.offs_d.rearrange("k (c p) -> (k c) p", p=P), offs[0:4 * NCHUNK, :]).then_inc(offs_stored, 16)

            sp.wait_ge(rowconst_ready, 1)

            def load(q, s, first):
                if not first:
                    sp.wait_ge(tp_ready, (q - SLOTS + 1) * NGRP)
                    sp.wait_ge(a8_used, q - SLOTS + 1)
                    sp.sem_inc(sp_go, 1)
                sp.dma_start(attr[:, s, :], K.ins["edge_attr_48"].rearrange("(p t) c -> p (t c)", p=P)[
                    :, bass.ds(q * (SUB * DH), SUB * DH)]).then_inc(attr_loaded, 16)
                sp.dma_start(a8[:, s, :], K.ins["edge_attr_8"].rearrange("(p t) c -> p (t c)", p=P)[
                    :, bass.ds(q * (SUB * DE), SUB * DE)]).then_inc(attr_loaded, 16)
                sp.wait_ge(attr_loaded, q * 32 + 32)
                sp.sem_inc(sp_go, 1)
            turns(sp, load)
            sp.wait_ge(offs_stored, 16)

        @block.vector
        def _(v):
            step = Chain(v, dve_chain)
            step(v.memset(pad[:], 0.0))
            v.memset(pad[:, :, C_SLO:C_DLO + 1:2], PADLO).then_inc(pad_ready, 1)
            v.memset(ones[:], 1.0)
            v.memset(zeros[:], 0.0)
            v.memset(zerof[:], 0.0)
            v.memset(onesrow[:], 1.0)
            v.memset(aT[:], 1.0)
            v.tensor_copy(buckets[:], K.c("bucket"))
            v.tensor_copy(before[:], K.c("before"))
            step(v.tensor_copy(notbefore[:], K.c("notbefore")))
            v.sem_inc(zero_done, 1)
            v.wait_ge(idx_loaded, 32)
            v.tensor_scalar(shi_i[:], src_i[:], 10, None, ALU.logical_shift_right)
            step(v.tensor_scalar(dhi_i[:], dst_i[:], 10, None, ALU.logical_shift_right))
            step(v.scalar_tensor_tensor(key[:], shi_i[:], float(NG), dhi_i[:], ALU.mult, ALU.add))

            def hist(q, s, first):
                if not first:
                    v.wait_ge(hist_used, q - SLOTS + 1)
                iota = K.c("iota")[:, 0:NG].unsqueeze(1).to_broadcast([P, SUB, NG])
                for one, group in ((ohs, shi_i), (ohd, dhi_i)):
                    ins = v.tensor_tensor(one[:, s, :, :], group[:, bass.ds(q * SUB, SUB)].unsqueeze(2).to_broadcast(
                        [P, SUB, NG]), iota, ALU.is_equal)
                ins.then_inc(hist_ready, 1)
            turns(v, hist)
            v.wait_ge(hist_used, NSUB)

            v.tensor_scalar(shi_i[:], src_i[:], 7, HI - 1, ALU.logical_shift_right, ALU.bitwise_and)
            step(v.tensor_scalar(dhi_i[:], dst_i[:], 7, HI - 1, ALU.logical_shift_right, ALU.bitwise_and))
            v.tensor_scalar(src_i[:], src_i[:], P - 1, None, ALU.bitwise_and)
            step(v.tensor_scalar(dst_i[:], dst_i[:], P - 1, None, ALU.bitwise_and))
            v.wait_ge(vec_loaded, 16)
            square = rows[:].rearrange("p s t c -> p (s t c)")[:, 0:EPP]
            step(v.tensor_tensor(norm, vec[:, :, 0], vec[:, :, 0], ALU.mult))
            for c in (1, 2):
                step(v.tensor_tensor(square, vec[:, :, c], vec[:, :, c], ALU.mult))
                ins = v.tensor_tensor(norm, norm, square, ALU.add)
                step(ins)
            v.sem_inc(norm2_ready, 1)
            v.wait_ge(act_norm, 1)
            step(v.tensor_scalar(norm, norm, 1e-12, None, ALU.add))
            step(v.reciprocal(norm, norm))
            step(v.tensor_tensor(vec[:], vec[:], norm.unsqueeze(2).to_broadcast([P, EPP, 3]), ALU.mult))
            step(v.memset(rows[:], 0.0))
            step(v.memset(rows[:].rearrange("p s t c -> p (s t) c")[:, :, C_HA + DH:ROW:HW], 1.0))
            v.sem_inc(rowconst_ready, 1)

            for c in range(GRP):
                ins = v.tensor_tensor(counts[:, c, :].rearrange("p (s d) -> p s d", d=NG),
                                      hist_ps[0:NG, c * NG:(c + 1) * NG].unsqueeze(1).to_broadcast([NG, NG, NG]),
                                      K.c("ident")[0:NG, 0:NG].unsqueeze(2).to_broadcast([NG, NG, NG]), ALU.mult)
            step(ins)
            v.sem_inc(counts_ready, 1)
            v.wait_ge(spread_ready, 1)
            step(v.tensor_copy(start[:, 0, :], counter[0]))
            for c in range(1, GRP):
                step(v.tensor_tensor(start[:, 0, :], start[:, 0, :], counter[c], ALU.add))
            step(v.tensor_scalar(cnt_i[:], start[:, 0, :], float(PAIR * P - 1), None, ALU.add))
            step(v.tensor_scalar(cnt_i[:], cnt_i[:], 8, None, ALU.logical_shift_right))
            step(v.tensor_scalar(tiles[:], cnt_i[:], float(PAIR), None, ALU.mult))
            step(v.tensor_tensor_scan(end[:], tiles[:], zerof[:], 0.0, ALU.add, ALU.add))
            step(v.tensor_tensor(start[:, 0, :], end[:], tiles[:], ALU.subtract))
            step(v.tensor_scalar(start[:, 0, :], start[:, 0, :], float(P), None, ALU.mult))
            for c in range(1, GRP):
                step(v.tensor_tensor(start[:, c, :], start[:, c - 1, :], counter[c - 1], ALU.add))
            v.sem_inc(start_ready, 1)

            def rank(q, s, first):
                for k in range(SUB):
                    if k % GRP == 0 and not first:
                        v.wait_ge(rank_used, q * SUB + (k + GRP - SUB))
                    if k % GRP == 0 and first and s > 0:
                        v.wait_ge(rank_used, q * SUB + k + GRP - SUB)
                    ins = v.tensor_scalar(oh[:, k, :], buckets[:], key[:, bass.ds(q * SUB + k, 1)], None, ALU.is_equal)
                    ins.then_inc(oh_ready, 1)
                for k in range(SUB):
                    v.wait_ge(p_ready, q * SUB + k + 1)
                    v.scalar_tensor_tensor(junk[:, k % GRP, :], counter[k % GRP], 1.0, oh[:, k, 0:NBKT], ALU.mult, ALU.mult,
                                           accum_out=pos[:, k:k + 1]).then_inc(sel_done, 1)
                v.wait_ge(sel_done, q * SUB + SUB)
                v.tensor_copy(pos_i[:], pos[:]).then_inc(place_step, 1)
                v.wait_ge(place_step, q * 3 + 1)
                v.tensor_scalar(part_i[:], pos_i[:], P - 1, None, ALU.bitwise_and)
                v.tensor_scalar(tile_i[:], pos_i[:], 7, None, ALU.logical_shift_right).then_inc(place_step, 1)
                v.wait_ge(place_step, q * 3 + 2)
                if not first:
                    v.wait_ge(slot_free, q - SLOTS + 1)
                v.scalar_tensor_tensor(place[:, s, :], part_i[:], float(NT), tile_i[:], ALU.mult,
                                       ALU.add).then_inc(place_step, 1)
                v.wait_ge(place_step, q * 3 + 3)
                v.sem_inc(place_ready, 1)

            def tile_groups():
                for c in range(NCHUNK):
                    step(v.tensor_scalar(junk[:, 0, :], end[:], K.c("tau")[:, c:c + 1], None, ALU.is_le, ALU.add,
                                         accum_out=tb[:, 1, c:c + 1]))
                    ins = v.tensor_scalar(junk[:, 0, 0:NG], end[:, NG - 1:NBKT:NG], K.c("tau")[:, c:c + 1], None, ALU.is_le,
                                          ALU.add, accum_out=tb[:, 0, c:c + 1])
                    step(ins)
                step(v.tensor_scalar(tb[:, 1, :], tb[:, 1, :], float(NBKT - 1), None, ALU.min))
                step(v.tensor_scalar(tb[:, 0, :], tb[:, 0, :], float(NG - 1), None, ALU.min))
                step(v.scalar_tensor_tensor(tb[:, 1, :], tb[:, 0, :], -float(NG), tb[:, 1, :], ALU.mult, ALU.add))
                bank = junk[:, 0, 0:2 * NCHUNK].rearrange("p (k c) -> p k c", k=2)
                step(v.tensor_scalar(tb[:, 2:4, :], tb[:, 0:2, :], float(CW), None, ALU.mult))
                for first in range(CG, NG, CG):
                    step(v.tensor_scalar(bank, tb[:, 0:2, :], float(first), float(BANK - CG * CW), ALU.is_ge, ALU.mult))
                    step(v.tensor_tensor(tb[:, 2:4, :], tb[:, 2:4, :], bank, ALU.add))
                step(v.tensor_scalar(tb[:, 0:2, :], tb[:, 0:2, :], float(HI), None, ALU.mult))
                v.sem_inc(groups_ready, 1)
                v.wait_ge(offs_turned, 1)
                step(v.tensor_copy(offs[0:4 * NCHUNK, :], off_ps[0:4 * NCHUNK, 0:P]))
                v.sem_inc(offs_ready, 1)
            tile_groups()
            turns(v, rank)

        @block.scalar
        def _(act):
            act.wait_ge(norm2_ready, 1)
            nc.scalar.activation(norm, norm, ACT.Sqrt).then_inc(act_norm, 1)
            act.wait_ge(rowconst_ready, 1)

            def fill(q, s, first):
                if not first:
                    act.wait_ge(slot_free, q - SLOTS + 1)
                cols = bass.ds(q * SUB, SUB)
                for c, a in ((C_SLO, src_i), (C_SHI, shi_i), (C_DLO, dst_i), (C_DHI, dhi_i)):
                    nc.scalar.copy(rows[:, s, :, c], a[:, cols])
                nc.scalar.copy(rows[:, s, :, C_R:C_R + 3], vec[:, cols, :])
                act.wait_ge(attr_loaded, q * 32 + 32)
                nc.scalar.copy(rows[:, s, :, C_A8:C_A8 + DE],
                               a8[:, s, :].rearrange("p (t c) -> p t c", c=DE)).then_inc(a8_used, 1)
                for g in range(NGRP):
                    act.wait_ge(tp_ready, q * NGRP + g + 1)
                    nc.scalar.copy(aT[0:DH, :], tp_ps[0:DH, 0:GRP * P]).then_inc(aT_ready, 1)
                    act.wait_ge(h_ready, q * NGRP + g + 1)
                    nc.scalar.activation(
                        rows[:, s, g * GRP:(g + 1) * GRP, C_HA:ROW].rearrange("p t (n c) -> p t n c", n=2)[:, :, :, 0:DH],
                        h_ps[:, 0:GRP * 2 * DH].rearrange("p (t n c) -> p t n c", n=2, c=DH), ACT.Relu).then_inc(row_ready, 1)
            turns(act, fill)

        @block.tensor
        def _(pe):
            pe.wait_ge(zero_done, 1)
            pe.matmul(hist_ps[0:NG, :], zeros[:, 0:NG], zeros[:], start=True, stop=False, skip_group_check=True)

            def hist(q, s, first):
                pe.wait_ge(hist_ready, q + 1)
                for k in range(SUB):
                    c = k % GRP
                    ins = pe.matmul(hist_ps[0:NG, c * NG:(c + 1) * NG], ohs[:, s, k, :], ohd[:, s, k, :],
                                    start=False, stop=False, skip_group_check=True)
                ins.then_inc(hist_used, 1)
            turns(pe, hist)

            def clear_counters():
                for bank in range(GRP):
                    pe.matmul(count_ps[:, bank, :], ones[:], zeros[:], start=True, stop=False, skip_group_check=True)
            pe.wait_ge(counts_ready, 1)
            clear_counters()
            for c in range(GRP):
                ins = pe.matmul(counter[c], onesrow[:], counts[:, c, :], start=False, stop=False, skip_group_check=True)
            ins.then_inc(spread_ready, 1)
            pe.wait_ge(start_ready, 1)
            clear_counters()
            for c in range(GRP):
                pe.matmul(counter[c], onesrow[0:1, :], start[0:1, c, :], start=False, stop=False, skip_group_check=True)
            pe.wait_ge(groups_ready, 1)
            pe.transpose(off_ps[0:4 * NCHUNK, 0:P], tb[:].rearrange("p k c -> p (k c)"), K.c("ident")).then_inc(offs_turned, 1)
            pe.wait_ge(offs_ready, 1)
            pe.wait_ge(w_loaded, 64)

            def rank(q, s, first):
                for k in range(SUB + LAG):
                    if k < SUB:
                        if k % GRP == 0:
                            turn_attributes(q, s, k // GRP, first)
                        pe.wait_ge(oh_ready, q * SUB + k + 1)
                        pe.matmul(counter[k % GRP], before[:], oh[:, k, 0:NBKT], start=False, stop=False,
                                  skip_group_check=True).then_inc(p_ready, 1)
                        if k % GRP == 2:
                            hidden(q, s, k // GRP, first)
                    if k >= LAG:
                        pe.wait_ge(sel_done, q * SUB + k - LAG + 1)
                        pe.matmul(counter[(k - LAG) % GRP], notbefore[:], oh[:, k - LAG, 0:NBKT], start=False, stop=False,
                                  skip_group_check=True).then_inc(rank_used, 1)

            def turn_attributes(q, s, g, first):
                if g == 0:
                    pe.wait_ge(attr_loaded, q * 32 + 32)
                    pe.sem_inc(pe_go, 1)
                if not (first and s == 0 and g == 0):
                    pe.wait_ge(aT_ready, q * NGRP + g)
                    pe.sem_inc(pe_go, 1)
                for i in range(GRP):
                    k = g * GRP + i
                    ins = pe.transpose(tp_ps[0:DH, i * P:(i + 1) * P], attr[:, s, k * DH:(k + 1) * DH], K.c("ident"))
                ins.then_inc(tp_ready, 1)

            def hidden(q, s, g, first):
                pe.wait_ge(aT_ready, q * NGRP + g + 1)
                if not (first and s == 0 and g == 0):
                    pe.wait_ge(row_ready, q * NGRP + g)
                for i in range(GRP):
                    ins = pe.matmul(h_ps[:, i * 2 * DH:(i + 1) * 2 * DH], aT[:, i * P:(i + 1) * P], w1[:],
                                    start=True, stop=True)
                ins.then_inc(h_ready, 1)
            turns(pe, rank)

        @block.gpsimd
        def _(pool):
            pool.wait_ge(es_filled, NT // PADT * 16)

            def scatter(q, s, first):
                pool.wait_ge(row_ready, q * NGRP + NGRP)
                pool.sem_inc(pool_go, 1)
                pool.wait_ge(place_ready, q + 1)
                pool.sem_inc(pool_go, 1)
                for k in range(SUB):
                    pool.indirect_dma_start(K.rows_d, bass.IndirectOffsetOnAxis(place[:, s, k:k + 1], axis=0),
                                            rows[:, s, k, :], None).then_inc(scattered[s], 16)
                    if k == 5 and not (first and s < 1):
                        b = (s - 1) % SLOTS
                        landed(q, b)
                        pool.sem_inc(slot_free, 1)

            def landed(q, b):
                if isinstance(q, int):
                    pool.wait_ge(scattered[b], 16 * SUB * ((q - 1) // SLOTS + 1))
                else:
                    pool.wait_ge(scattered[b], count[b])

            for s in range(SLOTS):
                scatter(s, s, True)
            with pool.Fori(1, NSUB // SLOTS) as turn:
                count = [(turn + 1) * (16 * SUB)] * (SLOTS - 1) + [turn * (16 * SUB)]
                for s in range(SLOTS):
                    scatter(turn * SLOTS + s, s, False)
            for s in range(SLOTS):
                pool.wait_ge(scattered[s], NSUB // SLOTS * 16 * SUB)


def unpack_indices(K):
    nc = K.nc
    R = 4
    with ExitStack() as ctx:
        nat = K.sb("nat", [P, NT, 4], F32, ctx)
        turned = K.sb("turned", [P, R, P], BF16, ctx)
        stage = K.sb("stage", [P, R, 4, LOOP], BF16, ctx)
        ident = K.sb("ident", [P, P], BF16, ctx)
        turn_ps = K.ps(ctx, "turn_ps", [P, R, 1024], BF16)
        staged, ident_ready = K.sem("u_staged"), K.sem("u_ident_ready")
        nat_loaded = [K.sem(f"u_nat_loaded{c}") for c in range(4)]
        nat_stored, rows_stored = K.sem("u_nat_stored"), [K.sem(f"u_rows_stored{r}") for r in range(R)]
        turn_ready, copied, pe_go = K.sem("u_turn_ready"), K.sem("u_copied"), K.sem("u_pe_go")
        cut = [0, 3 * LOOP, 28 * LOOP, 60 * LOOP, NT]
        rows_v = K.rows_d.rearrange("(p t) c -> p t c", p=P)

        def turns(eng, body):
            whole = NTURN // R
            for r in range(R):
                body(r, r, True)
            with eng.Fori(1, whole) as n:
                for r in range(R):
                    body(n * R + r, r, False)
            for r in range(NTURN - whole * R):
                body(whole * R + r, r, False)

        block = ctx.enter_context(nc.Block())

        @block.sync
        def _(sp):
            for c in range(4):
                sp.dma_start(nat[:, cut[c]:cut[c + 1], :], rows_v[:, cut[c]:cut[c + 1], 0:4]).then_inc(nat_loaded[c], 16)
            for c in range(4):
                sp.wait_ge(nat_loaded[c], 16)
            sp.dma_start(K.nat_d, nat[:].rearrange("p t c -> p (t c)")).then_inc(nat_stored, 16)

            def store(q, r, first):
                sp.wait_ge(copied, q + 1)
                sp.dma_start(K.idxT_d[bass.ds(q, 1)].rearrange("o (k e) -> (o k) e", e=P), turned[:, r, :]).then_inc(rows_stored[r], 16)
            turns(sp, store)
            sp.wait_ge(nat_stored, 16)
            for r in range(R):
                sp.wait_ge(rows_stored[r], 16 * len(range(r, NTURN, R)))

        @block.tensor
        def _(pe):
            pe.wait_ge(ident_ready, 1)

            def turn(q, r, first):
                pe.wait_ge(staged, q + 1)
                if not first:
                    pe.wait_ge(copied, q - R + 1)
                    pe.sem_inc(pe_go, 1)
                pe.transpose(turn_ps[:, r, 0:P], stage[:, r, :, :].rearrange("p c t -> p (c t)"),
                             ident[:]).then_inc(turn_ready, 1)
            turns(pe, turn)

        @block.vector
        def _(v):
            v.tensor_copy(ident[:], K.c("ident")).then_inc(ident_ready, 1)
            for c in range(4):
                v.wait_ge(nat_loaded[c], 16)

            def put(q, r, first):
                if not first:
                    v.wait_ge(turn_ready, q - R + 1)
                v.tensor_copy(stage[:, r, :, :], nat[:, bass.ds(q * LOOP, LOOP), :].rearrange(
                    "p t c -> p c t")).then_inc(staged, 1)
            turns(v, put)

        @block.scalar
        def _(act):
            def copy(q, r, first):
                act.wait_ge(turn_ready, q + 1)
                if not first:
                    act.wait_ge(rows_stored[r], stored(q, r))
                nc.scalar.copy(turned[:, r, :], turn_ps[:, r, 0:P]).then_inc(copied, 1)

            def stored(q, r):
                return q // R * 16 if isinstance(q, int) else uses[0] * 16
            uses = [None]
            whole = NTURN // R
            for r in range(R):
                copy(r, r, True)
            with act.Fori(1, whole) as n:
                uses[0] = n
                for r in range(R):
                    copy(n * R + r, r, False)
            for r in range(NTURN - whole * R):
                copy(whole * R + r, r, False)


class Batch:

    def __init__(self, turn, k):
        at = 0 if turn is None else turn
        self.n, self.i, self.use = at * KB + k, at * NSL + k // KS, at + k // KB
        self.k = k % KB
        self.h, self.b = self.k // KS, self.k % KS
        self.first = turn is None and k < KB


def run_batches(eng, stages):
    n_batches = NTURN * KB

    def at(turn, m):
        for lag, stage in stages:
            if turn is not None or 0 <= m - lag < n_batches:
                stage(Batch(turn, m - lag))
    for m in range(KB):
        at(None, m)
    with eng.Fori(1, NTURN) as turn:
        for m in range(KB):
            at(turn, m)
    for m in range(n_batches, n_batches + max(lag for lag, _ in stages)):
        at(None, m)


def edge_pass(K, name, gather, scatter, kind, tables, acc_out, cnt_out=None):
    nc = K.nc
    last, gathers = kind in ("first", "second"), kind != "stored"
    turned_rows = kind == "product"
    G = 1 if last else 2
    RM, RO, RZ = 4, 4, 4
    NTAB = len(tables)
    WN = (F + NV) * F
    NQ = F if kind == "first" else F + NV
    NJ = WN // NQ
    HB = KB // 2
    SHORT = 3 * NV if kind == "stored" else F
    halves = kind in ("copy", "second")
    counts = cnt_out is not None
    WIDE = CW if counts else P
    NBANK = -(-NG // CG) if counts else -(-NW // BANK)
    has_rows = kind in ("product", "first", "second")
    NLOAD = {"copy": 2, "stored": 2}.get(kind, 3)
    with ExitStack() as ctx:
        def sb(n, shape, dt=F32):
            return K.sb(f"{name}_{n}", shape, dt, ctx)

        def sem(n):
            return K.sem(f"{name}_{n}")

        natb = sb("natb", [P, NSL, SB, 4])
        ohlo = sb("ohlo", [P, KB, BT, P])
        ohhi = sb("ohhi", [P, KB, BT, HI])
        outer = sb("outer", [P, RO, BT, WIDE])
        zero = sb("zero", [P, 512], BF16)
        if gathers:
            NIDX = 2 if turned_rows else 1
            idxb = sb("idxb", [P, NSL, NIDX, SB * P], BF16)
            ohg = sb("ohg", [P, KB, BT, HI])
            far = sb("far", [P, 2, BT, P])
            ohT = sb("ohT", [P, KB, BT * P], BF16 if turned_rows else F32)
            masked = sb("masked", [P, RM, NTAB, BT * P])
            msg = sb("msg", [P, RO, BT, NJ if last else F])
        else:
            msg = sb("msg", [P, NSL * KS, BT, 3 * NV])
        if has_rows:
            rows = sb("rows", [P, NSL, SB, ROW])
        if kind == "product":
            prod = sb("prod", [P, 2, BT, DE * F])
            tsum = sb("tsum", [P, RO, BT, F])
        if last:
            hT = sb("hT", [HW, RZ, BT * P])
            z = sb("z", [P, RZ, BT, NQ])
            zv = sb("zv", [P, BT, F])
            prod = sb("prod", [P, 2, BT, WN])
            vecs = sb("vecs", [P, 2, HB * BT, 3 * NV])
        acc = K.ps(ctx, f"{name}_acc", [P, NBANK * BANK])
        if gathers:
            gps = K.ps(ctx, f"{name}_gps", [P, G, 512])
        if last:
            turn_ps = K.ps(ctx, f"{name}_turn", [P, 512])
            w_ps = K.ps(ctx, f"{name}_w", [P, 2, 512])
        elif turned_rows:
            fold_ps = K.ps(ctx, f"{name}_fold", [P, 512])

        loaded = [sem(f"loaded{h}") for h in range(NSL)]
        zero_ready, sp_go, pe_go, flushed = sem("zero_ready"), sem("sp_go"), sem("pe_go"), sem("flushed")
        oh_ready, outers, scattered = sem("oh_ready"), sem("outers"), sem("scattered")
        if counts:
            beside = sem("beside")
        places = sem("places") if gathers else oh_ready
        if gathers:
            place_step = sem("place_step")
            gathered, masks, folded, messages = sem("gathered"), sem("masks"), sem("folded"), sem("messages")
        if has_rows:
            dve_step, pool_go = sem("dve_step"), sem("pool_go")
        if gathers:
            pool_step, fold_step, halved = sem("pool_step"), sem("fold_step"), sem("halved")
        if kind == "product":
            sums = sem("sums")
        if last:
            turned, hT_ready, weights, multiplied = sem("turned"), sem("hT_ready"), sem("weights"), sem("multiplied")
            contracted = [sem("contracted0"), sem("contracted1")]
        if kind == "first":
            vec_stored, vec_ready = [sem(f"vec_stored{u}") for u in range(2)], sem("vec_ready")
        used = {"copy": masks, "product": dve_step if has_rows else None}.get(kind, outers) if gathers else outers

        lead = {oh_ready: LEAD - 1, outers: LEAD - 1 + SLAG * KS, places: LEAD - 1 + SLAG * KS if gathers else LEAD - 1}
        if not gathers:
            lead = {}
        elif NTAB == 1:
            lead[masks] = LEAD - 1 + G
        if turned_rows:
            lead[dve_step] = LEAD + 1
        if last:
            lead[contracted[0]], lead[contracted[1]] = LEAD + 2, LEAD + 4

        def start(eng, *semaphores):
            for s in semaphores:
                eng.sem_inc(s, lead.get(s, LEAD))

        def done(eng, s, n):
            eng.wait_ge(s, n + lead.get(s, LEAD))

        block = ctx.enter_context(nc.Block())

        @block.sync
        def _(sp):
            def load(i, h, turn, first):
                if not first:
                    done(sp, used, (i - NSL + 1) * KS)
                    sp.sem_inc(sp_go, 1)
                    done(sp, places, (i - NSL + 1) * KS)
                    sp.sem_inc(sp_go, 1)
                sp.dma_start(natb[:, h, :, :].rearrange("p t c -> p (t c)"),
                             K.nat_d[:, bass.ds(i * (SB * 4), SB * 4)]).then_inc(loaded[h], 16)
                if gathers:
                    sp.dma_start(idxb[:, h, :, :], K.idxT_d[bass.ds(turn, 1), :].rearrange(
                        "o (k e) -> (o k) e", k=4)[2 * gather:2 * gather + NIDX, h * SB * P:(h + 1) * SB * P
                                                   ].partition_broadcast(P)).then_inc(loaded[h], 16)
                else:
                    sp.dma_start(msg[:, h * KS:(h + 1) * KS, :, :].rearrange("p b t c -> p (b t c)"),
                                 K.vec_d[:, bass.ds(i * (SB * 3 * NV), SB * 3 * NV)]).then_inc(loaded[h], 16)
                if has_rows:
                    sp.dma_start(rows[:, h, :, :].rearrange("p t c -> p (t c)"),
                                 K.rows_d.rearrange("(p t) c -> p (t c)", p=P)[:, bass.ds(i * (SB * ROW), SB * ROW)]
                                 ).then_inc(loaded[h], 16)

            def store(turn, u):
                sp.wait_ge(vec_ready, turn * 2 + u + 1)
                sp.dma_start(K.vec_d[:, bass.ds(turn * LOOP * 3 * NV + u * (HB * BT * 3 * NV), HB * BT * 3 * NV)],
                             vecs[:, u, :, :].rearrange("p t c -> p (t c)")).then_inc(vec_stored[u], 16)
            for h in range(NSL):
                load(h, h, 0, True)
            with sp.Fori(1, NTURN) as turn:
                for h in range(NSL):
                    load(turn * NSL + h, h, turn, False)
                    if kind == "first" and h % 2 == 1:
                        store(turn - 1, h // 2)
            if kind == "first":
                for u in range(2):
                    store(NTURN - 1, u)
                for u in range(2):
                    sp.wait_ge(vec_stored[u], 16 * NTURN)

        @block.tensor
        def _(pe):
            start(pe, scattered, *((gathered,) if gathers else ()), *((folded,) if turned_rows else ()),
                  *((turned, weights) if last else ()))
            pe.wait_ge(zero_ready, 1 if gathers else 2)
            for bank in range(NBANK):
                pe.matmul(acc[:, bank * BANK:(bank + 1) * BANK], zero[:, 0:P], zero[:], start=True, stop=False,
                          skip_group_check=True)
            regs = {}
            base = ((gather if gathers else 1 - scatter) + (2 if counts else 0)) * OFFP

            def offsets(entry, *sides):
                split = [[k] for k in range(len(sides))] if counts else [list(range(len(sides)))]
                for part in split:
                    first, end = sides[part[0]], sides[part[-1]] + 1
                    most = (NBANK - 1) * BANK + (NG - 1) % CG * CW if counts and first == 1 else NBLK - HI
                    vals = nc.values_load_multi_w_load_instructions(
                        K.offs[base:base + 1, bass.ds(entry, 1), first:end, :].rearrange("o i s k -> o (i s k)"),
                        engines=(mybir.EngineType.PE,), min_val=0, max_val=most,
                        skip_runtime_bounds_check_because="made on the chip, clamped")[1]
                    for n, k in enumerate(part):
                        regs["scatter" if sides[k] else "gather"] = vals[n * SPAIR:(n + 1) * SPAIR]

            def load_offsets(B):
                if B.b == 0:
                    early = isinstance(B.i, int) and B.i < SLAG
                    offsets(B.i, *((0,) if early else (0, 1)))

            def pair(B, side):
                n = BT // PAIR
                return regs[side][B.b * n:(B.b + 1) * n]

            def gather_blocks(B, tab):
                if tab == 0:
                    load_offsets(B)
                    done(pe, oh_ready, B.n + 1)
                done(pe, masks, B.n * NTAB + tab + 1 - G)
                pe.sem_inc(pe_go, 1)
                offs = pair(B, "gather")
                if turned_rows:
                    for t, off in enumerate(offs):
                        cols = slice(t * PAIR * P, (t + 1) * PAIR * P)
                        for part in range(3):
                            ins = pe.matmul(gps[:, B.k % G, cols], tables[tab][:, part, bass.ds(off * F, P)],
                                            ohT[:, B.k, cols], start=(part == 0), stop=(part == 2))
                else:
                    for t in range(BT):
                        cols = slice(t * P, (t + 1) * P)
                        ins = pe.matmul(gps[:, B.k % G, cols], ohT[:, B.k, cols],
                                        tables[tab][:, bass.ds(offs[t // PAIR] * F, P)], start=True, stop=True)
                ins.then_inc(gathered, 1)

            def turn_hidden(B):
                at = C_HA if kind == "first" else C_HB
                done(pe, hT_ready, B.n)
                pe.sem_inc(pe_go, 1)
                for t in range(BT):
                    ins = pe.transpose(turn_ps[0:HW, t * P:(t + 1) * P], rows[:, B.h, B.b * BT + t, at:at + HW],
                                       K.c("ident"))
                ins.then_inc(turned, 1)

            def fold(B):
                done(pe, masks, B.n + 1)
                done(pe, dve_step, B.n)
                for t in range(BT):
                    ins = pe.matmul(fold_ps[:, t * P:(t + 1) * P], masked[:, B.k % RM, 0, t * P:(t + 1) * P], K.w_msg[:],
                                    start=True, stop=True)
                ins.then_inc(folded, 1)

            def edge_weights(B, tiles):
                if 0 in tiles:
                    done(pe, hT_ready, B.n + 1)
                if 0 in tiles:
                    done(pe, contracted[1], B.n * 2)
                else:
                    done(pe, contracted[0], B.n * 2 + 2)
                for t in tiles:
                    pe.matmul(w_ps[:, t % 2, 0:WN], hT[:, B.k % RZ, t * P:(t + 1) * P],
                              K.w2[0 if kind == "first" else 1][:], start=True, stop=True).then_inc(weights, 1)

            def scatter_sums(B):
                late = isinstance(B.n, int) and B.n + SLAG * KS >= NTURN * KB
                if B.b == 0 and (late or not gathers):
                    offsets(B.i + SLAG, 1)
                done(pe, places, B.n + 1)
                done(pe, outers, B.n + 1)
                pe.sem_inc(pe_go, 1)
                offs = pair(B, "scatter")
                for t in range(BT):
                    at = offs[t // PAIR] if counts else offs[t // PAIR] * F
                    ins = pe.matmul(acc[:, bass.ds(at, WIDE)], ohlo[:, B.k, t, :], outer[:, B.k % RO, t, :],
                                    start=False, stop=False, skip_group_check=True)
                ins.then_inc(scattered, 1)

            if not gathers:
                stages = [(0, scatter_sums)]
            else:
                stages = [(0, lambda B: gather_blocks(B, 0))]
                if last:
                    stages.append((0, turn_hidden))
                if turned_rows:
                    stages.append((1, fold))
                if last:
                    stages.append((2, lambda B: edge_weights(B, range(0, 2))))
                if NTAB == 2:
                    stages.append((0, lambda B: gather_blocks(B, 1)))
                else:
                    stages.append((SLAG * KS, scatter_sums))
                if last:
                    stages.append((2, lambda B: edge_weights(B, range(2, BT))))
                if NTAB == 2:
                    stages.append((SLAG * KS, scatter_sums))
            run_batches(pe, stages)

        @block.vector
        def _(v):
            start(v, oh_ready, *((masks,) if gathers else ()), *((dve_step,) if turned_rows else ()),
                  *((multiplied, *contracted) if last else ()), *((halved,) if gathers and not turned_rows else ()))
            if not gathers:
                v.memset(outer[:], 0.0).then_inc(zero_ready, 1)
                v.wait_ge(zero_ready, 1)
            v.memset(zero[:], 0.0).then_inc(zero_ready, 1)
            v.wait_ge(zero_ready, 1 if gathers else 2)

            def one_hots(B):
                done(v, scattered, B.n - KB + 1)
                if B.b == 0:
                    v.wait_ge(loaded[B.h], B.use * (16 * NLOAD) + 16 * NLOAD)
                tiles = slice(B.b * BT, (B.b + 1) * BT)
                ins = v.tensor_tensor(ohhi[:, B.k, :, :], natb[:, B.h, tiles, 2 * scatter + 1].unsqueeze(2).to_broadcast(
                    [P, BT, HI]), K.c("iota8").unsqueeze(1).to_broadcast([P, BT, HI]), ALU.is_equal)
                if gathers:
                    if not turned_rows:
                        v.tensor_tensor(ohg[:, B.k, :, :], natb[:, B.h, tiles, 2 * gather + 1].unsqueeze(2).to_broadcast(
                            [P, BT, HI]), K.c("iota8").unsqueeze(1).to_broadcast([P, BT, HI]), ALU.is_equal)
                    ins = v.tensor_scalar(ohT[:, B.k, :], idxb[:, B.h, 0, B.b * BT * P:(B.b + 1) * BT * P], K.c("lo"), None,
                                          ALU.is_equal)
                else:
                    for t in range(BT):
                        ins = v.tensor_scalar(ohlo[:, B.k, t, :], K.c("iota"),
                                              natb[:, B.h, B.b * BT + t, 2 * scatter:2 * scatter + 1], None, ALU.is_equal)
                ins.then_inc(oh_ready, 1)

            def mask(B, tab):
                done(v, gathered, B.n * NTAB + tab + 1)
                done(v, folded, B.n - RM + 1)
                if turned_rows:
                    ins = v.scalar_tensor_tensor(masked[:, B.k % RM, tab, :],
                                                 idxb[:, B.h, NIDX - 1, B.b * BT * P:(B.b + 1) * BT * P], K.c("blk"),
                                                 gps[:, B.k % G, :], ALU.is_equal, ALU.mult)
                else:
                    ins = v.tensor_tensor(masked[:, B.k % RM, tab, :].rearrange("p (b f) -> p b f", f=F),
                                          gps[:, B.k % G, :].rearrange("p (b f) -> p b f", f=F),
                                          ohg[:, B.k, :, :].rearrange("p t a -> p (t a)").unsqueeze(2).to_broadcast(
                                              [P, BT * HI, F]), ALU.mult)
                ins.then_inc(masks, 1)

            def half_blocks(B, tab):
                done(v, masks, B.n * NTAB + tab + 1)
                b = masked[:, B.k % RM, tab, :].rearrange("p (t b f) -> p t b f", b=HI, f=F)
                v.tensor_tensor(b[:, :, 0:4, :], b[:, :, 0:4, :], b[:, :, 4:8, :], ALU.add).then_inc(halved, 1)

            def product(B):
                done(v, folded, B.n + 1)
                done(v, sums, B.n - 1)
                a8 = rows[:, B.h, B.b * BT:(B.b + 1) * BT, C_A8:C_A8 + DE]
                v.tensor_tensor(prod[:, B.k % 2, :, :].rearrange("p t (j f) -> p t j f", j=DE),
                                fold_ps[:].rearrange("p (t j f) -> p t j f", t=BT, j=DE),
                                a8.unsqueeze(3).to_broadcast([P, BT, DE, F]), ALU.mult).then_inc(dve_step, 1)

            def contract(B):
                done(v, folded, B.n + 1)
                done(v, weights, B.n * BT + 1)
                done(v, messages, B.n - 1)
                multiply(B, range(0, 2))

            def multiply(B, tiles):
                a = prod[:, B.k % 2, :, :].rearrange("p t (q j) -> p t q j", j=NJ)
                for t in tiles:
                    if t > 0:
                        done(v, weights, B.n * BT + t + 1)
                    v.tensor_tensor(a[:, t, :, :], w_ps[:, t % 2, 0:WN].rearrange("p (q j) -> p q j", j=NJ),
                                    z[:, B.k % RZ, t, :].unsqueeze(2).to_broadcast([P, NQ, NJ]), ALU.mult
                                    ).then_inc(contracted[t // (BT // 2)], 1)

            def contract_rest(B):
                multiply(B, range(2, BT))
                for half in range(2):
                    done(v, contracted[half], B.n * 2 + 2)
                a = prod[:, B.k % 2, :, :].rearrange("p t (q j) -> p t q j", j=NJ)
                half = NQ // 2
                v.tensor_tensor(a[:, :, 0:half, :], a[:, :, 0:half, :], a[:, :, half:NQ, :], ALU.add).then_inc(multiplied, 1)

            stages = [(KS, lambda B: mask(B, 0))] if gathers else []
            if last:
                stages.append((KS + 2, contract))
            stages.append((0, one_hots))
            if halves:
                stages.append((KS, lambda B: half_blocks(B, 0)))
            if NTAB == 2:
                stages.append((KS, lambda B: mask(B, 1)))
            if last:
                stages.append((KS + 2, contract_rest))
            if NTAB == 2:
                stages.append((KS, lambda B: half_blocks(B, 1)))
            if kind == "product":
                stages.append((KS + 1, product))
            run_batches(v, stages)
            done(v, scattered, NTURN * KB)
            if counts:
                for bank in range(NBANK):
                    first, n = bank * CG, min(CG, NG - bank * CG)
                    sums_in = acc[:, bank * BANK:bank * BANK + n * CW].rearrange("p (g c) -> p g c", c=CW)
                    v.tensor_copy(acc_out[:, first * P:(first + n) * P].rearrange("p (g c) -> p g c", c=P),
                                  sums_in[:, :, 0:P]).then_inc(flushed, 1)
                    v.tensor_copy(cnt_out[:, first * HI:(first + n) * HI].rearrange("p (g c) -> p g c", c=HI),
                                  sums_in[:, :, P:CW]).then_inc(flushed, 1)
            else:
                v.tensor_copy(acc_out[:], acc[:, 0:NW]).then_inc(flushed, 1)

        @block.scalar
        def _(act):
            if not gathers:
                return
            start(act, places, place_step, *((hT_ready,) if last else (messages,) if turned_rows else ()))

            def measure(B):
                if B.b == 0:
                    act.wait_ge(loaded[B.h], B.use * (16 * NLOAD) + 16 * NLOAD)
                done(act, places, B.n - 1)
                for t in range(BT):
                    ins = nc.scalar.activation(far[:, B.k % 2, t, :], K.c("iota"), ACT.Abs, scale=-1.0,
                                               bias=natb[:, B.h, B.b * BT + t, 2 * scatter:2 * scatter + 1])
                ins.then_inc(place_step, 1)

            def make_places(B):
                done(act, place_step, B.n + 1)
                done(act, scattered, B.n - KB + 1)
                nc.scalar.activation(ohlo[:, B.k, :, :], far[:, B.k % 2, :, :], ACT.Relu, scale=-1.0,
                                     bias=K.c("one")).then_inc(places, 1)

            def take_hidden(B):
                done(act, turned, B.n + 1)
                done(act, weights, (B.n - RZ + 1) * BT)
                nc.scalar.copy(hT[:, B.k % RZ, :], turn_ps[0:HW, :]).then_inc(hT_ready, 1)

            def message(B):
                done(act, outers, B.n - RO + 1)
                done(act, sums, B.n + 1)
                nc.scalar.activation(msg[:, B.k % RO, :, :], tsum[:, B.k % RO, :, :], ACT.Silu,
                                     scale=float(1.0 / np.sqrt(F * DE))).then_inc(messages, 1)
            run_batches(act, ([(KS, take_hidden)] if last else [(KS + 1, message)] if turned_rows else []) + [
                (0, measure), (1, make_places)])

        @block.gpsimd
        def _(pool):
            start(pool, outers, *((messages, folded) if last else (sums,) if turned_rows else (folded, messages) if gathers else ()),
                  *((pool_step, fold_step) if gathers else ()), *((beside,) if counts else ()))
            if not gathers:
                pool.wait_ge(zero_ready, 1)

            def add(out, a, b):
                return nc.gpsimd.tensor_tensor(out, a, b, ALU.add)

            def fold_blocks(B, k):
                steps = {"copy": 1, "first": 2, "second": 6}[kind]
                blocks = masked[:, B.k % RM, :, :].rearrange("p n (t b f) -> p n t b f", b=HI, f=F)
                tab = 0 if kind != "second" or k in (0, 2) else 1
                b = blocks[:, tab]
                if k == 0 and last:
                    done(pool, multiplied, B.n - RZ + 1)

                def step(ins):
                    ins.then_inc(fold_step, 1)

                def after(n):
                    done(pool, fold_step, B.n * steps + n)

                def level(q):
                    return add(b[:, :, 0:q, :], b[:, :, 0:q, :], b[:, :, q:2 * q, :])

                if kind == "copy":
                    if k == 0:
                        done(pool, halved, B.n + 1)
                        step(level(2))
                    else:
                        after(1)
                        add(msg[:, B.k % RO, :, :], b[:, :, 0, :], b[:, :, 1, :]).then_inc(messages, 1)
                        done(pool, messages, B.n + 1)
                        pool.sem_inc(folded, 1)
                    return
                if kind == "first":
                    if k == 0:
                        done(pool, masks, B.n + 1)
                        step(level(4))
                    elif k == 1:
                        after(1)
                        step(level(2))
                    else:
                        after(2)
                        add(z[:, B.k % RZ, :, :], b[:, :, 0, :], b[:, :, 1, :]).then_inc(folded, 1)
                    return
                v3 = zv[:, :, 0:3 * NV].rearrange("p t (j c) -> p t j c", c=3)
                if k < 2:
                    done(pool, halved, B.n * NTAB + tab + 1)
                    step(level(2))
                elif k == 2:
                    after(1)
                    step(add(z[:, B.k % RZ, :, 0:F], b[:, :, 0, :], b[:, :, 1, :]))
                elif k == 3:
                    after(2)
                    step(add(zv[:], b[:, :, 0, :], b[:, :, 1, :]))
                elif k == 4:
                    after(4)
                    r = rows[:, B.h, B.b * BT:(B.b + 1) * BT, C_R:C_R + 3].unsqueeze(2).to_broadcast([P, BT, NV, 3])
                    step(nc.gpsimd.tensor_tensor(v3, v3, r, ALU.mult))
                elif k == 5:
                    after(5)
                    step(add(v3[:, :, :, 0], v3[:, :, :, 0], v3[:, :, :, 1]))
                else:
                    after(6)
                    add(z[:, B.k % RZ, :, F:F + NV], v3[:, :, :, 0], v3[:, :, :, 2]).then_inc(folded, 1)

            def rest_of_sum(B, k):
                steps = {"product": 2, "first": 3, "second": 3}[kind]
                a = prod[:, B.k % 2, :, :].rearrange("p t (q j) -> p t q j", j=F if kind == "product" else NJ)
                out = tsum[:, B.k % RO, :, :] if kind == "product" else msg[:, B.k % RO, :, :]

                def step(ins):
                    ins.then_inc(pool_step, 1)

                def level(q):
                    return add(a[:, :, 0:q, :], a[:, :, 0:q, :], a[:, :, q:2 * q, :])

                if k > 0 and k < 3:
                    done(pool, pool_step, B.n * steps + k)
                if k == 0 and kind == "product":
                    done(pool, dve_step, B.n + 1)
                    done(pool, messages, B.n - RO + 1)
                    step(level(4))
                elif k == 0:
                    done(pool, multiplied, B.n + 1)
                    step(level(4 if kind == "first" else 5))
                elif k == 1 and kind == "second":
                    step(add(a[:, :, 0, :], a[:, :, 0, :], a[:, :, 4, :]))
                elif k == 1 or k == 2 and kind == "second":
                    step(level(2))
                elif k == 2 or kind == "second":
                    if kind == "second":
                        done(pool, pool_step, B.n * steps + 3)
                    add(out, a[:, :, 0, :], a[:, :, 1, :]).then_inc(sums if kind == "product" else messages, 1)
                else:
                    store_vectors(B)

            def store_vectors(B):
                u = B.k // HB
                done(pool, messages, B.n + 1)
                if B.k % HB == 0 and not B.first:
                    pool.wait_ge(vec_stored[u], B.use * 16)
                    pool.sem_inc(pool_go, 1)
                r = rows[:, B.h, B.b * BT:(B.b + 1) * BT, C_R:C_R + 3].unsqueeze(2).to_broadcast([P, BT, NV, 3])
                nc.gpsimd.tensor_tensor(
                    vecs[:, u, B.k % HB * BT:(B.k % HB + 1) * BT, :].rearrange("p t (j c) -> p t j c", c=3),
                    msg[:, B.k % RO, :, F:F + NV].unsqueeze(3).to_broadcast([P, BT, NV, 3]), r, ALU.mult).then_inc(pool_step, 1)
                done(pool, pool_step, B.n * 3 + 3)
                if B.k % HB == HB - 1:
                    pool.sem_inc(vec_ready, 1)

            def spread(B):
                done(pool, messages if gathers else oh_ready, B.n + 1)
                done(pool, scattered, B.n - RO + 1)
                m = msg[:, B.k % RO if gathers else B.k, :, 0:SHORT]
                o = outer[:, B.k % RO, :, :]
                if counts:
                    nc.gpsimd.tensor_tensor(o[:, :, P:CW], ohhi[:, B.k, :, :], ohhi[:, B.k, :, :], ALU.mult
                                            ).then_inc(beside, 1)
                    done(pool, beside, B.n + 1)
                nc.gpsimd.tensor_tensor(
                    o[:, :, 0:P].rearrange("p t (a f) -> p t a f", f=F)[:, :, :, 0:SHORT],
                    ohhi[:, B.k, :, :].unsqueeze(3).to_broadcast([P, BT, HI, SHORT]),
                    m.unsqueeze(2).to_broadcast([P, BT, HI, SHORT]), ALU.mult).then_inc(outers, 1)

            def folds(*ks):
                return [(0, lambda B, k=k: fold_blocks(B, k)) for k in ks]

            def sums_left(lag, *ks):
                return [(lag, lambda B, k=k: rest_of_sum(B, k)) for k in ks]
            if kind == "product":
                run_batches(pool, sums_left(0, 0) + [(1, spread)] + sums_left(0, 1, 2))
            elif kind == "first":
                run_batches(pool, sums_left(2, 0) + folds(0) + sums_left(2, 1) + folds(1) + sums_left(2, 2) + folds(2) +
                            sums_left(2, 3) + [(2, spread)])
            elif kind == "second":
                run_batches(pool, folds(0, 1) + sums_left(2, 0) + folds(2, 3) + sums_left(2, 1) + folds(4) + sums_left(2, 2) +
                            folds(5) + sums_left(2, 3) + folds(6) + [(2, spread)])
            elif kind == "copy":
                run_batches(pool, folds(0) + [(1, spread)] + folds(1))
            else:
                run_batches(pool, [(0, spread)])


BDS = ["L0_gnn_W_msg_lin", "L0_gnn_W_upd_lin", "L1_gnn_w1a", "L1_gnn_w1b", "L1_gnn_w2a", "L1_gnn_w2b", "L2_gnn_W"]
VECS = ["L1_gnn_b1a", "L1_gnn_b1b", "L1_gnn_b2a", "L1_gnn_b2b", "L2_gnn_b", "L3_gnn_bn0_gs", "L3_gnn_bn0_bs",
        "L3_gnn_bn1_gs", "L3_gnn_bn1_bs", "L3_gnn_bn0_gv", "L1_gnn_eps1", "L1_gnn_eps2"]
EPS = 1e-5


def setup_nodes(K):
    nc = K.nc
    K.x = K.sb("x", [P, NBLK, F])
    K.acc = K.sb("acc", [P, NW])
    K.keep = K.sb("keep", [P, NBLK, F])
    K.src_count = K.sb("src_count", [P, NBLK])
    K.dst_count = K.sb("dst_count", [P, NBLK])
    K.tab = K.sb("tab", [P, 3, NW], BF16)
    K.vectors = K.sb("vectors", [P, NBLK, F])
    K.bd = K.sb("bd", [P, len(BDS), P])
    K.vecs = K.sb("vecs", [P, len(VECS), F])
    K.w_msg = K.sb("w_msg", [P, DE * F])
    K.w_upd = K.sb("w_upd", [P, HI, F * F])
    K.offs = K.sb("offs_rows", [3 * OFFP + 1, NSB + SLAG, 2, SPAIR], I32)
    K.w2 = [K.sb(f"w2_{n}", [HW, (F + NV) * F]) for n in range(2)]
    cleared, loaded, loaded2 = K.sem("n_cleared"), K.sem("n_loaded"), K.sem("n_loaded2")
    whole = N_NODES // P
    jobs = []
    for w, n in enumerate(BDS):
        jobs += [(K.bd[F * k:F * k + F, w, F * k:F * k + F], K.ins[n]) for k in range(HI)]
    for k in range(HI):
        jobs.append((K.w_msg[F * k:F * k + F, :], K.ins["L0_gnn_W_msg_tp"].rearrange("i j h -> i (j h)")))
        jobs.append((K.w_upd[F * k:F * k + F, k, :], K.ins["L0_gnn_W_upd_tp"].rearrange("i h k -> i (h k)")))
    for w, n in enumerate(VECS):
        a = K.ins[n]
        jobs.append((K.vecs[:, w, 0:a.shape[0]], a.partition_broadcast(P)))
    w0 = K.w2[0][:].rearrange("k (i j) -> k i j", j=F + NV)
    for rows, src in ((slice(0, DH), K.ins["L3_gnn_fc0_w2"]), (slice(DH, HW), K.ins["L3_gnn_fc0_b2"].rearrange("(a d) -> a d", a=1))):
        jobs.append((w0[rows, :, 0:F], src[:, 0:F * F].rearrange("k (i j) -> k i j", j=F)))
        jobs.append((w0[rows, :, F:F + NV], src[:, F * F:].rearrange("k (i j) -> k i j", j=NV)))
    jobs.append((K.w2[1][0:DH, :], K.ins["L3_gnn_fc1_w2"]))
    jobs.append((K.w2[1][DH:HW, :], K.ins["L3_gnn_fc1_b2"].rearrange("(a d) -> a d", a=1)))
    for side in (SRC, DST):
        pairs = K.offs_d[side:side + 1, 0:NPAIR].rearrange("o (i k) -> o i k", k=SPAIR)
        counted = K.offs_d[2 + side:3 + side, 0:NPAIR].rearrange("o (i k) -> o i k", k=SPAIR)
        for kind, target in ((0, pairs), (2, counted)):
            at, other = (kind + side) * OFFP, (kind + 1 - side) * OFFP
            jobs.append((K.offs[at:at + 1, 0:NSB, 0, :], pairs))
            jobs.append((K.offs[other:other + 1, SLAG:NSB + SLAG, 1, :], target))
    jobs.append((K.x[:, 0:whole, :], K.ins["x"][0:whole * P].rearrange("(b p) f -> p b f", p=P)))
    jobs.append((K.x[0:N_NODES - whole * P, whole, :], K.ins["x"][whole * P:N_NODES]))
    with nc.Block() as block:
        @block.vector
        def _(v):
            v.memset(K.bd[:], 0.0)
            v.memset(K.w_upd[:], 0.0)
            v.memset(K.vecs[:], 0.0)
            v.memset(K.x[:], 0.0).then_inc(cleared, 1)

        @block.sync
        def _(sp):
            sp.wait_ge(cleared, 1)
            for dst, src in jobs[0::2]:
                sp.dma_start(dst, src).then_inc(loaded, 16)
            sp.wait_ge(loaded, 16 * len(jobs[0::2]))

        @block.scalar
        def _(act):
            act.wait_ge(cleared, 1)
            for dst, src in jobs[1::2]:
                act.dma_start(dst, src).then_inc(loaded2, 16)
            act.wait_ge(loaded2, 16 * len(jobs[1::2]))


class Nodes:

    def __init__(self, K, name, linears=(), functions=(), totals=0):
        self.K, self.nc, self.name = K, K.nc, name
        self.linears, self.functions, self.totals = linears, functions, totals
        self.ctx = ExitStack()

    def __enter__(self):
        K, n, ctx = self.K, self.name, self.ctx
        self.y = K.sb(f"{n}_y", [P, NBLK, F], F32, ctx)
        self.sq = K.sb(f"{n}_sq", [P, NBLK, F], F32, ctx)
        self.s = K.sb(f"{n}_s", [P, NBLK], F32, ctx)
        self.r = K.sb(f"{n}_r", [P, NBLK], F32, ctx)
        self.part = K.sb(f"{n}_part", [P, F], F32, ctx)
        self.stat = K.sb(f"{n}_stat", [P, 4, F], F32, ctx)
        self.xT = K.sb(f"{n}_xT", [P, NW], F32, ctx)
        self.ones = K.sb(f"{n}_ones", [P, P], F32, ctx)
        self.turn_ps = K.ps(ctx, f"{n}_turn_ps", [P, 4 * 512])
        self.lin_ps = K.ps(ctx, f"{n}_lin_ps", [P, 4 * 512])
        self.dve = K.sem(f"{n}_dve")
        self.lin_in, self.lin_out = K.sem(f"{n}_lin_in"), K.sem(f"{n}_lin_out")
        self.turned, self.taken = K.sem(f"{n}_turned"), K.sem(f"{n}_taken")
        self.func_in, self.func_out = K.sem(f"{n}_func_in"), K.sem(f"{n}_func_out")
        self.tot_in, self.tot_out = K.sem(f"{n}_tot_in"), K.sem(f"{n}_tot_out")
        self.n_lin = self.n_func = self.n_tot = 0
        self.block = ctx.enter_context(self.nc.Block())
        return self

    def __exit__(self, *e):
        return self.ctx.__exit__(*e)

    def linear(self):
        self.n_lin += 1
        self.v.sem_inc(self.lin_in, 1)
        self.v.wait_ge(self.lin_out, self.n_lin)
        return self.lin_ps[:, 0:NW].rearrange("p (b f) -> p b f", f=F)

    def function(self):
        self.n_func += 1
        self.v.sem_inc(self.func_in, 1)
        self.v.wait_ge(self.func_out, self.n_func)

    def total(self):
        self.n_tot += 1
        self.v.sem_inc(self.tot_in, 1)
        self.v.wait_ge(self.tot_out, self.n_tot)
        return self.lin_ps[:, 0:F]

    def start_vector(self, v):
        self.v, self.step = v, Chain(v, self.dve)
        self.step(v.memset(self.ones[:], 1.0))

    def vec(self, name, n=F):
        return self.K.vecs[:, VECS.index(name), 0:n]

    def row(self, name):
        return self.vec(name).unsqueeze(1).to_broadcast([P, NBLK, F])

    def each(self, a):
        return a[:].unsqueeze(2).to_broadcast([P, NBLK, F])

    def split(self, tab, a):
        v, step, flat = self.v, self.step, a.rearrange("p b f -> p (b f)")
        rest = self.sq[:].rearrange("p b f -> p (b f)")
        step(v.tensor_copy(tab[:, 0, :], flat))
        step(v.tensor_tensor(rest, flat, tab[:, 0, :], ALU.subtract))
        step(v.tensor_copy(tab[:, 1, :], rest))
        step(v.tensor_tensor(rest, rest, tab[:, 1, :], ALU.subtract))
        step(v.tensor_copy(tab[:, 2, :], rest))

    def layernorm(self, out):
        v, step = self.v, self.step
        step(v.tensor_reduce(self.s[:], self.y[:], AX.X, ALU.add))
        step(v.tensor_scalar(self.s[:], self.s[:], 1.0 / F, None, ALU.mult))
        step(v.tensor_tensor(self.y[:], self.y[:], self.each(self.s), ALU.subtract))
        step(v.tensor_tensor(self.sq[:], self.y[:], self.y[:], ALU.mult))
        step(v.tensor_reduce(self.r[:], self.sq[:], AX.X, ALU.add))
        step(v.tensor_scalar(self.r[:], self.r[:], 1.0 / F, EPS, ALU.mult, ALU.add))
        self.function()
        step(v.reciprocal(self.r[:], self.r[:]))
        step(v.tensor_tensor(out, self.y[:], self.each(self.r), ALU.mult))

    def run_tensor(self, pe):
        K = self.K
        for k, (src, w) in enumerate(self.linears):
            pe.wait_ge(self.lin_in, k + 1)
            flat = src.rearrange("p b f -> p (b f)")
            for g in range(NG):
                ins = pe.transpose(self.turn_ps[:, g * P:(g + 1) * P], flat[:, g * P:(g + 1) * P], K.c("ident"))
            ins.then_inc(self.turned, 1)
            pe.wait_ge(self.taken, k + 1)
            if w is None:
                self.update_products(pe)
                continue
            for g in range(NG):
                ins = pe.matmul(self.lin_ps[:, g * P:(g + 1) * P], self.xT[:, g * P:(g + 1) * P], K.bd[:, BDS.index(w), :],
                                start=True, stop=True)
            ins.then_inc(self.lin_out, 1)
        for k in range(self.totals):
            pe.wait_ge(self.tot_in, k + 1)
            pe.matmul(self.lin_ps[:, 0:F], self.ones[:], self.part[:], start=True, stop=True).then_inc(self.tot_out, 1)

    def run_scalar(self, act):
        lin = func = 0
        for f in self.functions:
            if f is None:
                lin += 1
                act.wait_ge(self.turned, lin)
                self.nc.scalar.copy(self.xT[:], self.turn_ps[:, 0:NW]).then_inc(self.taken, 1)
            else:
                func += 1
                act.wait_ge(self.func_in, func)
                out, in_, name, scale = f
                self.nc.scalar.activation(out, in_, name, scale=scale).then_inc(self.func_out, 1)

    def engines(self, lead):
        @self.block.vector
        def _(v):
            self.start_vector(v)
            lead(v)

        @self.block.tensor
        def _(pe):
            pe.wait_ge(self.dve, 1)
            self.run_tensor(pe)

        @self.block.scalar
        def _(act):
            self.run_scalar(act)


def sqrt_r(N):
    return (N.r[:], N.r[:], ACT.Sqrt, 1.0)


def acc_nodes(K):
    return K.acc[:].rearrange("p (b f) -> p b f", f=F)


def first_table(K):
    with Nodes(K, "n0") as N:
        N.engines(lambda v: N.split(K.tab, K.x[:]))


def update_first(K):
    lin_norm, upd_norm = 1.0 / np.sqrt(F), 1.0 / np.sqrt(F * F)
    with Nodes(K, "n1") as N:
        agg = K.sb("n1_agg", [P, NBLK, F], F32, N.ctx)
        prod = K.sb("n1_prod", [P, 4, F, F], F32, N.ctx)
        upd_ready, upd_used = K.sem("n1_upd_ready"), K.sem("n1_upd_used")
        half = HI // 2

        def bank(n):
            return N.lin_ps[:, n % 2 * 1024:n % 2 * 1024 + half * F * F]

        def update_products(pe):
            for n in range(2 * NG):
                if n >= 2:
                    pe.wait_ge(upd_used, n - 1)
                for k in range(half):
                    ins = pe.matmul(bank(n)[:, k * F * F:(k + 1) * F * F], N.xT[:, n // 2 * P:(n // 2 + 1) * P],
                                    K.w_upd[:, n % 2 * half + k, :], start=True, stop=True)
                ins.then_inc(upd_ready, 1)
        N.update_products = update_products
        N.linears = [(acc_nodes(K), "L0_gnn_W_msg_lin"), (K.x[:], None), (N.y[:], "L0_gnn_W_upd_lin")]
        N.functions = [None, None, (N.y[:], N.y[:], ACT.Silu, float(lin_norm * upd_norm)), None, sqrt_r(N)]

        def lead(v):
            step = N.step
            step(v.tensor_copy(agg[:], N.linear()))
            N.n_lin += 1
            v.sem_inc(N.lin_in, 1)
            for n in range(2 * NG):
                v.wait_ge(upd_ready, n + 1)
                blocks = slice(n * half, (n + 1) * half)
                v.tensor_tensor(prod[:], bank(n).rearrange("p (b h k) -> p b h k", h=F, k=F),
                                agg[:, blocks, :].unsqueeze(3).to_broadcast([P, half, F, F]), ALU.mult).then_inc(upd_used, 1)
                v.wait_ge(upd_used, n + 1)
                step(v.tensor_reduce(N.y[:, blocks, :], prod[:].rearrange("p b h k -> p b k h"), AX.X, ALU.add))
            N.n_lin -= 1
            N.function()
            u = N.linear()
            step(v.scalar_tensor_tensor(N.y[:], K.x[:], 2.0 / lin_norm, u, ALU.mult, ALU.add))
            step(v.tensor_scalar(N.y[:], N.y[:], float(lin_norm), None, ALU.mult))
            N.layernorm(K.x[:])
        N.engines(lead)


def gin(K, N, v, x, eps, wa, wb):
    step = N.step
    step(v.tensor_scalar(N.s[:, 0:1], N.vec(eps, 1), 1.0, None, ALU.add))
    flat = x.rearrange("p b f -> p (b f)")
    step(v.scalar_tensor_tensor(N.y[:].rearrange("p b f -> p (b f)"), flat, N.s[:, 0:1], K.acc[:], ALU.mult, ALU.add))
    step(v.tensor_tensor(N.y[:], N.linear(), N.row(wa), ALU.add))
    step(v.tensor_scalar(N.y[:], N.y[:], 0.0, None, ALU.max))
    step(v.tensor_tensor(N.y[:], N.linear(), N.row(wb), ALU.add))


def gin_first(K):
    with Nodes(K, "n2") as N:
        N.linears = [(N.y[:], "L1_gnn_w1a"), (N.y[:], "L1_gnn_w1b")]
        N.functions = [None, None]

        def lead(v):
            gin(K, N, v, K.x[:], "L1_gnn_eps1", "L1_gnn_b1a", "L1_gnn_b1b")
            N.step(v.tensor_scalar(K.keep[:], N.y[:], 0.0, None, ALU.max))
        N.engines(lead)


def gin_second(K):
    with Nodes(K, "n3") as N:
        dinv = K.dst_count
        N.linears = [(N.y[:], "L1_gnn_w2a"), (N.y[:], "L1_gnn_w2b"), (K.x[:], "L2_gnn_W")]
        N.functions = [None, None, (N.sq[:], N.y[:], ACT.Exp, 1.0), (N.s[:], N.s[:], ACT.Ln, 1.0), sqrt_r(N),
                       (dinv[:], dinv[:], ACT.Sqrt, 1.0), None]

        def lead(v):
            step = N.step
            gin(K, N, v, K.keep[:], "L1_gnn_eps2", "L1_gnn_b2a", "L1_gnn_b2b")
            step(v.tensor_reduce(N.s[:], N.y[:], AX.X, ALU.max))
            step(v.tensor_tensor(N.y[:], N.y[:], N.each(N.s), ALU.subtract))
            N.function()
            step(v.tensor_reduce(N.s[:], N.sq[:], AX.X, ALU.add))
            N.function()
            step(v.tensor_tensor(N.y[:], N.y[:], N.each(N.s), ALU.subtract))
            step(v.tensor_tensor(N.y[:], N.y[:], K.x[:], ALU.add))
            N.layernorm(K.x[:])
            step(v.tensor_scalar(dinv[:], dinv[:], 1.0, None, ALU.add))
            N.function()
            step(v.reciprocal(dinv[:], dinv[:]))
            step(v.tensor_tensor(K.keep[:], N.linear(), N.each(dinv), ALU.mult))
        N.engines(lead)


def gcn(K):
    with Nodes(K, "n4") as N:
        N.functions = [sqrt_r(N)]

        def lead(v):
            step = N.step
            step(v.tensor_tensor(N.y[:], acc_nodes(K), K.keep[:], ALU.add))
            step(v.tensor_tensor(N.y[:], N.y[:], N.each(K.dst_count), ALU.mult))
            step(v.tensor_tensor(N.y[:], N.y[:], N.row("L2_gnn_b"), ALU.add))
            step(v.tensor_tensor(N.y[:], N.y[:], K.x[:], ALU.add))
            N.layernorm(K.x[:])
        N.engines(lead)


def batch_norm(K, N, v, a, gain, bias):
    step = N.step
    mean, scale = N.stat[:, 0, :], N.stat[:, 1, :]
    valid = K.c("valid").unsqueeze(2).to_broadcast([P, NBLK, F])

    def over_nodes(x, out, bias):
        step(v.tensor_reduce(N.part[:], x.rearrange("p b f -> p f b"), AX.X, ALU.add))
        step(v.tensor_scalar(out, N.total(), 1.0 / N_NODES, bias, ALU.mult, ALU.add))

    def spread(x):
        return x.unsqueeze(1).to_broadcast([P, NBLK, F])
    over_nodes(a, mean, 0.0)
    step(v.tensor_tensor(a, a, spread(mean), ALU.subtract))
    step(v.tensor_tensor(N.sq[:], a, a, ALU.mult))
    step(v.tensor_tensor(N.sq[:], N.sq[:], valid, ALU.mult))
    over_nodes(N.sq[:], scale, EPS)
    N.function()
    step(v.reciprocal(scale, scale))
    step(v.tensor_tensor(scale, scale, N.vec(gain), ALU.mult))
    step(v.tensor_tensor(a, a, spread(scale), ALU.mult))
    step(v.tensor_tensor(a, a, spread(N.vec(bias)), ALU.add))


def sqrt_stat(N, k):
    return (N.stat[:, k, :], N.stat[:, k, :], ACT.Sqrt, 1.0)


def mean_of(K, N, v, factor):
    N.step(v.tensor_scalar(N.r[:], K.src_count[:], 1.0, None, ALU.max))
    N.step(v.reciprocal(N.r[:], N.r[:]))
    N.step(v.tensor_scalar(N.r[:], N.r[:], float(factor), None, ALU.mult))


def norm_first(K):
    with Nodes(K, "n6", totals=3) as N:
        N.functions = [sqrt_stat(N, 1), sqrt_stat(N, 2)]

        def lead(v):
            step = N.step
            mean_of(K, N, v, 1.0 / np.sqrt(F))
            step(v.tensor_tensor(N.y[:], K.keep[:], N.each(N.r), ALU.mult))
            batch_norm(K, N, v, N.y[:], "L3_gnn_bn0_gs", "L3_gnn_bn0_bs")
            step(v.tensor_copy(K.keep[:], N.y[:]))
            step(v.tensor_scalar(N.r[:], N.r[:], float(np.sqrt(3.0)), None, ALU.mult))
            step(v.tensor_tensor(N.y[:], acc_nodes(K), N.each(N.r), ALU.mult))
            step(v.tensor_tensor(N.sq[:], N.y[:], N.y[:], ALU.mult))
            step(v.tensor_reduce(N.part[:], N.sq[:].rearrange("p b f -> p f b"), AX.X, ALU.add))
            tot = N.total()
            scale = N.stat[:, 2, 0:NV]
            step(v.memset(N.stat[:, 2, :], 1.0))
            step(v.tensor_reduce(scale, tot[:, 0:3 * NV].rearrange("p (j c) -> p j c", c=3), AX.X, ALU.add))
            step(v.tensor_scalar(scale, scale, 1.0 / (3 * N_NODES), EPS, ALU.mult, ALU.add))
            N.function()
            step(v.reciprocal(scale, scale))
            step(v.tensor_tensor(scale, scale, N.vec("L3_gnn_bn0_gv", NV), ALU.mult))
            step(v.memset(N.stat[:, 3, :], 0.0))
            step(v.tensor_copy(N.stat[:, 3, 0:3 * NV].rearrange("p (j c) -> p j c", c=3),
                               scale.unsqueeze(2).to_broadcast([P, NV, 3])))
            step(v.tensor_tensor(K.vectors[:], N.y[:], N.stat[:, 3, :].unsqueeze(1).to_broadcast([P, NBLK, F]), ALU.mult))
        N.engines(lead)


def finish(K):
    whole = N_NODES // P
    with Nodes(K, "n7", totals=2) as N:
        N.functions = [sqrt_stat(N, 1), sqrt_r(N)]
        stored = K.sem("n7_stored")

        def lead(v):
            step = N.step
            mean_of(K, N, v, 1.0 / np.sqrt(F + NV))
            step(v.tensor_tensor(N.y[:], acc_nodes(K), N.each(N.r), ALU.mult))
            batch_norm(K, N, v, N.y[:], "L3_gnn_bn1_gs", "L3_gnn_bn1_bs")
            step(v.tensor_tensor(N.y[:], N.y[:], K.x[:], ALU.add))
            N.layernorm(K.keep[:])
            v.sem_inc(N.lin_in, 1)
        N.engines(lead)

        @N.block.sync
        def _(sp):
            sp.wait_ge(N.lin_in, 1)
            sp.dma_start(K.out[0:whole * P].rearrange("(b p) f -> p b f", p=P), K.keep[:, 0:whole, :]).then_inc(stored, 16)
            sp.dma_start(K.out[whole * P:N_NODES], K.keep[0:N_NODES - whole * P, whole, :]).then_inc(stored, 16)
            sp.wait_ge(stored, 32)


def columns(a):
    return a[:].rearrange("p b f -> p (b f)")


def program(nc, ins, out):
    with ExitStack() as ctx:
        K = Kernel(nc, ctx, ins, out)
        load_constants(K)
        K.end_phase()
        sort_edges(K)
        K.end_phase()
        unpack_indices(K)
        K.end_phase()
        setup_nodes(K)
        K.end_phase()
        first_table(K)
        K.end_phase()
        edge_pass(K, "e0", DST, SRC, "product", [K.tab], K.acc, K.src_count)
        K.end_phase()
        update_first(K)
        K.end_phase()
        edge_pass(K, "e1", SRC, DST, "copy", [columns(K.x)], K.acc, K.dst_count)
        K.end_phase()
        gin_first(K)
        K.end_phase()
        edge_pass(K, "e2", SRC, DST, "copy", [columns(K.keep)], K.acc)
        K.end_phase()
        gin_second(K)
        K.end_phase()
        edge_pass(K, "e3", SRC, DST, "copy", [columns(K.keep)], K.acc)
        K.end_phase()
        gcn(K)
        K.end_phase()
        edge_pass(K, "e4", DST, SRC, "first", [columns(K.x)], columns(K.keep))
        K.end_phase()
        edge_pass(K, "e5", None, SRC, "stored", [], K.acc)
        K.end_phase()
        norm_first(K)
        K.end_phase()
        edge_pass(K, "e6", DST, SRC, "second", [columns(K.keep), columns(K.vectors)], K.acc)
        K.end_phase()
        finish(K)
        K.end_phase()


_INS = ["x", "src", "dst", "edge_attr_3", "edge_attr_48", "edge_attr_8",
        "L0_gnn_W_msg_tp", "L0_gnn_W_msg_lin", "L0_gnn_W_upd_tp", "L0_gnn_W_upd_lin",
        "L1_gnn_eps1", "L1_gnn_w1a", "L1_gnn_b1a", "L1_gnn_w1b", "L1_gnn_b1b",
        "L1_gnn_eps2", "L1_gnn_w2a", "L1_gnn_b2a", "L1_gnn_w2b", "L1_gnn_b2b", "L2_gnn_W", "L2_gnn_b",
        "L3_gnn_fc0_w1", "L3_gnn_fc0_b1", "L3_gnn_fc0_w2", "L3_gnn_fc0_b2",
        "L3_gnn_fc1_w1", "L3_gnn_fc1_b1", "L3_gnn_fc1_w2", "L3_gnn_fc1_b2",
        "L3_gnn_bn0_gs", "L3_gnn_bn0_bs", "L3_gnn_bn0_gv", "L3_gnn_bn1_gs", "L3_gnn_bn1_bs"]


def kernel(**inputs):
    import concourse.bacc as bacc
    from concourse.bass_utils import run_bass_kernel_spmd

    nc = bacc.Bacc("TRN2", target_bir_lowering=False, num_devices=1)
    arrays = {"in_consts": build_constants()}
    for name in _INS:
        a = np.ascontiguousarray(inputs[name])
        arrays[f"in_{name}"] = a.reshape(1) if a.ndim == 0 else a
    ins = {n[3:]: nc.dram_tensor(n, a.shape, mybir.dt.from_np(a.dtype), kind="ExternalInput").ap()
           for n, a in arrays.items()}
    out = nc.dram_tensor("out", (N_NODES, F), F32, kind="ExternalOutput").ap()
    program(nc, ins, out)
    r = run_bass_kernel_spmd(nc, [arrays], core_ids=[0])
    return r.results[0]["out"]
```
